# Optimizing a Trainium2 kernel written in Bass

```python
import numpy as np
import jax
import jax.numpy as jnp

def _softmax(x, axis=-1):
    return jax.nn.softmax(x, axis=axis)

def _gelu(x):
    return jax.nn.gelu(x, approximate=True)

def _silu(x):
    return jax.nn.silu(x)

def _sigmoid(x):
    return jax.nn.sigmoid(x)

def _layernorm(x, axis=-1, eps=1e-05):
    m = jnp.mean(x, axis=axis, keepdims=True)
    v = jnp.var(x, axis=axis, keepdims=True)
    return (x - m) / jnp.sqrt(v + eps)

def _scatter_add(tgt, idx, src, axis=0):
    return tgt.at[idx].add(src)

def _segment_sum(src, seg, n):
    return jax.ops.segment_sum(src, seg, n)
kernel_name = 'mk_adaln_d2_jaxref_r8_a68f01'

def setup_inputs(seed: int=0):
    np.random.seed(seed)
    _w = jnp.asarray

    def _L0_attn_setup():
        import jax, jax.numpy as jnp
        import numpy as np
        B, S, D, H = (2, 256, 128, 16)
        HD = D // H
        LN_EPS = 1e-05
        key = jax.random.key(seed)
        ks = jax.random.split(key, 8)
        inv = 1.0 / np.sqrt(D)
        return {'embedded': jax.random.normal(ks[0], (B, S, D), dtype=jnp.float32), 'Wq': jax.random.normal(ks[1], (D, D), dtype=jnp.float32) * inv, 'bq': jax.random.normal(ks[2], (D,), dtype=jnp.float32) * 0.01, 'Wk': jax.random.normal(ks[3], (D, D), dtype=jnp.float32) * inv, 'bk': jax.random.normal(ks[4], (D,), dtype=jnp.float32) * 0.01, 'Wv': jax.random.normal(ks[5], (D, D), dtype=jnp.float32) * inv, 'bv': jax.random.normal(ks[6], (D,), dtype=jnp.float32) * 0.01, 'gamma': jnp.ones((D,), dtype=jnp.float32), 'beta': jnp.zeros((D,), dtype=jnp.float32)}
    _L0_attn_in = _L0_attn_setup()

    def _L0_ffn_setup():
        import jax, jax.numpy as jnp
        import numpy as np
        HID = 128
        NH = 16
        NKV = 4
        HD = HID // NH
        E = 8
        TOPK = 2
        FFN = 256
        EPS = 1e-05
        THETA = 10000.0

        def _rmsnorm(x, w):
            var = jnp.mean(x * x, axis=-1, keepdims=True)
            return x * jax.lax.rsqrt(var + EPS) * w

        def _rope_tables(S):
            inv_freq = 1.0 / THETA ** (jnp.arange(0, HD, 2, dtype=jnp.float32) / HD)
            freqs = jnp.arange(S, dtype=jnp.float32)[:, None] * inv_freq[None, :]
            emb = jnp.concatenate([freqs, freqs], axis=-1)
            return (jnp.cos(emb), jnp.sin(emb))

        def _apply_rope(t, cos, sin):
            t1, t2 = jnp.split(t, 2, axis=-1)
            rot = jnp.concatenate([-t2, t1], axis=-1)
            return t * cos[None, :, None, :] + rot * sin[None, :, None, :]
        key = jax.random.key(seed)
        ks = jax.random.split(key, 6)
        B, S = (1, 256)
        x = jax.random.normal(ks[0], (B, S, HID), dtype=jnp.float32)
        wqkv = jax.random.normal(ks[1], ((NH + 2 * NKV) * HD, HID), dtype=jnp.float32) * 0.02
        wo = jax.random.normal(ks[2], (HID, NH * HD), dtype=jnp.float32) * 0.02
        gate_w = jax.random.normal(ks[3], (E, HID), dtype=jnp.float32) * 0.02
        w13 = jax.random.normal(ks[4], (E, 2 * FFN, HID), dtype=jnp.float32) * 0.02
        w2 = jax.random.normal(ks[5], (E, HID, FFN), dtype=jnp.float32) * 0.02
        return {'x': x, 'ln1_w': jnp.ones((HID,), jnp.float32), 'ln2_w': jnp.ones((HID,), jnp.float32), 'wqkv': wqkv, 'wo': wo, 'gate_w': gate_w, 'w13': w13, 'w2': w2}
    _L0_ffn_in = _L0_ffn_setup()
    _L0_c = _w((lambda *s: np.random.randn(*s).astype(np.float32) * 0.05)(1, 128))
    _L0_wmod = _w((lambda *s: np.random.randn(*s).astype(np.float32) * 0.05)(128, 6 * 128) * 128 ** (-0.5))

    def _L1_attn_setup():
        import jax, jax.numpy as jnp
        import numpy as np
        DIM = 128
        HEADS = 16
        NEG = 10000000000.0

        def split_heads(v, heads):
            b, s, d = v.shape
            hd = d // heads
            v = v.reshape(b, s, hd, heads)
            return jnp.transpose(v, (0, 3, 1, 2))

        def merge_heads(v):
            b, h, s, hd = v.shape
            v = jnp.transpose(v, (0, 2, 3, 1))
            return v.reshape(b, s, h * hd)
        key = jax.random.key(seed)
        kx, kq, kk, kv, ko = jax.random.split(key, 5)
        x = jax.random.normal(kx, (2, 256, DIM), dtype=jnp.float32)
        qw = 0.05 * jax.random.normal(kq, (DIM, DIM), dtype=jnp.float32)
        kw = 0.05 * jax.random.normal(kk, (DIM, DIM), dtype=jnp.float32)
        vw = 0.05 * jax.random.normal(kv, (DIM, DIM), dtype=jnp.float32)
        ow = 0.05 * jax.random.normal(ko, (DIM, DIM), dtype=jnp.float32)
        return {'x': x, 'qw': qw, 'kw': kw, 'vw': vw, 'ow': ow}
    _L1_attn_in = _L1_attn_setup()

    def _L1_ffn_setup():
        import jax, jax.numpy as jnp
        import numpy as np
        DIM = 128
        DEPTH = 2
        HEADS = 8
        DIM_HEAD = 64
        WINDOW = 64
        INNER = HEADS * DIM_HEAD
        HID = int(DIM * 4 * 2 / 3)
        B, N = (2, 1024)
        QK_SCALE = 8.0

        def shift_token(t):
            t1, t2 = jnp.split(t, 2, axis=-1)
            t2 = jnp.pad(t2, ((0, 0), (1, 0), (0, 0)))[:, :-1]
            return jnp.concatenate([t1, t2], axis=-1)

        def l2norm(t):
            return t / jnp.clip(jnp.linalg.norm(t, axis=-1, keepdims=True), 1e-12)

        def rotate_half(x):
            x1, x2 = jnp.split(x, 2, axis=-1)
            return jnp.concatenate([-x2, x1], axis=-1)

        def rotary_xpos(q, k):
            n = q.shape[-2]
            half_idx = jnp.arange(0, DIM_HEAD, 2, dtype=jnp.float32)
            inv_freq = 1.0 / 10000.0 ** (half_idx / DIM_HEAD)
            t = jnp.arange(n, dtype=jnp.float32)
            freqs = t[:, None] * inv_freq[None, :]
            freqs = jnp.concatenate([freqs, freqs], axis=-1)
            base = (half_idx + 0.4 * DIM_HEAD) / (1.4 * DIM_HEAD)
            power = (t - n // 2) / float(WINDOW // 2)
            scale = base[None, :] ** power[:, None]
            scale = jnp.concatenate([scale, scale], axis=-1)
            cos, sin = (jnp.cos(freqs), jnp.sin(freqs))
            q = q * cos * scale + rotate_half(q) * sin * scale
            k = k * cos / scale + rotate_half(k) * sin / scale
            return (q, k)

        def local_attention(q, k, v):
            b, h, n, d = q.shape
            w = n // WINDOW
            bq = q.reshape(b, h, w, WINDOW, d) * QK_SCALE
            bk = k.reshape(b, h, w, WINDOW, d)
            bv = v.reshape(b, h, w, WINDOW, d)

            def look_around(t):
                p = jnp.pad(t, ((0, 0), (0, 0), (1, 0), (0, 0), (0, 0)))
                return jnp.concatenate([p[:, :, :w], p[:, :, 1:]], axis=3)
            bk, bv = (look_around(bk), look_around(bv))
            bt = jnp.arange(n).reshape(w, WINDOW)
            btp = jnp.pad(bt, ((1, 0), (0, 0)), constant_values=-1)
            btk = jnp.concatenate([btp[:w], btp[1:]], axis=1)
            sim = jnp.einsum('bhwid,bhwjd->bhwij', bq, bk)
            i = bt[:, :, None]
            j = btk[:, None, :]
            mask = (i < j) | (i > j + WINDOW) | (j == -1)
            sim = jnp.where(mask, -jnp.finfo(sim.dtype).max, sim)
            attn = jax.nn.softmax(sim, axis=-1)
            out = jnp.einsum('bhwij,bhwjd->bhwid', attn, bv)
            return out.reshape(b, h, n, d)

        def _layer(x, wqkv, qs, ksc, wo, lg, lb, w1, b1, w2, b2):
            b, n, _ = x.shape
            h = shift_token(x)
            qkv = h @ wqkv
            q, k, v = jnp.split(qkv, 3, axis=-1)
            to_heads = lambda t: t.reshape(b, n, HEADS, DIM_HEAD).transpose(0, 2, 1, 3)
            q, k, v = (to_heads(q), to_heads(k), to_heads(v))
            q = l2norm(q) * qs
            k = l2norm(k) * ksc
            q, k = rotary_xpos(q, k)
            o = local_attention(q, k, v)
            o = o.transpose(0, 2, 1, 3).reshape(b, n, INNER)
            x = x + o @ wo
            h = shift_token(x)
            mu = h.mean(-1, keepdims=True)
            var = h.var(-1, keepdims=True)
            h = (h - mu) / jnp.sqrt(var + 1e-05) * lg + lb
            h = h @ w1 + b1
            a, g = jnp.split(h, 2, axis=-1)
            h = a * jax.nn.gelu(g, approximate=False)
            x = x + h @ w2 + b2
            return x
        key = jax.random.key(seed)
        ks = jax.random.split(key, 6)
        return {'x': jax.random.normal(ks[0], (B, N, DIM), jnp.float32), 'wqkv': jax.random.normal(ks[1], (DEPTH, DIM, 3 * INNER), jnp.float32) * 0.02, 'q_scale': jnp.ones((DEPTH, DIM_HEAD), jnp.float32), 'k_scale': jnp.ones((DEPTH, DIM_HEAD), jnp.float32), 'wo': jax.random.normal(ks[2], (DEPTH, INNER, DIM), jnp.float32) * 0.02, 'ln_g': jnp.ones((DEPTH, DIM), jnp.float32), 'ln_b': jnp.zeros((DEPTH, DIM), jnp.float32), 'w1': jax.random.normal(ks[3], (DEPTH, DIM, 2 * HID), jnp.float32) * 0.02, 'b1': jnp.zeros((DEPTH, 2 * HID), jnp.float32), 'w2': jax.random.normal(ks[4], (DEPTH, HID, DIM), jnp.float32) * 0.02, 'b2': jnp.zeros((DEPTH, DIM), jnp.float32)}
    _L1_ffn_in = _L1_ffn_setup()
    _L1_c = _w((lambda *s: np.random.randn(*s).astype(np.float32) * 0.05)(1, 128))
    _L1_wmod = _w((lambda *s: np.random.randn(*s).astype(np.float32) * 0.05)(128, 6 * 128) * 128 ** (-0.5))
    _d = {'L0_attn_embedded': _L0_attn_in['embedded'], 'L0_attn_Wq': _L0_attn_in['Wq'], 'L0_attn_bq': _L0_attn_in['bq'], 'L0_attn_Wk': _L0_attn_in['Wk'], 'L0_attn_bk': _L0_attn_in['bk'], 'L0_attn_Wv': _L0_attn_in['Wv'], 'L0_attn_bv': _L0_attn_in['bv'], 'L0_attn_gamma': _L0_attn_in['gamma'], 'L0_attn_beta': _L0_attn_in['beta'], 'L0_ffn_ln1_w': _L0_ffn_in['ln1_w'], 'L0_ffn_ln2_w': _L0_ffn_in['ln2_w'], 'L0_ffn_wqkv': _L0_ffn_in['wqkv'], 'L0_ffn_wo': _L0_ffn_in['wo'], 'L0_ffn_gate_w': _L0_ffn_in['gate_w'], 'L0_ffn_w13': _L0_ffn_in['w13'], 'L0_ffn_w2': _L0_ffn_in['w2'], 'L0_c': _L0_c, 'L0_wmod': _L0_wmod, 'L1_attn_qw': _L1_attn_in['qw'], 'L1_attn_kw': _L1_attn_in['kw'], 'L1_attn_vw': _L1_attn_in['vw'], 'L1_attn_ow': _L1_attn_in['ow'], 'L1_ffn_wqkv': _L1_ffn_in['wqkv'], 'L1_ffn_q_scale': _L1_ffn_in['q_scale'], 'L1_ffn_k_scale': _L1_ffn_in['k_scale'], 'L1_ffn_wo': _L1_ffn_in['wo'], 'L1_ffn_ln_g': _L1_ffn_in['ln_g'], 'L1_ffn_ln_b': _L1_ffn_in['ln_b'], 'L1_ffn_w1': _L1_ffn_in['w1'], 'L1_ffn_b1': _L1_ffn_in['b1'], 'L1_ffn_w2': _L1_ffn_in['w2'], 'L1_ffn_b2': _L1_ffn_in['b2'], 'L1_c': _L1_c, 'L1_wmod': _L1_wmod}
    _x0 = _d['L0_attn_embedded']
    _d['L0_attn_embedded'] = jax.random.normal(jax.random.fold_in(jax.random.key(seed), 1), (1, 2048, 128), dtype=_x0.dtype)
    del _x0
    return _d

def reference(L0_attn_embedded, L0_attn_Wq, L0_attn_bq, L0_attn_Wk, L0_attn_bk, L0_attn_Wv, L0_attn_bv, L0_attn_gamma, L0_attn_beta, L0_ffn_ln1_w, L0_ffn_ln2_w, L0_ffn_wqkv, L0_ffn_wo, L0_ffn_gate_w, L0_ffn_w13, L0_ffn_w2, L0_c, L0_wmod, L1_attn_qw, L1_attn_kw, L1_attn_vw, L1_attn_ow, L1_ffn_wqkv, L1_ffn_q_scale, L1_ffn_k_scale, L1_ffn_wo, L1_ffn_ln_g, L1_ffn_ln_b, L1_ffn_w1, L1_ffn_b1, L1_ffn_w2, L1_ffn_b2, L1_c, L1_wmod):

    def _L0_attn_ref(embedded, Wq, bq, Wk, bk, Wv, bv, gamma, beta):
        import jax, jax.numpy as jnp
        import numpy as np
        B, S, D, H = (2, 256, 128, 16)
        HD = D // H
        LN_EPS = 1e-05
        b, s, d = embedded.shape
        q = embedded @ Wq.T + bq
        k = embedded @ Wk.T + bk
        v = embedded @ Wv.T + bv
        q = q.reshape(b, s, H, HD).transpose(0, 2, 1, 3)
        k = k.reshape(b, s, H, HD).transpose(0, 2, 1, 3)
        v = v.reshape(b, s, H, HD).transpose(0, 2, 1, 3)
        qk = jnp.einsum('bhqd,bhkd->bhqk', q, k)
        qk = jnp.where(jnp.isnan(qk), -jnp.inf, qk)
        qk = qk / jnp.float32(np.sqrt(s))
        p = jax.nn.softmax(qk, axis=-1)
        p = jnp.where(jnp.isnan(p), 0.0, p)
        v = jnp.where(jnp.isnan(v), 0.0, v)
        mask = jnp.triu(jnp.ones((s, s), dtype=p.dtype), k=0)
        p = p * mask
        z = jnp.einsum('bhqk,bhkd->bhqd', p, v)
        z = z.reshape(b, s, d)
        x = embedded + z
        mu = jnp.mean(x, axis=-1, keepdims=True)
        var = jnp.mean(jnp.square(x - mu), axis=-1, keepdims=True)
        out = (x - mu) * jax.lax.rsqrt(var + LN_EPS) * gamma + beta
        return out

    def _L0_ffn_ref(x, ln1_w, ln2_w, wqkv, wo, gate_w, w13, w2):
        import jax, jax.numpy as jnp
        import numpy as np
        HID = 128
        NH = 16
        NKV = 4
        HD = HID // NH
        E = 8
        TOPK = 2
        FFN = 256
        EPS = 1e-05
        THETA = 10000.0

        def _rmsnorm(x, w):
            var = jnp.mean(x * x, axis=-1, keepdims=True)
            return x * jax.lax.rsqrt(var + EPS) * w

        def _rope_tables(S):
            inv_freq = 1.0 / THETA ** (jnp.arange(0, HD, 2, dtype=jnp.float32) / HD)
            freqs = jnp.arange(S, dtype=jnp.float32)[:, None] * inv_freq[None, :]
            emb = jnp.concatenate([freqs, freqs], axis=-1)
            return (jnp.cos(emb), jnp.sin(emb))

        def _apply_rope(t, cos, sin):
            t1, t2 = jnp.split(t, 2, axis=-1)
            rot = jnp.concatenate([-t2, t1], axis=-1)
            return t * cos[None, :, None, :] + rot * sin[None, :, None, :]
        B, S, _ = x.shape
        h = _rmsnorm(x, ln1_w)
        qkv = jnp.einsum('bsh,oh->bso', h, wqkv)
        q = qkv[..., :NH * HD].reshape(B, S, NH, HD)
        k = qkv[..., NH * HD:(NH + NKV) * HD].reshape(B, S, NKV, HD)
        v = qkv[..., (NH + NKV) * HD:].reshape(B, S, NKV, HD)
        cos, sin = _rope_tables(S)
        q = _apply_rope(q, cos, sin)
        k = _apply_rope(k, cos, sin)
        groups = NH // NKV
        k = jnp.repeat(k, groups, axis=2)
        v = jnp.repeat(v, groups, axis=2)
        scale = HD ** (-0.5)
        scores = jnp.einsum('bqhd,bkhd->bhqk', q, k) * scale
        causal = jnp.tril(jnp.ones((S, S), dtype=bool))
        scores = jnp.where(causal[None, None], scores, jnp.finfo(scores.dtype).min)
        probs = jax.nn.softmax(scores, axis=-1)
        attn = jnp.einsum('bhqk,bkhd->bqhd', probs, v).reshape(B, S, NH * HD)
        x = x + jnp.einsum('bso,ho->bsh', attn, wo)
        h = _rmsnorm(x, ln2_w).reshape(-1, HID)
        T = h.shape[0]
        logits = jnp.einsum('th,eh->te', h, gate_w)
        rprobs = jax.nn.softmax(logits.astype(jnp.float32), axis=-1)
        topw, topi = jax.lax.top_k(rprobs, TOPK)
        topw = topw / jnp.sum(topw, axis=-1, keepdims=True)
        wfull = jnp.zeros((T, E), jnp.float32).at[jnp.arange(T)[:, None], topi].set(topw)
        wfull = wfull.astype(h.dtype)
        out = jnp.zeros((T, HID), h.dtype)
        for e in range(E):
            w1 = w13[e, :FFN]
            w3 = w13[e, FFN:]
            g = jax.nn.silu(h @ w1.T) * (h @ w3.T)
            out = out + jnp.einsum('tf,hf->th', g, w2[e]) * wfull[:, e:e + 1]
        return x + out.reshape(B, S, HID)

    def _L1_attn_ref(x, qw, kw, vw, ow):
        import jax, jax.numpy as jnp
        import numpy as np
        DIM = 128
        HEADS = 16
        NEG = 10000000000.0

        def split_heads(v, heads):
            b, s, d = v.shape
            hd = d // heads
            v = v.reshape(b, s, hd, heads)
            return jnp.transpose(v, (0, 3, 1, 2))

        def merge_heads(v):
            b, h, s, hd = v.shape
            v = jnp.transpose(v, (0, 2, 3, 1))
            return v.reshape(b, s, h * hd)
        b, s, d = x.shape
        Q = split_heads(x @ qw, HEADS)
        K = split_heads(x @ kw, HEADS)
        V = split_heads(x @ vw, HEADS)
        score = jnp.einsum('bhqd,bhkd->bhqk', Q, K) / jnp.sqrt(jnp.float32(d))
        causal = jnp.tril(jnp.ones((1, 1, s, s), dtype=score.dtype))
        score = score - NEG * (1.0 - causal)
        weights = jax.nn.softmax(score, axis=-1)
        attn = jnp.einsum('bhqk,bhkd->bhqd', weights, V)
        return merge_heads(attn) @ ow

    def _L1_ffn_ref(x, wqkv, q_scale, k_scale, wo, ln_g, ln_b, w1, b1, w2, b2):
        import jax, jax.numpy as jnp
        import numpy as np
        DIM = 128
        DEPTH = 2
        HEADS = 8
        DIM_HEAD = 64
        WINDOW = 64
        INNER = HEADS * DIM_HEAD
        HID = int(DIM * 4 * 2 / 3)
        B, N = (2, 1024)
        QK_SCALE = 8.0

        def shift_token(t):
            t1, t2 = jnp.split(t, 2, axis=-1)
            t2 = jnp.pad(t2, ((0, 0), (1, 0), (0, 0)))[:, :-1]
            return jnp.concatenate([t1, t2], axis=-1)

        def l2norm(t):
            return t / jnp.clip(jnp.linalg.norm(t, axis=-1, keepdims=True), 1e-12)

        def rotate_half(x):
            x1, x2 = jnp.split(x, 2, axis=-1)
            return jnp.concatenate([-x2, x1], axis=-1)

        def rotary_xpos(q, k):
            n = q.shape[-2]
            half_idx = jnp.arange(0, DIM_HEAD, 2, dtype=jnp.float32)
            inv_freq = 1.0 / 10000.0 ** (half_idx / DIM_HEAD)
            t = jnp.arange(n, dtype=jnp.float32)
            freqs = t[:, None] * inv_freq[None, :]
            freqs = jnp.concatenate([freqs, freqs], axis=-1)
            base = (half_idx + 0.4 * DIM_HEAD) / (1.4 * DIM_HEAD)
            power = (t - n // 2) / float(WINDOW // 2)
            scale = base[None, :] ** power[:, None]
            scale = jnp.concatenate([scale, scale], axis=-1)
            cos, sin = (jnp.cos(freqs), jnp.sin(freqs))
            q = q * cos * scale + rotate_half(q) * sin * scale
            k = k * cos / scale + rotate_half(k) * sin / scale
            return (q, k)

        def local_attention(q, k, v):
            b, h, n, d = q.shape
            w = n // WINDOW
            bq = q.reshape(b, h, w, WINDOW, d) * QK_SCALE
            bk = k.reshape(b, h, w, WINDOW, d)
            bv = v.reshape(b, h, w, WINDOW, d)

            def look_around(t):
                p = jnp.pad(t, ((0, 0), (0, 0), (1, 0), (0, 0), (0, 0)))
                return jnp.concatenate([p[:, :, :w], p[:, :, 1:]], axis=3)
            bk, bv = (look_around(bk), look_around(bv))
            bt = jnp.arange(n).reshape(w, WINDOW)
            btp = jnp.pad(bt, ((1, 0), (0, 0)), constant_values=-1)
            btk = jnp.concatenate([btp[:w], btp[1:]], axis=1)
            sim = jnp.einsum('bhwid,bhwjd->bhwij', bq, bk)
            i = bt[:, :, None]
            j = btk[:, None, :]
            mask = (i < j) | (i > j + WINDOW) | (j == -1)
            sim = jnp.where(mask, -jnp.finfo(sim.dtype).max, sim)
            attn = jax.nn.softmax(sim, axis=-1)
            out = jnp.einsum('bhwij,bhwjd->bhwid', attn, bv)
            return out.reshape(b, h, n, d)

        def _layer(x, wqkv, qs, ksc, wo, lg, lb, w1, b1, w2, b2):
            b, n, _ = x.shape
            h = shift_token(x)
            qkv = h @ wqkv
            q, k, v = jnp.split(qkv, 3, axis=-1)
            to_heads = lambda t: t.reshape(b, n, HEADS, DIM_HEAD).transpose(0, 2, 1, 3)
            q, k, v = (to_heads(q), to_heads(k), to_heads(v))
            q = l2norm(q) * qs
            k = l2norm(k) * ksc
            q, k = rotary_xpos(q, k)
            o = local_attention(q, k, v)
            o = o.transpose(0, 2, 1, 3).reshape(b, n, INNER)
            x = x + o @ wo
            h = shift_token(x)
            mu = h.mean(-1, keepdims=True)
            var = h.var(-1, keepdims=True)
            h = (h - mu) / jnp.sqrt(var + 1e-05) * lg + lb
            h = h @ w1 + b1
            a, g = jnp.split(h, 2, axis=-1)
            h = a * jax.nn.gelu(g, approximate=False)
            x = x + h @ w2 + b2
            return x
        for l in range(DEPTH):
            x = _layer(x, wqkv[l], q_scale[l], k_scale[l], wo[l], ln_g[l], ln_b[l], w1[l], b1[l], w2[l], b2[l])
        return x
    x = L0_attn_embedded
    mod = (_silu(L0_c) @ L0_wmod).reshape(L0_c.shape[0], 6, 1, -1)
    sa, ca, ga, sb, cb, gb = (mod[:, 0], mod[:, 1], mod[:, 2], mod[:, 3], mod[:, 4], mod[:, 5])
    ga = (2 * (ga >= 0) - 1) * jnp.maximum(jnp.abs(ga), 0.25)
    gb = (2 * (gb >= 0) - 1) * jnp.maximum(jnp.abs(gb), 0.25)
    h = _layernorm(x, axis=-1) * (1 + ca) + sa
    x = x + ga * _L0_attn_ref(h, L0_attn_Wq, L0_attn_bq, L0_attn_Wk, L0_attn_bk, L0_attn_Wv, L0_attn_bv, L0_attn_gamma, L0_attn_beta)
    h = _layernorm(x, axis=-1) * (1 + cb) + sb
    x = x + gb * _L0_ffn_ref(h, L0_ffn_ln1_w, L0_ffn_ln2_w, L0_ffn_wqkv, L0_ffn_wo, L0_ffn_gate_w, L0_ffn_w13, L0_ffn_w2)
    mod = (_silu(L1_c) @ L1_wmod).reshape(L1_c.shape[0], 6, 1, -1)
    sa, ca, ga, sb, cb, gb = (mod[:, 0], mod[:, 1], mod[:, 2], mod[:, 3], mod[:, 4], mod[:, 5])
    ga = (2 * (ga >= 0) - 1) * jnp.maximum(jnp.abs(ga), 0.25)
    gb = (2 * (gb >= 0) - 1) * jnp.maximum(jnp.abs(gb), 0.25)
    h = _layernorm(x, axis=-1) * (1 + ca) + sa
    x = x + ga * _L1_attn_ref(h, L1_attn_qw, L1_attn_kw, L1_attn_vw, L1_attn_ow)
    h = _layernorm(x, axis=-1) * (1 + cb) + sb
    x = x + gb * _L1_ffn_ref(h, L1_ffn_wqkv, L1_ffn_q_scale, L1_ffn_k_scale, L1_ffn_wo, L1_ffn_ln_g, L1_ffn_ln_b, L1_ffn_w1, L1_ffn_b1, L1_ffn_w2, L1_ffn_b2)
    return x

_drawn_inputs = setup_inputs


def setup_inputs(seed=0):
    import zlib

    import numpy as np

    out = dict(_drawn_inputs(seed))
    spreads = {'L0_attn_gamma': (1.0, 0.2),
     'L0_attn_beta': (0.0, 0.405),
     'L0_ffn_ln1_w': (1.0, 0.6),
     'L0_ffn_ln2_w': (1.0, 0.6),
     'L1_ffn_q_scale': (1.0, 0.6),
     'L1_ffn_k_scale': (1.0, 0.6),
     'L1_ffn_ln_g': (1.0, 0.6),
     'L1_ffn_ln_b': (0.0, 0.8),
     'L1_ffn_b1': (0.0, 0.8),
     'L1_ffn_b2': (0.0, 0.8)}
    factors = {'L0_attn_Wq': 8.0,
     'L0_attn_bq': 8.0,
     'L0_attn_Wk': 8.0,
     'L0_attn_bk': 64.0,
     'L0_attn_Wv': 8.0,
     'L0_attn_bv': 8.0,
     'L0_ffn_wqkv': 8.0,
     'L0_ffn_wo': 8.0,
     'L0_ffn_gate_w': 8.0,
     'L0_ffn_w13': 8.0,
     'L0_ffn_w2': 8.0,
     'L1_attn_qw': 8.0,
     'L1_attn_kw': 8.0,
     'L1_attn_vw': 8.0,
     'L1_attn_ow': 8.0,
     'L1_ffn_wqkv': 8.0,
     'L1_ffn_wo': 8.0,
     'L1_ffn_w1': 8.0,
     'L1_ffn_w2': 8.0}
    for name, (base, spread) in spreads.items():
        noise = np.random.default_rng([zlib.crc32(name.encode()), seed]).standard_normal(out[name].shape)
        drawn = base * np.exp(spread * noise) if base else spread * noise
        out[name] = jnp.asarray(drawn.astype(out[name].dtype))
    for name, factor in factors.items():
        out[name] = (out[name] * factor).astype(out[name].dtype)
    return out
```

```python
from contextlib import ExitStack

import concourse.bass as bass
from concourse import mybir

F32 = mybir.dt.float32
BF16 = mybir.dt.bfloat16
ACT = mybir.ActivationFunctionType
ALU = mybir.AluOpType
AX = mybir.AxisListType

P = 128
S = 2048
NT = S // P
BANK = 512
NC = S // BANK
NH = 16
HD = P // NH
NPIECE = 3
KPROD = NPIECE * NPIECE * HD
MROW = 96
NBUF = 3
AHEAD = 2
VW = 32
NE, FF = 8, 256
LH, LD = 8, 64
INNER = LH * LD
NPAIR = LH // 2
WINDOW = 64
KEYS = P + WINDOW
HID = int(P * 4 * 2 / 3)
LN_EPS = 1e-5
NEG = -1e30


def chunk(c):
    return slice(c * BANK, (c + 1) * BANK)


def bank(psum, n, wide=1):
    return psum[:, n * BANK:(n + wide) * BANK]


def load_inputs(nc, psum, x, x_T, ident, loads):
    with ExitStack() as ctx:
        x_tok = ctx.enter_context(nc.sbuf_tensor("x_tok", [P, NT, P], F32))
        turned = [bank(psum, c) for c in range(NC)]
        x_in = ctx.enter_context(nc.semaphore("x_in"))
        loaded = ctx.enter_context(nc.semaphore("loaded"))
        turned_full = ctx.enter_context(nc.semaphore("turned_full"))
        x_done = ctx.enter_context(nc.semaphore("x_done"))
        block = ctx.enter_context(nc.Block())
        here, there = loads[0::2], loads[1::2]

        @block.sync
        def _(sp):
            sp.dma_start(x_tok[:, :, :], x[0].rearrange("(t p) f -> p t f", p=P)).then_inc(x_in, 16)
            sp.dma_start(ident[0], ident[1]).then_inc(x_in, 16)
            for to, source in here:
                sp.dma_start(to, source).then_inc(loaded, 16)
            sp.wait_ge(loaded, 16 * len(loads))

        @block.scalar
        def _(act):
            for to, source in there:
                act.dma_start(to, source).then_inc(loaded, 16)

        @block.tensor
        def _(pe):
            pe.wait_ge(x_in, 32)
            for t in range(NT):
                m = nc.tensor.transpose(turned[t // 4][:, t % 4 * P:(t % 4 + 1) * P], x_tok[:, t, :], ident[0])
                if t % 4 == 3:
                    m.then_inc(turned_full, 1)

        @block.vector
        def _(dve):
            for c in range(NC):
                dve.wait_ge(turned_full, c + 1)
                nc.vector.tensor_copy(x_T[:, chunk(c)], turned[c][:, :]).then_inc(x_done, 1)


def store_output(nc, psum, x_T, out, ident):
    with ExitStack() as ctx:
        x_tok = ctx.enter_context(nc.sbuf_tensor("out_tok", [P, NT, P], F32))
        turned = [bank(psum, c) for c in range(NC)]
        turned_full = ctx.enter_context(nc.semaphore("out_turned_full"))
        tok_done = ctx.enter_context(nc.semaphore("tok_done"))
        stored = ctx.enter_context(nc.semaphore("stored"))
        block = ctx.enter_context(nc.Block())

        @block.tensor
        def _(pe):
            for t in range(NT):
                m = nc.tensor.transpose(turned[t // 4][:, t % 4 * P:(t % 4 + 1) * P], x_T[:, t * P:(t + 1) * P], ident)
                if t % 4 == 3:
                    m.then_inc(turned_full, 1)

        @block.vector
        def _(dve):
            for c in range(NC):
                dve.wait_ge(turned_full, c + 1)
                nc.vector.tensor_copy(x_tok[:, 4 * c:4 * c + 4, :], turned[c][:, :].rearrange("p (t f) -> p t f", f=P)).then_inc(tok_done, 1)

        @block.sync
        def _(sp):
            for c in range(NC):
                sp.wait_ge(tok_done, c + 1)
                sp.dma_start(out[0, c * BANK:(c + 1) * BANK, :].rearrange("(t p) f -> p t f", p=P),
                             x_tok[:, 4 * c:4 * c + 4, :]).then_inc(stored, 16)
            sp.wait_ge(stored, 16 * NC)


def modulation(nc, psum, layers, mod, gamma, beta, gated):
    NL = len(layers)
    with ExitStack() as ctx:
        c_silu = ctx.enter_context(nc.sbuf_tensor("c_silu", [P, NL], F32))
        sign = ctx.enter_context(nc.sbuf_tensor("gate_sign", [P, NL, 2], F32))
        size = ctx.enter_context(nc.sbuf_tensor("gate_size", [P, NL, 2], F32))
        mod_ps = bank(psum, 0)[:, 0:6 * NL].rearrange("p (l i n) -> p l i n", l=NL, i=2)
        silu_done = ctx.enter_context(nc.semaphore("silu_done"))
        mod_full = ctx.enter_context(nc.semaphore("mod_full"))
        mod_step = ctx.enter_context(nc.semaphore("mod_step"))
        block = ctx.enter_context(nc.Block())

        @block.scalar
        def _(act):
            for l, (c, _) in enumerate(layers):
                nc.scalar.activation(c_silu[:, l:l + 1], c, ACT.Silu).then_inc(silu_done, 1)

        @block.tensor
        def _(pe):
            for l, (_, wmod) in enumerate(layers):
                pe.wait_ge(silu_done, l + 1)
                for n in range(6):
                    m = nc.tensor.matmul(mod_ps[:, l, n // 3, n % 3:n % 3 + 1], wmod[:, n * P:(n + 1) * P],
                                         c_silu[:, l:l + 1], start=True, stop=True)
            m.then_inc(mod_full, 1)

        @block.vector
        def _(dve):
            dve.wait_ge(mod_full, 1)
            nc.vector.tensor_copy(mod[:, :, :, 0], mod_ps[:, :, :, 0])
            nc.vector.tensor_scalar(mod[:, :, :, 1], mod_ps[:, :, :, 1], 1.0, None, ALU.add)
            nc.vector.tensor_scalar(sign[:, :, :], mod_ps[:, :, :, 2], 0.0, 2.0, ALU.is_ge, ALU.mult).then_inc(mod_step, 1)
            nc.vector.tensor_scalar(size[:, :, :], mod_ps[:, :, :, 2], -1.0, 0.25, ALU.mult, ALU.max).then_inc(mod_step, 1)
            dve.wait_ge(mod_step, 2)
            nc.vector.tensor_tensor(size[:, :, :], size[:, :, :], mod_ps[:, :, :, 2], ALU.max).then_inc(mod_step, 1)
            dve.wait_ge(mod_step, 3)
            nc.vector.scalar_tensor_tensor(mod[:, :, :, 2], sign[:, :, :], -1.0, size[:, :, :], ALU.add, ALU.mult).then_inc(mod_step, 1)
            dve.wait_ge(mod_step, 4)
            nc.vector.tensor_tensor(gated[:, 0:1], gamma, mod[:, 0, 0, 2:3], ALU.mult)
            nc.vector.tensor_tensor(gated[:, 1:2], beta, mod[:, 0, 0, 2:3], ALU.mult)


def norm(nc, psum, name, src_T, out_T, mean_of, eps, scale, shift=None, add_to=None):
    centred = shift is not None
    with ExitStack() as ctx:
        sb = lambda n: ctx.enter_context(nc.sbuf_tensor(f"{name}_{n}", [P, S], F32))
        square, std, inv = sb("square"), sb("std"), sb("inv")
        centre = sb("centre") if centred else src_T
        eps_col = ctx.enter_context(nc.sbuf_tensor(f"{name}_eps", [P, 1], F32))
        mean = [bank(psum, c) for c in range(NC)]
        var = [bank(psum, NC + c) for c in range(NC)]
        sem = lambda n: ctx.enter_context(nc.semaphore(f"{name}_{n}"))
        eps_set = sem("eps_set")
        mean_full = sem("mean_full")
        centre_done = sem("centre_done")
        square_done = sem("square_done")
        var_full = sem("var_full")
        std_done = sem("std_done")
        inv_done = sem("inv_done")
        out_step = sem("out_step")
        block = ctx.enter_context(nc.Block())

        @block.tensor
        def _(pe):
            if centred:
                for c in range(NC):
                    nc.tensor.matmul(mean[c][:, :], mean_of, src_T[:, chunk(c)], start=True, stop=True).then_inc(mean_full, 1)
            for c in range(NC):
                pe.wait_ge(square_done, c + 1)
                nc.tensor.matmul(var[c][:, :], mean_of, square[:, chunk(c)], start=True, stop=True).then_inc(var_full, 1)

        @block.scalar
        def _(act):
            for c in range(NC):
                if centred:
                    act.wait_ge(centre_done, c + 1)
                nc.scalar.activation(square[:, chunk(c)], centre[:, chunk(c)], ACT.Square).then_inc(square_done, 1)
            act.wait_ge(eps_set, 1)
            for c in range(NC):
                act.wait_ge(var_full, c + 1)
                nc.scalar.activation(std[:, chunk(c)], var[c][:, :], ACT.Sqrt, bias=eps_col[:, :]).then_inc(std_done, 1)

        @block.vector
        def _(dve):
            nc.vector.memset(eps_col[:, :], eps).then_inc(eps_set, 1)
            if centred:
                for c in range(NC):
                    dve.wait_ge(mean_full, c + 1)
                    nc.vector.tensor_tensor(centre[:, chunk(c)], src_T[:, chunk(c)], mean[c][:, :], ALU.subtract).then_inc(centre_done, 1)
                dve.wait_ge(centre_done, NC)
            for c in range(NC):
                dve.wait_ge(std_done, c + 1)
                nc.vector.reciprocal(inv[:, chunk(c)], std[:, chunk(c)]).then_inc(inv_done, 1)
                dve.wait_ge(inv_done, c + 1)
                to = out_T[:, chunk(c)] if add_to is None else inv[:, chunk(c)]
                nc.vector.scalar_tensor_tensor(to, centre[:, chunk(c)], scale, inv[:, chunk(c)], ALU.mult, ALU.mult).then_inc(out_step, 1)
                if centred:
                    dve.wait_ge(out_step, c + 1)
                    if add_to is None:
                        nc.vector.tensor_scalar(to, to, shift, None, ALU.add)
                    else:
                        nc.vector.scalar_tensor_tensor(add_to[:, chunk(c)], to, shift, add_to[:, chunk(c)], ALU.add, ALU.add)


def project(nc, psum, name, h_T, wq, wk, wv, q_dram, k_dram, v_tok, bias=None, rope=None):
    with ExitStack() as ctx:
        raw = [[bank(psum, 2 * b + n) for n in range(2)] for b in range(2)]
        v_ps = [bank(psum, 4 + b) for b in range(2)]
        full = ctx.enter_context(nc.sbuf_tensor(f"{name}_full", [P, 2, BANK], F32))
        rest = ctx.enter_context(nc.sbuf_tensor(f"{name}_rest", [P, 2, BANK], F32))
        turn = ctx.enter_context(nc.sbuf_tensor(f"{name}_turn", [P, 2, BANK], F32))
        piece = ctx.enter_context(nc.sbuf_tensor(f"{name}_piece", [P, 2, NPIECE, BANK], BF16))
        sem = lambda n: ctx.enter_context(nc.semaphore(f"{name}_{n}"))
        raw_full = sem("raw_full")
        raw_free = sem("raw_free")
        full_done = sem("full_done")
        turn_done = sem("turn_done")
        piece1 = sem("piece1")
        rest_done = sem("rest_done")
        piece2 = sem("piece2")
        piece3 = sem("piece3")
        v_full = sem("v_full")
        v_free = sem("v_free")
        stored = [sem(f"stored{b}") for b in range(2)]
        block = ctx.enter_context(nc.Block())
        work = [(c, i) for c in range(NC) for i in range(2)]

        @block.tensor
        def _(pe):
            for n, (c, i) in enumerate(work):
                if n >= 2:
                    pe.wait_ge(raw_free, n - 1)
                m = nc.tensor.matmul(raw[n % 2][0][:, :], (wq, wk)[i], h_T[:, chunk(c)], start=True, stop=True)
                if rope:
                    m = nc.tensor.matmul(raw[n % 2][1][:, :], rope[i], h_T[:, chunk(c)], start=True, stop=True)
                m.then_inc(raw_full, 1)
            for t in range(NT):
                if t % 4 == 0 and t >= 8:
                    pe.wait_ge(v_free, t // 4 - 1)
                m = nc.tensor.matmul(v_ps[t // 4 % 2][:, t % 4 * P:(t % 4 + 1) * P], h_T[:, t * P:(t + 1) * P], wv, start=True, stop=True)
                if t % 4 == 3:
                    m.then_inc(v_full, 1)

        @block.vector
        def _(dve):
            for n, (c, i) in enumerate(work):
                to, ps = full[:, n % 2, :], raw[n % 2]
                dve.wait_ge(raw_full, n + 1)
                if rope:
                    nc.vector.tensor_tensor(to, ps[0][:, :], rope[2][:, chunk(c)], ALU.mult).then_inc(turn_done, 1)
                    nc.vector.tensor_tensor(turn[:, n % 2, :], ps[1][:, :], rope[3][:, chunk(c)], ALU.mult).then_inc(raw_free, 1)
                    dve.wait_ge(turn_done, n + 1)
                    dve.wait_ge(raw_free, n + 1)
                    nc.vector.tensor_tensor(to, to, turn[:, n % 2, :], ALU.add).then_inc(full_done, 1)
                elif bias:
                    nc.vector.tensor_scalar(to, ps[0][:, :], bias[i], None, ALU.add).then_inc(raw_free, 1)
                else:
                    nc.vector.tensor_copy(to, ps[0][:, :]).then_inc(raw_free, 1)
                dve.wait_ge(full_done if rope else raw_free, n + 1)
                dve.wait_ge(piece1, n + 1)
                if n >= 2:
                    dve.wait_ge(piece3, n - 1)
                nc.vector.tensor_tensor(rest[:, n % 2, :], to, piece[:, n % 2, 0, :], ALU.subtract).then_inc(rest_done, 1)
            for c in range(NC):
                dve.wait_ge(v_full, c + 1)
                to, ps = v_tok[:, 4 * c:4 * c + 4, :], v_ps[c % 2][:, :].rearrange("p (t f) -> p t f", f=P)
                if bias:
                    nc.vector.tensor_tensor(to, ps, bias[2][:, :].unsqueeze(1).to_broadcast([P, 4, P]), ALU.add).then_inc(v_free, 1)
                else:
                    nc.vector.tensor_copy(to, ps).then_inc(v_free, 1)

        @block.scalar
        def _(act):
            for n, (c, i) in enumerate(work):
                act.wait_ge(full_done if rope else raw_free, n + 1)
                if n >= 2:
                    act.wait_ge(stored[n % 2], 16 * (n // 2))
                nc.scalar.activation(piece[:, n % 2, 0, :], full[:, n % 2, :], ACT.Copy).then_inc(piece1, 1)
                act.wait_ge(rest_done, n + 1)
                nc.scalar.activation(piece[:, n % 2, 1, :], rest[:, n % 2, :], ACT.Copy).then_inc(piece2, 1)

        @block.gpsimd
        def _(pool):
            for n, (c, i) in enumerate(work):
                pool.wait_ge(piece2, n + 1)
                nc.gpsimd.tensor_tensor(piece[:, n % 2, 2, :], rest[:, n % 2, :], piece[:, n % 2, 1, :], ALU.subtract).then_inc(piece3, 1)

        @block.sync
        def _(sp):
            for n, (c, i) in enumerate(work):
                sp.wait_ge(piece3, n + 1)
                sp.dma_start((q_dram, k_dram)[i][:, :, chunk(c)].rearrange("n p s -> p n s"),
                             piece[:, n % 2, :, :]).then_inc(stored[n % 2], 16)
            for b in range(2):
                sp.wait_ge(stored[b], 16 * NC)


def divide_by_sums(nc, psum, name, z_T, den, head_rows, x_T, wo=None, gate=None, regroup=None):
    with ExitStack() as ctx:
        den_ps = [bank(psum, c) for c in range(NC)]
        out_ps = [bank(psum, NC + c) for c in range(NC)]
        inv = ctx.enter_context(nc.sbuf_tensor(f"{name}_inv", [NH, S], F32))
        sem = lambda n: ctx.enter_context(nc.semaphore(f"{name}_{n}"))
        inv_done = sem("inv_done")
        den_full = sem("den_full")
        z_done = sem("z_done")
        out_full = sem("out_full")
        block = ctx.enter_context(nc.Block())

        @block.tensor
        def _(pe):
            for c in range(NC):
                pe.wait_ge(inv_done, c + 1)
                nc.tensor.matmul(den_ps[c][:, :], head_rows, inv[:, chunk(c)], start=True, stop=True).then_inc(den_full, 1)
            if wo is not None:
                for c in range(NC):
                    pe.wait_ge(z_done, c + 1)
                    nc.tensor.matmul(out_ps[c][:, :], wo, z_T[:, chunk(c)], start=True, stop=True).then_inc(out_full, 1)
            else:
                pe.wait_ge(z_done, NC)
                spread = z_T.rearrange("p (r g) -> p g r", g=NH)
                for h in range(NH):
                    for k in range(4):
                        for quadrant in range(4):
                            at = h * 32 + 24 - HD * k
                            m = nc.tensor.matmul(out_ps[h // 4][32 * quadrant:32 * quadrant + 32, h % 4 * P:(h % 4 + 1) * P],
                                                 regroup[:, at:at + 32], spread[:, 4 * quadrant + k, :],
                                                 start=k == 0, stop=k == 3, skip_group_check=True)
                    if h % 4 == 3:
                        m.then_inc(out_full, 1)

        @block.vector
        def _(dve):
            for c in range(NC):
                nc.vector.reciprocal(inv[:, chunk(c)], den[:, chunk(c)]).then_inc(inv_done, 1)
            for c in range(NC):
                dve.wait_ge(den_full, c + 1)
                nc.vector.tensor_tensor(z_T[:, chunk(c)], z_T[:, chunk(c)], den_ps[c][:, :], ALU.mult).then_inc(z_done, 1)
            for c in range(NC):
                dve.wait_ge(out_full, c + 1 if wo is not None else NC)
                if wo is not None:
                    nc.vector.scalar_tensor_tensor(x_T[:, chunk(c)], out_ps[c][:, :], gate, x_T[:, chunk(c)], ALU.mult, ALU.add)
                else:
                    nc.vector.tensor_tensor(z_T[:, chunk(c)], x_T[:, chunk(c)], out_ps[c][:, :], ALU.add)


def attention(nc, psum, name, causal, scale, q_dram, k_dram, v_tok, z_dram, den_dram, z_T, den, ident_bf, mask_qk, mask_kq, keep_kq=None):
    with ExitStack() as ctx:
        sb = lambda n, s, d=F32: ctx.enter_context(nc.sbuf_tensor(f"{name}_{n}", s, d))
        sem = lambda n: ctx.enter_context(nc.semaphore(f"{name}_{n}"))
        q_stack = [sb(f"q_stack{b}", [P, S], BF16) for b in range(NBUF)]
        k_stack = [sb(f"k_stack{b}", [P, S], BF16) for b in range(NBUF)]
        probs = [sb(f"probs{b}", [P, S]) for b in range(2)]
        diag = sb("diag", [P, P])
        v_one = sb("v_one", [P, NT, VW])
        v_only = sb("v_only", [P, NT, VW])
        one_only = sb("one_only", [P, VW])
        part_max = sb("part_max", [P, NT, 4])
        neg_max = sb("neg_max", [P, NT])
        rest1 = sb("rest1", [P, NT])
        rest2 = sb("rest2", [P, NT])
        max_rows = sb("max_rows", [P, NT, 32], BF16)
        zero = sb("zero", [P, 4])
        z_sb = sb("z_sb", [P, BANK])
        st = [bank(psum, 2 * b, 2) for b in range(2)]
        mx = [bank(psum, 4 + b) for b in range(3)]
        z_ps = bank(psum, 7)

        stack_in = [sem(f"stack_in{b}") for b in range(NBUF)]
        buffers_set = sem("buffers_set")
        v_in = sem("v_in")
        mx_full = sem("mx_full")
        mx_free = sem("mx_free")
        max_ready = sem("max_ready")
        max_split = sem("max_split")
        pool_step = sem("pool_step")
        st_full = sem("st_full")
        st_free = sem("st_free")
        pv_done = sem("pv_done")
        diag_done = sem("diag_done")
        z_free = sem("z_free")
        z_in = sem("z_in")
        z_out = sem("z_out")

        order = [NT - 1 - u if causal else u for u in range(NT)]
        mx_tiles = [(qt // 4 + 1) if causal else 4 for qt in order]
        mx_before = [sum(mx_tiles[:u]) for u in range(NT)]
        MX = sum(mx_tiles)
        group = [order[4 * j] // 4 for j in range(4)]
        halves = [[hf for hf in range(2) if not causal or kb * P < (hf + 1) * 1024] for kb in range(NT)]

        def ring_of(with_next):
            ring = []
            for kb in range(NT):
                ring += [("exp", kb, hf) for hf in halves[kb]]
                if with_next and (kb + AHEAD) % 4 == 0:
                    ring.append(("max", (kb + AHEAD) // 4 - 1, 0))
            return ring

        rings = {w: ring_of(w) for w in (True, False)}
        places = {w: {r: n for n, r in enumerate(rings[w])} for w in rings}
        E = len(rings[True])
        assert E % 2 == 0 and AHEAD in (1, 2, 3)
        STACK = 16 * (NPIECE * NPIECE + NPIECE)
        ZOUT = 16 * 8
        G = 4

        def width(qt, c):
            end = (qt + 1) * P if causal else S
            return min(BANK, end - c * BANK)

        block = ctx.enter_context(nc.Block())

        @block.sync
        def _(sp):
            def load(h, b):
                for stack, dram in ((q_stack[b], q_dram), (k_stack[b], k_dram)):
                    rows = dram[:, bass.ds(h * HD, HD), :]
                    if stack is q_stack[b]:
                        for i in range(NPIECE):
                            for j in range(NPIECE):
                                r = (i * NPIECE + j) * HD
                                sp.dma_start(stack[r:r + HD, :], rows[i]).then_inc(stack_in[b], 16)
                    else:
                        for i in range(NPIECE):
                            r = i * NPIECE * HD
                            sp.dma_start(stack[r:r + NPIECE * HD, :], rows).then_inc(stack_in[b], 16)

            def body(h, b, load_more):
                sp.wait_ge(pv_done, (h + 1) * NT)
                if load_more:
                    load(h + NBUF, b)
                sp.wait_ge(z_free, h + 1)
                tiles = lambda rows: rows.rearrange("r (c j i) -> r c j i", j=4, i=P)
                for j in range(4):
                    part = lambda r0, r1: z_sb[32 * j + r0:32 * j + r1, :].rearrange("r (c i) -> r c i", i=P)
                    sp.dma_start(tiles(z_dram[bass.ds(h * HD, HD), :])[:, :, j, :], part(0, HD)).then_inc(z_out, 16)
                    sp.dma_start(tiles(den_dram[bass.ds(h, 1), :])[:, :, j, :], part(HD, HD + 1)).then_inc(z_out, 16)

            sp.wait_ge(buffers_set, 2)
            for b in range(NBUF):
                load(b, b)
            with sp.Fori(0, (NH - 1) // NBUF - 1) as i:
                for r in range(NBUF):
                    body(i * NBUF + r, r, True)
            body(NH - 4, 0, True)
            for h in range(NH - 3, NH):
                body(h, h % NBUF, False)
            sp.wait_ge(z_out, ZOUT * NH)
            sp.dma_start(z_T, z_dram).then_inc(z_in, 16)
            sp.dma_start(den, den_dram).then_inc(z_in, 16)
            sp.wait_ge(z_in, 32)


        @block.gpsimd
        def _(pool):
            def values(h):
                src = v_tok[:, :, bass.ds(h * HD, HD)]
                nc.gpsimd.tensor_copy(v_one[:, :, 0:HD], src)
                nc.gpsimd.tensor_copy(v_only[:, :, 0:HD], src).then_inc(v_in, 1)

            pool.wait_ge(buffers_set, 2)

            def split(h, j):
                n = slice(4 * group[j], 4 * group[j] + 4)
                base = (h * 4 + j) * 4
                pool.wait_ge(max_ready, h * 4 + j + 1)
                nc.gpsimd.tensor_tensor(max_rows[:, n, 0], neg_max[:, n], zero[:, 0:4], ALU.add).then_inc(pool_step, 1)
                pool.wait_ge(pool_step, base + 1)
                nc.gpsimd.tensor_tensor(rest1[:, n], neg_max[:, n], max_rows[:, n, 0], ALU.subtract).then_inc(pool_step, 1)
                pool.wait_ge(pool_step, base + 2)
                nc.gpsimd.tensor_tensor(max_rows[:, n, 1], rest1[:, n], zero[:, 0:4], ALU.add).then_inc(pool_step, 1)
                pool.wait_ge(pool_step, base + 3)
                nc.gpsimd.tensor_tensor(rest2[:, n], rest1[:, n], max_rows[:, n, 1], ALU.subtract).then_inc(pool_step, 1)
                pool.wait_ge(pool_step, base + 4)
                nc.gpsimd.tensor_tensor(max_rows[:, n, 2], rest2[:, n], zero[:, 0:4], ALU.add).then_inc(max_split, 1)

            def body(h, with_next):
                for kb in range(NT):
                    if not causal:
                        pool.wait_ge(st_free, G + h * E + places[with_next][("exp", kb, kb // 8)] + 1)
                        if kb > 0:
                            pool.wait_ge(pv_done, h * NT + kb)
                        nc.gpsimd.tensor_tensor(diag[:, :], probs[kb % 2][:, kb * P:kb * P + P], keep_kq,
                                                ALU.mult).then_inc(diag_done, 1)
                    if with_next and kb + AHEAD < NT and (kb + AHEAD) % 4 == 3:
                        split(h + 1, (kb + AHEAD) // 4)
                if with_next:
                    pool.wait_ge(pv_done, h * NT + NT)
                    pool.wait_ge(buffers_set, 2)
                    values(h + 1)

            values(0)
            for j in range(4):
                split(0, j)
            with pool.Fori(0, NH - 1) as h:
                body(h, True)
            body(NH - 1, False)

        @block.vector
        def _(dve):
            for b in range(NBUF):
                nc.vector.memset(q_stack[b][64:128, :], 0.0)
                nc.vector.memset(k_stack[b][64:128, :], 0.0)
            nc.vector.memset(max_rows[:, :, :], 0.0)
            nc.vector.memset(v_one[:, :, :], 0.0)
            nc.vector.memset(v_only[:, :, :], 0.0)
            nc.vector.memset(zero[:, :], 0.0)
            nc.vector.memset(one_only[:, :], 0.0).then_inc(buffers_set, 1)
            dve.wait_ge(buffers_set, 1)
            for b in range(NBUF):
                nc.vector.memset(k_stack[b][MROW:MROW + NPIECE, :], 1.0)
            nc.vector.memset(v_one[:, :, HD:HD + 1], 1.0)
            nc.vector.memset(one_only[:, HD:HD + 1], 1.0).then_inc(buffers_set, 1)

            def maxima(h, r):
                for u, qt in enumerate(order):
                    for c in range(mx_tiles[u]):
                        n = mx_before[u] + c
                        dve.wait_ge(mx_full, h * MX + n + 1)
                        nc.vector.tensor_reduce(part_max[:, qt, c:c + 1], mx[(r * MX + n) % 3][:, 0:width(qt, c)],
                                                AX.X, ALU.max).then_inc(mx_free, 1)
                    if u % 4 == 3:
                        g = qt // 4
                        dve.wait_ge(mx_free, h * MX + n + 1)
                        nc.vector.tensor_reduce(neg_max[:, 4 * g:4 * g + 4], part_max[:, 4 * g:4 * g + 4, 0:mx_tiles[u]],
                                                AX.X, ALU.max, negate=True).then_inc(max_ready, 1)

            maxima(0, 0)
            with dve.Fori(0, (NH - 1) // NBUF) as i:
                for r in range(NBUF):
                    maxima(i * NBUF + 1 + r, 1 + r)

        @block.scalar
        def _(act):
            def body(h, b, with_next):
                for e, (kind, kb, hf) in enumerate(rings[with_next]):
                    n = G + h * E + e
                    slot = (G + e) % 2
                    if kind == "exp":
                        lo = max(kb * P, hf * 1024) if causal else hf * 1024
                        hi = (hf + 1) * 1024
                        act.wait_ge(st_full, n + 1)
                        if hf == halves[kb][0] and not (kb < 2 and isinstance(h, int) and h == 0):
                            act.wait_ge(pv_done, h * NT + kb - 1)
                        nc.scalar.activation(probs[kb % 2][:, lo:hi], st[slot][:, lo - hf * 1024:1024], ACT.Exp,
                                             scale=scale).then_inc(st_free, 1)
                    else:
                        act.wait_ge(st_full, n + 1)
                        g = group[kb]
                        nc.scalar.activation(q_stack[(b + 1) % NBUF][MROW:P, 4 * g * P:4 * (g + 1) * P],
                                             st[slot][MROW:P, 0:BANK // 2].bitcast(BF16), ACT.Copy).then_inc(st_free, 1)
                act.wait_ge(pv_done, (h + 1) * NT)
                if not (isinstance(h, int) and h == 0):
                    act.wait_ge(z_out, h * ZOUT)
                nc.scalar.activation(z_sb[:, :], z_ps[:, :], ACT.Copy).then_inc(z_free, 1)

            for j in range(4):
                g = group[j]
                act.wait_ge(st_full, j + 1)
                nc.scalar.activation(q_stack[0][MROW:P, 4 * g * P:4 * (g + 1) * P],
                                     st[j % 2][MROW:P, 0:BANK // 2].bitcast(BF16), ACT.Copy).then_inc(st_free, 1)
            body(0, 0, True)
            with act.Fori(0, NH // NBUF - 1) as i:
                for r in range(NBUF):
                    body(i * NBUF + 1 + r, (1 + r) % NBUF, True)
            for h in range(NH - 3, NH):
                body(h, h % NBUF, h < NH - 1)

        @block.tensor
        def _(pe):
            def max_tiles(h, r, u, some):
                qt, b = order[u], r % NBUF
                for c in some:
                    if c >= mx_tiles[u]:
                        continue
                    n, w = mx_before[u] + c, width(qt, c)
                    diagonal = causal and c == qt // 4
                    if not (isinstance(h, int) and h * MX + n < 3):
                        pe.wait_ge(mx_free, h * MX + n - 2)
                    tile = mx[(r * MX + n) % 3]
                    m = nc.tensor.matmul(tile[:, 0:w], q_stack[b][0:KPROD, qt * P:(qt + 1) * P],
                                         k_stack[b][0:KPROD, c * BANK:c * BANK + w], start=True, stop=not diagonal,
                                         skip_group_check=True)
                    if diagonal:
                        m = nc.tensor.matmul(tile[:, w - P:w], ident_bf, mask_qk, start=False, stop=True,
                                             skip_group_check=True)
                    m.then_inc(mx_full, 1)

            def max_transpose(h, j, n, slot):
                pe.wait_ge(max_split, h * 4 + j + 1)
                if not (isinstance(n, int) and n < 2):
                    pe.wait_ge(st_free, n - 1)
                out = st[slot][MROW:P, 0:BANK // 2].bitcast(BF16)
                for t in range(4):
                    m = nc.tensor.transpose(out[:, t * P:(t + 1) * P], max_rows[:, 4 * group[j] + t, :], ident_bf)
                m.then_inc(st_full, 1)

            def scores(h, b, kb, hf, with_next):
                e = places[with_next][("exp", kb, hf)]
                n = G + h * E + e
                slot = (G + e) % 2
                pe.wait_ge(st_free, n - 1)
                lo = max(kb * P, hf * 1024) if causal else hf * 1024
                for c in range(2):
                    a, z = max(lo, hf * 1024 + c * BANK), hf * 1024 + (c + 1) * BANK
                    if a >= z:
                        continue
                    diagonal = causal and a == kb * P
                    m = nc.tensor.matmul(st[slot][:, a - hf * 1024:z - hf * 1024], k_stack[b][:, kb * P:(kb + 1) * P],
                                         q_stack[b][:, a:z], start=True, stop=not diagonal, skip_group_check=True)
                    if diagonal:
                        m = nc.tensor.matmul(st[slot][:, a - hf * 1024:a - hf * 1024 + P], ident_bf, mask_kq,
                                             start=False, stop=True, skip_group_check=True)
                m.then_inc(st_full, 1)

            def products(h, kb, with_next):
                pe.wait_ge(st_free, G + h * E + places[with_next][("exp", kb, halves[kb][-1])] + 1)
                if kb == 0:
                    pe.wait_ge(v_in, h + 1)
                    if not (isinstance(h, int) and h == 0):
                        pe.wait_ge(z_free, h)
                pr = probs[kb % 2][:, :].rearrange("p (c j i) -> p c j i", j=4, i=P)
                done = []

                def part(j, c0, c1, weights, start):
                    if c0 < c1:
                        done.append(nc.tensor.matmul(z_ps[32 * j:32 * j + VW, c0 * P:c1 * P], weights,
                                                     pr[:, c0:c1, j, :], start=start, stop=kb == NT - 1,
                                                     skip_group_check=True))

                mid = [max(0, -(-(kb - j) // 4)) for j in range(4)]
                for j in range(4):
                    part(j, mid[j], 4, v_one[:, kb, :] if causal else one_only[:, :], kb == 0)
                if not causal:
                    for j in range(4):
                        part(j, 0, mid[j], v_one[:, kb, :], False)
                    pe.wait_ge(diag_done, h * NT + kb + 1)
                    j, c = kb % 4, kb // 4
                    done.append(nc.tensor.matmul(z_ps[32 * j:32 * j + VW, c * P:(c + 1) * P], v_only[:, kb, :],
                                                 diag[:, :], start=False, stop=kb == NT - 1, skip_group_check=True))
                done[-1].then_inc(pv_done, 1)

            def body(h, r, loads, next1=True, next2=True):
                b = r % NBUF
                for kb in range(NT):
                    ahead, u = divmod(kb + AHEAD, NT)
                    go = next2 if ahead else next1
                    if ahead and u == 0 and next2:
                        pe.wait_ge(stack_in[(r + 2) % NBUF], loads * STACK)
                    first, *second = halves[kb]
                    scores(h, b, kb, first, next1)
                    if go:
                        max_tiles(h + 1 + ahead, r + 1 + ahead, u, (0, 1))
                    if kb > 0:
                        products(h, kb - 1, next1)
                    if second:
                        scores(h, b, kb, second[0], next1)
                    if go:
                        max_tiles(h + 1 + ahead, r + 1 + ahead, u, (2, 3))
                    if next1 and (kb + AHEAD) % 4 == 0:
                        j = (kb + AHEAD) // 4 - 1
                        e = places[True][("max", j, 0)]
                        max_transpose(h + 1, j, G + h * E + e, (G + e) % 2)
                products(h, NT - 1, next1)

            pe.wait_ge(buffers_set, 2)
            pe.wait_ge(stack_in[0], STACK)
            for u in range(NT):
                max_tiles(0, 0, u, range(4))
                if u % 4 == 3:
                    max_transpose(0, u // 4, u // 4, u // 4 % 2)
            pe.wait_ge(stack_in[1], STACK)
            for u in range(AHEAD):
                max_tiles(1, 1, u, range(4))
            pe.wait_ge(st_free, G)
            body(0, 0, 1)
            with pe.Fori(0, NH // NBUF - 1) as i:
                for r in range(NBUF):
                    body(i * NBUF + 1 + r, 1 + r, i + 2)
            for h in range(NH - 3, NH):
                body(h, h % NBUF, (h + 2) // NBUF + 1, h + 1 < NH, h + 2 < NH)

def router(nc, psum, h_T, gate_w, rank, ident, w_rows):
    with ExitStack() as ctx:
        sb = lambda n, d=F32: ctx.enter_context(nc.sbuf_tensor(f"route_{n}", [P, NT, NE], d))
        logits, is_top, order, taken, left = sb("logits"), sb("is_top"), sb("order"), [sb("first"), sb("second")], sb("left")
        share = sb("share")
        col = lambda n: ctx.enter_context(nc.sbuf_tensor(f"route_{n}", [P, NT], F32))
        top, best, gap, odds, total, w1, w2 = [col("top1"), col("top2")], col("best"), col("gap"), col("odds"), col("total"), col("w1"), col("w2")
        pieces = ctx.enter_context(nc.sbuf_tensor("route_pieces", [P, NT, NPIECE, NE], BF16))
        logit_ps = bank(psum, 0)[:, 0:NT * NE].rearrange("p (t e) -> p t e", e=NE)
        row_ps = [bank(psum, 1 + b)[0:NPIECE * NE, :].bitcast(BF16) for b in range(2)]
        logits_full = ctx.enter_context(nc.semaphore("logits_full"))
        rows_clear = ctx.enter_context(nc.semaphore("rows_clear"))
        step = ctx.enter_context(nc.semaphore("route_step"))
        gap_done = ctx.enter_context(nc.semaphore("gap_done"))
        odds_done = ctx.enter_context(nc.semaphore("odds_done"))
        pieces_done = ctx.enter_context(nc.semaphore("pieces_done"))
        rows_full = ctx.enter_context(nc.semaphore("rows_full"))
        wide = lambda a: a[:, :].unsqueeze(2).to_broadcast([P, NT, NE])
        block = ctx.enter_context(nc.Block())

        @block.tensor
        def _(pe):
            for t in range(NT):
                m = nc.tensor.matmul(logit_ps[:, t, :], h_T[:, t * P:(t + 1) * P], gate_w, start=True, stop=True)
            m.then_inc(logits_full, 1)
            pe.wait_ge(pieces_done, 1)
            for t in range(NT):
                m = nc.tensor.transpose(row_ps[t // 8][:, t % 8 * P:(t % 8 + 1) * P],
                                        pieces[:, t, :, :].rearrange("p n e -> p (n e)"), ident)
                if t % 8 == 7:
                    m.then_inc(rows_full, 1)

        @block.scalar
        def _(act):
            act.wait_ge(gap_done, 1)
            nc.scalar.activation(odds[:, :], gap[:, :], ACT.Exp).then_inc(odds_done, 1)

        @block.vector
        def _(dve):
            nc.vector.memset(w_rows[:, :], 0.0).then_inc(rows_clear, 1)
            dve.wait_ge(logits_full, 1)
            nc.vector.tensor_copy(logits[:, :, :], logit_ps[:, :, :]).then_inc(step, 1)
            n = 1
            for r, source in enumerate((logits, left)):
                dve.wait_ge(step, n)
                nc.vector.tensor_reduce(top[r][:, :], source[:, :, :], AX.X, ALU.max).then_inc(step, 1)
                dve.wait_ge(step, n + 1)
                nc.vector.tensor_tensor(is_top[:, :, :], source[:, :, :], wide(top[r]), ALU.is_equal).then_inc(step, 1)
                dve.wait_ge(step, n + 2)
                nc.vector.tensor_tensor(order[:, :, :], is_top[:, :, :], rank.unsqueeze(1).to_broadcast([P, NT, NE]), ALU.mult).then_inc(step, 1)
                dve.wait_ge(step, n + 3)
                nc.vector.tensor_reduce(best[:, :], order[:, :, :], AX.X, ALU.max).then_inc(step, 1)
                dve.wait_ge(step, n + 4)
                nc.vector.tensor_tensor(taken[r][:, :, :], order[:, :, :], wide(best), ALU.is_equal).then_inc(step, 1)
                n += 5
                if r == 0:
                    dve.wait_ge(step, n)
                    nc.vector.scalar_tensor_tensor(left[:, :, :], taken[0][:, :, :], NEG, logits[:, :, :], ALU.mult, ALU.add).then_inc(step, 1)
                    n += 1
            nc.vector.tensor_tensor(gap[:, :], top[1][:, :], top[0][:, :], ALU.subtract).then_inc(gap_done, 1)
            dve.wait_ge(odds_done, 1)
            nc.vector.tensor_scalar(total[:, :], odds[:, :], 1.0, None, ALU.add).then_inc(step, 1)
            dve.wait_ge(step, n + 1)
            nc.vector.reciprocal(w1[:, :], total[:, :]).then_inc(step, 1)
            dve.wait_ge(step, n + 2)
            nc.vector.tensor_tensor(w2[:, :], odds[:, :], w1[:, :], ALU.mult).then_inc(step, 1)
            dve.wait_ge(step, n + 3)
            nc.vector.tensor_tensor(share[:, :, :], taken[0][:, :, :], wide(w1), ALU.mult)
            nc.vector.tensor_tensor(left[:, :, :], taken[1][:, :, :], wide(w2), ALU.mult).then_inc(step, 1)
            dve.wait_ge(step, n + 4)
            nc.vector.tensor_tensor(share[:, :, :], share[:, :, :], left[:, :, :], ALU.add).then_inc(step, 1)
            for i in range(NPIECE):
                dve.wait_ge(step, n + 5 + 2 * i)
                last = nc.vector.tensor_copy(pieces[:, :, i, :], share[:, :, :])
                if i < NPIECE - 1:
                    last.then_inc(step, 1)
                    dve.wait_ge(step, n + 6 + 2 * i)
                    nc.vector.tensor_tensor(share[:, :, :], share[:, :, :], pieces[:, :, i, :], ALU.subtract).then_inc(step, 1)
                else:
                    last.then_inc(pieces_done, 1)
            dve.wait_ge(rows_clear, 1)
            for b in range(2):
                dve.wait_ge(rows_full, b + 1)
                nc.vector.tensor_copy(w_rows[0:NPIECE * NE, b * 2 * BANK:(b + 1) * 2 * BANK], row_ps[b][:, :])


def experts(nc, psum, h_T, w13, w2, w_rows, pick, y_T, x_T, gate):
    with ExitStack() as ctx:
        g_ps, u_ps, w_ps = ([bank(psum, 2 * n + b) for b in range(2)] for n in range(3))
        out_ps = bank(psum, 6)
        sb = lambda n: [ctx.enter_context(nc.sbuf_tensor(f"moe_{n}{b}", [P, BANK], F32)) for b in range(2)]
        silu, up, act_w = sb("silu"), sb("up"), sb("act_w")
        total = sb("total")[0]
        sem = lambda n: ctx.enter_context(nc.semaphore(f"moe_{n}"))
        up_full = sem("up_full")
        w_full = sem("w_full")
        silu_done = sem("silu_done")
        up_done = sem("up_done")
        act_done = sem("act_done")
        down_done = sem("down_done")
        out_free = sem("out_free")
        N = 2 * NE
        block = ctx.enter_context(nc.Block())

        @block.tensor
        def _(pe):
            def down(c, n):
                pe.wait_ge(act_done, c * N + n + 1)
                nc.tensor.matmul(out_ps[:, :], w2[:, n // 2, n % 2, :], act_w[n % 2][:, :], start=n == 0,
                                 stop=n == N - 1).then_inc(down_done, 1)

            def body(c, some_before):
                at = bass.ds(c * BANK, BANK)
                for n in range(N):
                    e, f = divmod(n, 2)
                    if some_before or n >= 2:
                        pe.wait_ge(up_done, c * N + n - 1)
                    if f == 0:
                        if some_before or e >= 2:
                            pe.wait_ge(act_done, c * N + n - 2)
                        nc.tensor.matmul(w_ps[e % 2][:, :], pick[:, e, :], w_rows[:, at], start=True, stop=True).then_inc(w_full, 1)
                    nc.tensor.matmul(g_ps[n % 2][:, :], w13[:, e, f * P:(f + 1) * P], h_T[:, at], start=True, stop=True)
                    nc.tensor.matmul(u_ps[n % 2][:, :], w13[:, e, FF + f * P:FF + (f + 1) * P], h_T[:, at],
                                     start=True, stop=True).then_inc(up_full, 1)
                    if n >= 1:
                        if n == 1 and some_before:
                            pe.wait_ge(out_free, c)
                        down(c, n - 1)
                down(c, N - 1)

            body(0, False)
            with pe.Fori(1, NC) as c:
                body(c, True)

        @block.scalar
        def _(act):
            def body(c):
                for n in range(N):
                    act.wait_ge(up_full, c * N + n + 1)
                    nc.scalar.activation(silu[n % 2][:, :], g_ps[n % 2][:, :], ACT.Silu).then_inc(silu_done, 1)

            with act.Fori(0, NC) as c:
                body(c)

        @block.vector
        def _(dve):
            def body(c, some_before):
                at = bass.ds(c * BANK, BANK)
                for n in range(N):
                    dve.wait_ge(silu_done, c * N + n + 1)
                    nc.vector.tensor_tensor(up[n % 2][:, :], silu[n % 2][:, :], u_ps[n % 2][:, :], ALU.mult).then_inc(up_done, 1)
                    dve.wait_ge(up_done, c * N + n + 1)
                    dve.wait_ge(w_full, c * NE + n // 2 + 1)
                    if some_before or n >= 2:
                        dve.wait_ge(down_done, c * N + n - 1)
                    nc.vector.tensor_tensor(act_w[n % 2][:, :], up[n % 2][:, :], w_ps[n // 2 % 2][:, :], ALU.mult).then_inc(act_done, 1)
                dve.wait_ge(down_done, c * N + N)
                nc.vector.tensor_tensor(total[:, :], y_T[:, at], out_ps[:, :], ALU.add).then_inc(out_free, 1)
                dve.wait_ge(out_free, c + 1)
                nc.vector.scalar_tensor_tensor(x_T[:, at], total[:, :], gate, x_T[:, at], ALU.mult, ALU.add)

            body(0, False)
            with dve.Fori(1, NC) as c:
                body(c, True)


def shift_tokens(nc, name, src_T, out_T):
    with ExitStack() as ctx:
        block = ctx.enter_context(nc.Block())

        @block.vector
        def _(dve):
            nc.vector.tensor_copy(out_T[0:P // 2, :], src_T[0:P // 2, :])

        @block.scalar
        def _(act):
            nc.scalar.activation(out_T[P // 2:P, 1:S], src_T[P // 2:P, 0:S - 1], ACT.Copy)

        @block.gpsimd
        def _(pool):
            nc.gpsimd.memset(out_T[P // 2:P, 0:1], 0.0)


def local_attention(nc, psum, name, hs_T, w_in, w_v, w_out, tables, scales, sum_of, bands, ident, ident_bf, x_T):
    with ExitStack() as ctx:
        sb = lambda n, s, d=F32: ctx.enter_context(nc.sbuf_tensor(f"{name}_{n}", s, d))
        sem = lambda n: ctx.enter_context(nc.semaphore(f"{name}_{n}"))
        hs = [sb(f"hs{b}", [P, P]) for b in range(2)]
        square = [sb(f"square{i}", [P, NPAIR, P]) for i in range(2)]
        log = [sb(f"log{i}", [P, NPAIR, P]) for i in range(2)]
        clipped = [sb(f"clipped{i}", [P, NPAIR, P]) for i in range(2)]
        inv = [sb(f"inv{i}", [P, NPAIR, P]) for i in range(2)]
        straight = [sb(f"straight{i}", [P, NPAIR, P]) for i in range(2)]
        swapped = [sb(f"swapped{i}", [P, NPAIR, P]) for i in range(2)]
        turned = [sb(f"turned{i}", [P, NPAIR, P]) for i in range(2)]
        q = sb("q", [P, NPAIR, P])
        k = [sb(f"k{b}", [P, NPAIR, KEYS]) for b in range(2)]
        v = [sb(f"v{b}", [P, INNER]) for b in range(2)]
        neg_max = sb("neg_max", [P, LH])
        bias = sb("bias", [P, LH])
        den = sb("den", [P, LH])
        inv_den = sb("inv_den", [P, LH])
        probs = sb("probs", [P, LH, KEYS])
        shares = sb("shares", [P, LH, KEYS])
        own_T = sb("own_T", [P, LH, P])
        past_T = sb("past_T", [P, LH, P])
        o_T = sb("o_T", [P, NPAIR, P])
        unshift = sb("unshift", [P, 1])
        zeros = sb("zeros", [P, NPAIR, WINDOW])
        front = [bank(psum, n) for n in range(4)]
        back = [bank(psum, 4 + n) for n in range(4)]

        hs_in = sem("hs_in")
        k_past = sem("k_past")
        raw_full = sem("raw_full")
        square_done = sem("square_done")
        sum_full = sem("sum_full")
        clip_done = sem("clip_done")
        log_done = sem("log_done")
        inv_done = sem("inv_done")
        table_done = sem("table_done")
        turned_done = sem("turned_done")
        qk_done = sem("qk_done")
        v_full = sem("v_full")
        v_done = sem("v_done")
        score_full = sem("score_full")
        max_done = sem("max_done")
        bias_done = sem("bias_done")
        exp_done = sem("exp_done")
        inv_den_done = sem("inv_den_done")
        share_done = sem("share_done")
        flip_full = sem("flip_full")
        own_done = sem("own_done")
        past_done = sem("past_done")
        o_full = sem("o_full")
        o_done = sem("o_done")
        out_full = sem("out_full")
        out_done = sem("out_done")
        setup = sem("setup")
        SCALE = 8.0
        MIN_NORM = 1e-12
        LOG_SHIFT = 16
        block = ctx.enter_context(nc.Block())

        def tiles(engine, body):
            body(0, 0, True)
            with engine.Fori(0, NT // 2 - 1) as i:
                body(i * 2 + 1, 1, False)
                body(i * 2 + 2, 0, False)
            body(NT - 1, 1, False)

        @block.gpsimd
        def _(pool):
            def body(t, b, first):
                if not first:
                    pool.wait_ge(v_full, t)
                pool.wait_ge(setup, 1)
                nc.gpsimd.tensor_copy(hs[b][:, :], hs_T[:, bass.ds(t * P, P)]).then_inc(hs_in, 1)
                if not first:
                    pool.wait_ge(score_full, t)
                    nc.gpsimd.tensor_tensor(k[b][:, :, 0:WINDOW], k[1 - b][:, :, P:KEYS], zeros[:, :, :], ALU.add).then_inc(k_past, 1)
                for i in range(2):
                    pool.wait_ge(table_done, t * 4 + 2 * i + 2)
                    nc.gpsimd.tensor_tensor(turned[i][:, :, :], straight[i][:, :, :], swapped[i][:, :, :], ALU.add).then_inc(turned_done, 1)
                    pool.wait_ge(inv_done, t * 2 + i + 1)
                    pool.wait_ge(turned_done, t * 2 + i + 1)
                    to = q[:, :, :] if i == 0 else k[b][:, :, WINDOW:KEYS]
                    nc.gpsimd.tensor_tensor(to, turned[i][:, :, :], inv[i][:, :, :], ALU.mult).then_inc(qk_done, 1)

            tiles(pool, body)

        @block.tensor
        def _(pe):
            def body(t, b, first):
                pe.wait_ge(hs_in, t + 1)
                for n in range(4):
                    if n == 0 and not first:
                        pe.wait_ge(max_done, t * 4)
                        pe.wait_ge(exp_done, t)
                    for m in range(NPAIR):
                        last = nc.tensor.matmul(front[n][:, m * P:(m + 1) * P], w_in[:, n, m, :], hs[b][:, :], start=True, stop=True)
                    if n % 2 == 1:
                        last.then_inc(raw_full, 1)
                if not first:
                    pe.wait_ge(o_done, t)
                    pe.wait_ge(out_done, t)
                nc.tensor.matmul(back[2][:, :], hs[b][:, :], w_v, start=True, stop=True).then_inc(v_full, 1)
                for i in range(2):
                    pe.wait_ge(square_done, t * 2 + i + 1)
                    for half in range(2):
                        r = slice(half * LD, (half + 1) * LD)
                        last = nc.tensor.matmul(back[i][r, :], sum_of[:, half, :], square[i][:, :, :], start=True, stop=True)
                    last.then_inc(sum_full, 1)
                pe.wait_ge(table_done, t * 4 + 4)
                pe.wait_ge(qk_done, t * 2 + 2)
                if not first:
                    pe.wait_ge(k_past, t)
                for m in range(NPAIR):
                    for half in range(2):
                        r = slice(half * LD, (half + 1) * LD)
                        to = front[2 * half + m // 2][:, m % 2 * KEYS:(m % 2 + 1) * KEYS]
                        nc.tensor.matmul(to, q[r, m, :], k[b][r, m, :], start=m % 2 == 0, stop=False, skip_group_check=True)
                for n in range(4):
                    last = nc.tensor.matmul(front[n][:, 0:2 * KEYS], ident_bf, bands[0 if first else 1], start=False, stop=True, skip_group_check=True)
                last.then_inc(score_full, 1)
                pe.wait_ge(share_done, t + 1)
                for g in range(2):
                    if g == 0:
                        pe.wait_ge(clip_done, t * 2 + 2)
                    else:
                        pe.wait_ge(own_done, t * 2 + 1)
                        pe.wait_ge(past_done, t * 2 + 1)
                    for n in range(4):
                        h = 4 * g + n
                        nc.tensor.transpose(back[0][:, n * P:(n + 1) * P], shares[:, h, WINDOW:KEYS], ident)
                        last = nc.tensor.transpose(back[1][0:WINDOW, n * P:(n + 1) * P], shares[:, h, 0:WINDOW], ident)
                    last.then_inc(flip_full, 1)
                pe.wait_ge(own_done, t * 2 + 2)
                pe.wait_ge(past_done, t * 2 + 2)
                pe.wait_ge(v_done, t + 1)
                for m in range(NPAIR):
                    for past in range(2):
                        for half in range(2):
                            h = 2 * m + half
                            to = back[3][half * LD:(half + 1) * LD, m * P:(m + 1) * P]
                            col = slice(h * LD, (h + 1) * LD)
                            if past:
                                last = nc.tensor.matmul(to, v[1 - b][WINDOW:P, col], past_T[WINDOW:P, h, :], start=False, stop=True, skip_group_check=True)
                            else:
                                last = nc.tensor.matmul(to, v[b][:, col], own_T[:, h, :], start=m == 0, stop=False, skip_group_check=True)
                last.then_inc(o_full, 1)
                pe.wait_ge(o_done, t + 1)
                for m in range(NPAIR):
                    last = nc.tensor.matmul(back[2][:, 0:P], w_out[:, m, :], o_T[:, m, :], start=m == 0, stop=m == NPAIR - 1)
                last.then_inc(out_full, 1)

            pe.wait_ge(setup, 1)
            tiles(pe, body)

        @block.scalar
        def _(act):
            def body(t, b, first):
                for i in range(2):
                    act.wait_ge(raw_full, t * 2 + i + 1)
                    nc.scalar.activation(square[i][:, :, :], front[2 * i][:, :].rearrange("p (m i) -> p m i", m=NPAIR), ACT.Square).then_inc(square_done, 1)
                act.wait_ge(v_full, t + 1)
                nc.scalar.activation(v[b][:, :], back[2][:, :], ACT.Copy).then_inc(v_done, 1)
                for i in range(2):
                    act.wait_ge(clip_done, t * 2 + i + 1)
                    nc.scalar.activation(log[i][:, :, :], clipped[i][:, :, :], ACT.Ln, scale=2.0 ** LOG_SHIFT).then_inc(log_done, 1)
                    act.wait_ge(log_done, t * 2 + i + 1)
                    nc.scalar.activation(inv[i][:, :, :], log[i][:, :, :], ACT.Exp, scale=-0.5, bias=unshift[:, :]).then_inc(inv_done, 1)
                act.wait_ge(bias_done, t + 1)
                for h in range(LH):
                    m, half = divmod(h, 2)
                    src = front[2 * half + m // 2][:, m % 2 * KEYS:(m % 2 + 1) * KEYS]
                    last = nc.scalar.activation(probs[:, h, :], src, ACT.Exp, scale=SCALE, bias=bias[:, h:h + 1], accum_out=den[:, h:h + 1])
                last.then_inc(exp_done, 1)
                for g in range(2):
                    act.wait_ge(flip_full, t * 2 + g + 1)
                    nc.scalar.activation(own_T[:, 4 * g:4 * g + 4, :], back[0][:, :].rearrange("p (h i) -> p h i", h=4), ACT.Copy).then_inc(own_done, 1)
                act.wait_ge(o_full, t + 1)
                nc.scalar.activation(o_T[:, :, :], back[3][:, :].rearrange("p (m i) -> p m i", m=NPAIR), ACT.Copy).then_inc(o_done, 1)

            act.wait_ge(setup, 1)
            tiles(act, body)

        @block.vector
        def _(dve):
            def body(t, b, first):
                for i in range(2):
                    dve.wait_ge(raw_full, t * 2 + i + 1)
                    if not first:
                        dve.wait_ge(turned_done, t * 2)
                    for n, to in ((1, swapped[i]), (0, straight[i])):
                        if n == 0:
                            dve.wait_ge(square_done, t * 2 + i + 1)
                        table = tables[:, 2 * i + n, bass.ds(t * P, P)].unsqueeze(1).to_broadcast([P, NPAIR, P])
                        nc.vector.scalar_tensor_tensor(to[:, :, :], front[2 * i + n][:, :].rearrange("p (m i) -> p m i", m=NPAIR),
                                                       scales[2 * i + n], table, ALU.mult, ALU.mult).then_inc(table_done, 1)
                for i in range(2):
                    dve.wait_ge(sum_full, t * 2 + i + 1)
                    nc.vector.tensor_scalar(clipped[i][:, :, :], back[i][:, :].rearrange("p (m i) -> p m i", m=NPAIR), MIN_NORM ** 2, None, ALU.max).then_inc(clip_done, 1)
                dve.wait_ge(score_full, t + 1)
                for n in range(4):
                    half, m2 = divmod(n, 2)
                    heads = slice(4 * m2 + half, 4 * m2 + half + 3, 2)
                    nc.vector.tensor_reduce(neg_max[:, heads], front[n][:, 0:2 * KEYS].rearrange("p (h k) -> p h k", h=2), AX.X, ALU.max, negate=True).then_inc(max_done, 1)
                dve.wait_ge(max_done, t * 4 + 4)
                nc.vector.tensor_scalar(bias[:, :], neg_max[:, :], SCALE, None, ALU.mult).then_inc(bias_done, 1)
                dve.wait_ge(exp_done, t + 1)
                nc.vector.reciprocal(inv_den[:, :], den[:, :]).then_inc(inv_den_done, 1)
                dve.wait_ge(inv_den_done, t + 1)
                nc.vector.tensor_tensor(shares[:, :, :], probs[:, :, :], inv_den[:, :].unsqueeze(2).to_broadcast([P, LH, KEYS]), ALU.mult).then_inc(share_done, 1)
                for g in range(2):
                    dve.wait_ge(flip_full, t * 2 + g + 1)
                    nc.vector.tensor_copy(past_T[WINDOW:P, 4 * g:4 * g + 4, :], back[1][0:WINDOW, :].rearrange("p (h i) -> p h i", h=4)).then_inc(past_done, 1)
                dve.wait_ge(out_full, t + 1)
                at = bass.ds(t * P, P)
                nc.vector.tensor_tensor(x_T[:, at], x_T[:, at], back[2][:, 0:P], ALU.add).then_inc(out_done, 1)

            nc.vector.memset(unshift[:, :], 0.5 * LOG_SHIFT * 0.6931471805599453)
            nc.vector.memset(k[0][:, :, 0:WINDOW], 0.0)
            nc.vector.memset(zeros[:, :, :], 0.0)
            nc.vector.memset(v[1][:, :], 0.0).then_inc(setup, 1)
            tiles(dve, body)


def feed_forward(nc, psum, name, u_T, w1, b1, w2, b2, x_T):
    parts = [min(P, HID - n * P) for n in range(-(-HID // P))]
    NP = len(parts)
    with ExitStack() as ctx:
        a_ps, g_ps, out_ps = ([bank(psum, 2 * n + b) for b in range(2)] for n in range(3))
        gelu = [ctx.enter_context(nc.sbuf_tensor(f"{name}_gelu{b}", [P, BANK], F32)) for b in range(2)]
        mixed = [ctx.enter_context(nc.sbuf_tensor(f"{name}_mixed{b}", [P, BANK], F32)) for b in range(2)]
        sem = lambda n: ctx.enter_context(nc.semaphore(f"{name}_{n}"))
        up_full = sem("up_full")
        gelu_done = sem("gelu_done")
        mixed_done = sem("mixed_done")
        down_done = sem("down_done")
        out_done = sem("out_done")
        work = [(c, n) for c in range(NC) for n in range(NP)]
        block = ctx.enter_context(nc.Block())

        @block.tensor
        def _(pe):
            def down(i):
                c, n = work[i]
                pe.wait_ge(mixed_done, i + 1)
                if n == 0 and c >= 2:
                    pe.wait_ge(out_done, c - 1)
                nc.tensor.matmul(out_ps[c % 2][:, :], w2[0:parts[n], n, :], mixed[i % 2][0:parts[n], :], start=n == 0,
                                 stop=n == NP - 1).then_inc(down_done, 1)

            for i, (c, n) in enumerate(work):
                if i >= 2:
                    pe.wait_ge(mixed_done, i - 1)
                for to, at in ((a_ps, 0), (g_ps, HID)):
                    m = nc.tensor.matmul(to[i % 2][0:parts[n], :], w1[:, at + n * P:at + n * P + parts[n]], u_T[:, chunk(c)], start=True, stop=True)
                m.then_inc(up_full, 1)
                if i >= 1:
                    down(i - 1)
            down(len(work) - 1)

        @block.scalar
        def _(act):
            for i, (c, n) in enumerate(work):
                act.wait_ge(up_full, i + 1)
                r = slice(0, parts[n])
                nc.scalar.activation(gelu[i % 2][r, :], g_ps[i % 2][r, :], ACT.Gelu, bias=b1[r, 1, n:n + 1]).then_inc(gelu_done, 1)

        @block.vector
        def _(dve):
            def add(c):
                dve.wait_ge(down_done, (c + 1) * NP)
                nc.vector.scalar_tensor_tensor(x_T[:, chunk(c)], out_ps[c % 2][:, :], b2, x_T[:, chunk(c)], ALU.add, ALU.add).then_inc(out_done, 1)

            for i, (c, n) in enumerate(work):
                dve.wait_ge(gelu_done, i + 1)
                if i >= 2:
                    dve.wait_ge(down_done, i - 1)
                r = slice(0, parts[n])
                nc.vector.scalar_tensor_tensor(mixed[i % 2][r, :], a_ps[i % 2][r, :], b1[r, 0, n:n + 1], gelu[i % 2][r, :], ALU.add, ALU.mult).then_inc(mixed_done, 1)
                if n == 0 and c >= 1:
                    add(c - 1)
            add(NC - 1)


def clear_semaphores(nc, first):
    last = max(nc.released_uncleared_semaphores)
    with nc.Block() as block:
        @block.gpsimd
        def _(pool):
            pool.sem_clear(range(first, last + 1))


def forward(nc, a, out):
    with ExitStack() as ctx:
        sb = lambda n, s, d=F32: ctx.enter_context(nc.sbuf_tensor(n, s, d))
        x_T, h_T, u_T, z_T = (sb(n, [P, S])[:, :] for n in ("x_T", "h_T", "u_T", "z_T"))
        psum = ctx.enter_context(nc.psum_tensor("psum", [P, 8 * BANK], F32))
        v_tok = sb("v_tok", [P, NT, P])
        den = sb("den", [NH, S])[:, :]
        q_dram = nc.dram_tensor("q_pieces", [NPIECE, P, S], BF16, kind="Internal").ap()
        k_dram = nc.dram_tensor("k_pieces", [NPIECE, P, S], BF16, kind="Internal").ap()
        z_dram = nc.dram_tensor("z_heads", [P, S], F32, kind="Internal").ap()
        den_dram = nc.dram_tensor("den_heads", [NH, S], F32, kind="Internal").ap()

        def held(scope, *names):
            return {n: scope.enter_context(nc.sbuf_tensor(f"{n}_sb", list(a[n].shape), a[n].dtype)) for n in names}

        full = lambda t: t[tuple(slice(None) for _ in t.shape)]
        early = held(ctx, "mean_of", "head_rows", "regroup", "masks", "keep_kq", "cols", "wmods", "cs", "w_attn0", "bv0", "w_attn1", "w_attn2")
        mod = sb("mod", [P, 2, 2, 3])
        gated = sb("gated", [P, 2])
        ident = sb("ident_sb", [P, P])[:, :]
        late = held(ctx, "tables", "w_in", "w_v", "w_out", "sum_of", "bands", "w_up", "b_up", "w_down")
        moe = ctx.enter_context(ExitStack())
        late.update(held(moe, "gate_w", "rank", "pick", "w13", "w2"))
        late_in = ctx.enter_context(nc.semaphore("late_in"))

        first_sem = nc.free_semaphores[0]
        load_inputs(nc, psum, a["x"], x_T, (ident, a["ident"]), [(full(b), a[n]) for n, b in early.items()])
        with nc.Block() as block:
            @block.scalar
            def _(act):
                for n, b in late.items():
                    act.dma_start(full(b), a[n]).then_inc(late_in, 16)

        w0, w1, w2 = early["w_attn0"], early["w_attn1"], early["w_attn2"]
        mean_of, head_rows = full(early["mean_of"]), full(early["head_rows"])
        cols = {n: early["cols"][:, i:i + 1] for i, n in enumerate(COLS)}
        ident_bf, mask_qk, mask_kq = (early["masks"][:, i, :] for i in range(3))
        shift_of = lambda l, i: mod[:, l, i, 0:1]
        scale_of = lambda l, i: mod[:, l, i, 1:2]
        gate_of = lambda l, i: mod[:, l, i, 2:3]
        modulation(nc, psum, [(early["cs"][:, l:l + 1], early["wmods"][:, l, :]) for l in range(2)], mod,
                   cols["gamma"], cols["beta"], gated)

        norm(nc, psum, "ln0a", x_T, h_T, mean_of, LN_EPS, scale_of(0, 0), shift_of(0, 0))
        project(nc, psum, "proj0", h_T, w0[:, 0, :], w0[:, 1, :], w0[:, 2, :], q_dram, k_dram, v_tok,
                bias=(cols["bq"], cols["bk"], early["bv0"]))
        attention(nc, psum, "att0", False, S ** -0.5, q_dram, k_dram, v_tok, z_dram, den_dram, z_T, den,
                  ident_bf, mask_qk, mask_kq, early["keep_kq"][:, :])
        divide_by_sums(nc, psum, "com0", z_T, den, head_rows, h_T, regroup=full(early["regroup"]))
        norm(nc, psum, "ln0z", z_T, None, mean_of, LN_EPS, gated[:, 0:1], gated[:, 1:2], add_to=x_T)
        norm(nc, psum, "ln0b", x_T, h_T, mean_of, LN_EPS, scale_of(0, 1), shift_of(0, 1))
        norm(nc, psum, "rms1", h_T, u_T, mean_of, 1e-5, cols["ln1"])
        with ExitStack() as rope:
            angle = rope.enter_context(nc.sbuf_tensor("rope_sb", [P, 2, S], F32))
            rope_in = rope.enter_context(nc.semaphore("rope_in"))
            with nc.Block() as block:
                @block.sync
                def _(sp):
                    sp.dma_start(angle[:, :, :], a["rope"]).then_inc(rope_in, 16)
                    sp.wait_ge(rope_in, 16)
            project(nc, psum, "proj1", u_T, w1[:, 0, :], w1[:, 1, :], w1[:, 2, :], q_dram, k_dram, v_tok,
                    rope=(w1[:, 3, :], w1[:, 4, :], angle[:, 0, :], angle[:, 1, :]))
        attention(nc, psum, "att1", True, HD ** -0.5, q_dram, k_dram, v_tok, z_dram, den_dram, z_T, den, ident_bf, mask_qk, mask_kq)
        divide_by_sums(nc, psum, "com1", z_T, den, head_rows, h_T, w1[:, 5, :], 1.0)
        norm(nc, psum, "rms2", h_T, u_T, mean_of, 1e-5, cols["ln2"])
        with nc.Block() as block:
            @block.sync
            def _(sp):
                sp.wait_ge(late_in, 16 * len(late))
        w_rows = moe.enter_context(nc.sbuf_tensor("w_rows", [P, S], BF16))[:, :]
        router(nc, psum, u_T, full(late["gate_w"]), full(late["rank"]), ident_bf, w_rows)
        experts(nc, psum, u_T, late["w13"], late["w2"], w_rows, late["pick"], h_T, x_T, gate_of(0, 1))
        moe.close()
        clear_semaphores(nc, first_sem)
        norm(nc, psum, "ln1a", x_T, h_T, mean_of, LN_EPS, scale_of(1, 0), shift_of(1, 0))
        project(nc, psum, "proj2", h_T, w2[:, 0, :], w2[:, 1, :], w2[:, 2, :], q_dram, k_dram, v_tok)
        attention(nc, psum, "att2", True, P ** -0.5, q_dram, k_dram, v_tok, z_dram, den_dram, z_T, den, ident_bf, mask_qk, mask_kq)
        divide_by_sums(nc, psum, "com2", z_T, den, head_rows, x_T, w2[:, 3, :], gate_of(1, 0))
        norm(nc, psum, "ln1b", x_T, h_T, mean_of, LN_EPS, scale_of(1, 1), shift_of(1, 1))
        for l in range(2):
            shift_tokens(nc, f"shift{l}a", h_T, u_T)
            local_attention(nc, psum, f"local{l}", u_T, late["w_in"][:, l], late["w_v"][:, l, :], late["w_out"][:, l],
                            late["tables"], [cols[f"scale{l}{n}"] for n in range(4)], late["sum_of"],
                            [late["bands"][:, i] for i in range(2)], ident, ident_bf, h_T)
            shift_tokens(nc, f"shift{l}b", h_T, u_T)
            norm(nc, psum, f"lnf{l}", u_T, z_T, mean_of, LN_EPS, cols[f"lg{l}"], cols[f"lb{l}"])
            feed_forward(nc, psum, f"ff{l}", z_T, late["w_up"][:, l, :], late["b_up"][:, l], late["w_down"][:, l], cols[f"b2{l}"], h_T)
        with ExitStack() as last:
            with nc.Block() as block:
                @block.vector
                def _(dve):
                    nc.vector.scalar_tensor_tensor(x_T, h_T, gate_of(1, 1), x_T, ALU.mult, ALU.add)
        store_output(nc, psum, x_T, out, ident)


COLS = ["gamma", "beta", "bq", "bk", "ln1", "ln2"] + [f"scale{l}{n}" for l in range(2) for n in range(4)] \
    + [f"{n}{l}" for l in range(2) for n in ("lg", "lb", "b2")]


def constants():
    import numpy as np
    f32, bf16 = np.float32, mybir.dt.np(BF16)
    i = np.arange(P)
    c = {"ident": np.eye(P, dtype=f32), "mean_of": np.full((P, P), 1.0 / P, f32)}
    c["head_rows"] = np.repeat(np.eye(NH, dtype=f32), HD, axis=1)
    regroup = np.zeros((P, NH * 32 + 24), f32)
    for p in range(P):
        regroup[p, 24 + p // HD * 32 + p % HD] = 1
    c["regroup"] = regroup
    mask_qk = np.where(i[None, :] > i[:, None], NEG, 0.0)
    c["masks"] = np.stack([np.eye(P), mask_qk, mask_qk.T], axis=1).astype(bf16)
    c["keep_kq"] = (i[:, None] >= i[None, :]).astype(f32)
    c["rank"] = np.broadcast_to(np.arange(NE, 0, -1).astype(f32), (P, NE)).copy()
    pick = np.zeros((P, NE, P), bf16)
    for e in range(NE):
        pick[e:NPIECE * NE:NE, e, :] = 1
    c["pick"] = pick
    c["sum_of"] = np.repeat(np.repeat(np.eye(2, dtype=f32), LD, axis=0)[:, :, None], LD, axis=2)
    j = np.arange(KEYS)[None, :] - WINDOW
    seen = (j <= i[:, None]) & (j >= i[:, None] - WINDOW)
    bands = np.stack([np.where(seen & (j >= 0), 0.0, NEG), np.where(seen, 0.0, NEG)])
    c["bands"] = np.ascontiguousarray(np.stack([bands, bands], axis=1).transpose(2, 0, 1, 3)).astype(bf16)
    t = np.arange(S, dtype=f32)

    def angles(dim):
        inv = (f32(1) / (f32(10000.0) ** (np.arange(0, dim, 2, dtype=f32) / f32(dim)).astype(f32))).astype(f32)
        freq = (t[:, None] * inv[None, :]).astype(f32).astype(np.float64)
        freq = np.concatenate([freq, freq], axis=1).T
        sign = np.where(np.arange(dim) < dim // 2, -1.0, 1.0)[:, None]
        return np.cos(freq).astype(f32), (np.sin(freq) * sign).astype(f32)

    cos, sin = angles(HD)
    c["rope"] = np.ascontiguousarray(np.tile(np.stack([cos, sin], axis=1), (NH, 1, 1)))
    cos, sin = angles(LD)
    half = np.arange(0, LD, 2, dtype=f32)
    base = ((half + f32(0.4 * LD)) / f32(1.4 * LD)).astype(f32)
    power = ((t - S // 2) / f32(WINDOW // 2)).astype(f32)
    scale = (base[None, :].astype(np.float64) ** power[:, None]).astype(f32)
    scale = np.concatenate([scale, scale], axis=1).T
    tables = np.stack([cos * scale, sin * scale, cos / scale, sin / scale], axis=1).astype(f32)
    c["tables"] = np.ascontiguousarray(np.tile(tables, (2, 1, 1)))
    return c


def layout(np, i):
    cont = np.ascontiguousarray
    swap = lambda w, dim: w.reshape(-1, 2, dim // 2, w.shape[-1])[:, ::-1].reshape(w.shape)
    a = {"x": i["L0_attn_embedded"], "cs": cont(np.concatenate([i["L0_c"], i["L1_c"]], axis=0).T)}
    a["wmods"] = cont(np.stack([i["L0_wmod"], i["L1_wmod"]], axis=1))
    a["w_attn0"] = cont(np.stack([i[f"L0_attn_W{n}"].T for n in "qkv"], axis=1))
    a["bv0"] = cont(np.broadcast_to(i["L0_attn_bv"], (P, P)))
    w = i["L0_ffn_wqkv"]
    q, kv = w[:P], w[P:]
    nkv = kv.shape[0] // HD // 2
    k, v = (np.repeat(part.reshape(nkv, HD, P), NH // nkv, axis=0).reshape(P, P) for part in (kv[:nkv * HD], kv[nkv * HD:]))
    a["w_attn1"] = cont(np.stack([q.T, k.T, v.T, swap(q, HD).T, swap(k, HD).T, i["L0_ffn_wo"].T], axis=1))
    by_head = lambda w: w.reshape(P, HD, NH).transpose(0, 2, 1).reshape(P, P)
    a["w_attn2"] = cont(np.stack([by_head(i["L1_attn_qw"]), by_head(i["L1_attn_kw"]), by_head(i["L1_attn_vw"]),
                                  by_head(i["L1_attn_ow"].T).T], axis=1))
    a["gate_w"] = cont(i["L0_ffn_gate_w"].T)
    a["w13"] = cont(i["L0_ffn_w13"].transpose(2, 0, 1))
    a["w2"] = cont(i["L0_ffn_w2"].reshape(NE, P, 2, P).transpose(3, 0, 2, 1))
    w = i["L1_ffn_wqkv"]
    cols = lambda n: w[:, :, n * INNER:(n + 1) * INNER]
    swap_cols = lambda w: w.reshape(2, P, LH, 2, LD // 2)[:, :, :, ::-1].reshape(2, P, INNER)
    four = np.stack([cols(0), swap_cols(cols(0)), cols(1), swap_cols(cols(1))], axis=2)
    a["w_in"] = cont(four.reshape(2, P, 4, NPAIR, P).transpose(1, 0, 2, 3, 4))
    a["w_v"] = cont(cols(2).transpose(1, 0, 2))
    a["w_out"] = cont(i["L1_ffn_wo"].reshape(2, NPAIR, P, P).transpose(2, 0, 1, 3))
    parts = -(-HID // P)
    a["w_up"] = cont(i["L1_ffn_w1"].transpose(1, 0, 2))
    padded = lambda x: np.concatenate([x, np.zeros((*x.shape[:-2], parts * P - HID, x.shape[-1]), x.dtype)], axis=-2)
    a["b_up"] = cont(padded(i["L1_ffn_b1"].reshape(2, 2, HID, 1)).reshape(2, 2, parts, P).transpose(3, 0, 1, 2))
    a["w_down"] = cont(padded(i["L1_ffn_w2"]).reshape(2, parts, P, P).transpose(2, 0, 1, 3))
    one = {"gamma": i["L0_attn_gamma"], "beta": i["L0_attn_beta"], "bq": i["L0_attn_bq"], "bk": i["L0_attn_bk"],
           "ln1": i["L0_ffn_ln1_w"], "ln2": i["L0_ffn_ln2_w"]}
    for l in range(2):
        for n, s in enumerate((i["L1_ffn_q_scale"][l], i["L1_ffn_k_scale"][l])):
            one[f"scale{l}{2 * n}"] = np.tile(s, 2)
            one[f"scale{l}{2 * n + 1}"] = np.tile(s.reshape(2, -1)[::-1].reshape(-1), 2)
        one[f"lg{l}"], one[f"lb{l}"], one[f"b2{l}"] = i["L1_ffn_ln_g"][l], i["L1_ffn_ln_b"][l], i["L1_ffn_b2"][l]
    a["cols"] = cont(np.stack([one[n] for n in COLS], axis=1))
    return a


def kernel(**inputs):
    import numpy as _np
    import concourse.bacc as _bacc
    from concourse import mybir as _mybir
    from concourse.bass_utils import run_bass_kernel_spmd as _run

    nc = _bacc.Bacc("TRN2", target_bir_lowering=False, num_devices=1)
    arrays = {**layout(_np, {n: _np.asarray(x) for n, x in inputs.items()}), **constants()}
    views = {n: nc.dram_tensor(f"in_{n}", x.shape, _mybir.dt.from_np(x.dtype), kind="ExternalInput").ap()
             for n, x in arrays.items()}
    out = nc.dram_tensor("out_0", (1, S, P), F32, kind="ExternalOutput").ap()
    forward(nc, views, out)
    r = _run(nc, [{f"in_{n}": x for n, x in arrays.items()}], core_ids=[0])
    return r.results[0]["out_0"]
```

```python
from contextlib import ExitStack

import concourse.bass as bass
from concourse import mybir

F32 = mybir.dt.float32
BF16 = mybir.dt.bfloat16
ACT = mybir.ActivationFunctionType
ALU = mybir.AluOpType
AX = mybir.AxisListType

P = 128
S = 2048
NT = S // P
BANK = 512
NC = S // BANK
NH = 16
HD = P // NH
NPIECE = 3
KPROD = NPIECE * NPIECE * HD
MROW = 96
NBUF = 3
AHEAD = 2
VW = 32
NE, FF = 8, 256
LH, LD = 8, 64
INNER = LH * LD
NPAIR = LH // 2
WINDOW = 64
KEYS = P + WINDOW
HID = int(P * 4 * 2 / 3)
LN_EPS = 1e-5
NEG = -1e30


def chunk(c):
    return slice(c * BANK, (c + 1) * BANK)


def bank(psum, n, wide=1):
    return psum[:, n * BANK:(n + wide) * BANK]


def load_inputs(nc, psum, x, x_T, ident, loads):
    with ExitStack() as ctx:
        x_tok = ctx.enter_context(nc.sbuf_tensor("x_tok", [P, NT, P], F32))
        turned = [bank(psum, c) for c in range(NC)]
        x_in = ctx.enter_context(nc.semaphore("x_in"))
        loaded = ctx.enter_context(nc.semaphore("loaded"))
        turned_full = ctx.enter_context(nc.semaphore("turned_full"))
        x_done = ctx.enter_context(nc.semaphore("x_done"))
        block = ctx.enter_context(nc.Block())
        here, there = loads[0::2], loads[1::2]

        @block.sync
        def _(sp):
            sp.dma_start(x_tok[:, :, :], x[0].rearrange("(t p) f -> p t f", p=P)).then_inc(x_in, 16)
            sp.dma_start(ident[0], ident[1]).then_inc(x_in, 16)
            for to, source in here:
                sp.dma_start(to, source).then_inc(loaded, 16)
            sp.wait_ge(loaded, 16 * len(loads))

        @block.scalar
        def _(act):
            for to, source in there:
                act.dma_start(to, source).then_inc(loaded, 16)

        @block.tensor
        def _(pe):
            pe.wait_ge(x_in, 32)
            for t in range(NT):
                m = nc.tensor.transpose(turned[t // 4][:, t % 4 * P:(t % 4 + 1) * P], x_tok[:, t, :], ident[0])
                if t % 4 == 3:
                    m.then_inc(turned_full, 1)

        @block.vector
        def _(dve):
            for c in range(NC):
                dve.wait_ge(turned_full, c + 1)
                nc.vector.tensor_copy(x_T[:, chunk(c)], turned[c][:, :]).then_inc(x_done, 1)


def store_output(nc, psum, x_T, out, ident):
    with ExitStack() as ctx:
        x_tok = ctx.enter_context(nc.sbuf_tensor("out_tok", [P, NT, P], F32))
        turned = [bank(psum, c) for c in range(NC)]
        turned_full = ctx.enter_context(nc.semaphore("out_turned_full"))
        tok_done = ctx.enter_context(nc.semaphore("tok_done"))
        stored = ctx.enter_context(nc.semaphore("stored"))
        block = ctx.enter_context(nc.Block())

        @block.tensor
        def _(pe):
            for t in range(NT):
                m = nc.tensor.transpose(turned[t // 4][:, t % 4 * P:(t % 4 + 1) * P], x_T[:, t * P:(t + 1) * P], ident)
                if t % 4 == 3:
                    m.then_inc(turned_full, 1)

        @block.vector
        def _(dve):
            for c in range(NC):
                dve.wait_ge(turned_full, c + 1)
                nc.vector.tensor_copy(x_tok[:, 4 * c:4 * c + 4, :], turned[c][:, :].rearrange("p (t f) -> p t f", f=P)).then_inc(tok_done, 1)

        @block.sync
        def _(sp):
            for c in range(NC):
                sp.wait_ge(tok_done, c + 1)
                sp.dma_start(out[0, c * BANK:(c + 1) * BANK, :].rearrange("(t p) f -> p t f", p=P),
                             x_tok[:, 4 * c:4 * c + 4, :]).then_inc(stored, 16)
            sp.wait_ge(stored, 16 * NC)


def modulation(nc, psum, layers, mod, gamma, beta, gated):
    NL = len(layers)
    with ExitStack() as ctx:
        c_silu = ctx.enter_context(nc.sbuf_tensor("c_silu", [P, NL], F32))
        sign = ctx.enter_context(nc.sbuf_tensor("gate_sign", [P, NL, 2], F32))
        size = ctx.enter_context(nc.sbuf_tensor("gate_size", [P, NL, 2], F32))
        mod_ps = bank(psum, 0)[:, 0:6 * NL].rearrange("p (l i n) -> p l i n", l=NL, i=2)
        silu_done = ctx.enter_context(nc.semaphore("silu_done"))
        mod_full = ctx.enter_context(nc.semaphore("mod_full"))
        mod_step = ctx.enter_context(nc.semaphore("mod_step"))
        block = ctx.enter_context(nc.Block())

        @block.scalar
        def _(act):
            for l, (c, _) in enumerate(layers):
                nc.scalar.activation(c_silu[:, l:l + 1], c, ACT.Silu).then_inc(silu_done, 1)

        @block.tensor
        def _(pe):
            for l, (_, wmod) in enumerate(layers):
                pe.wait_ge(silu_done, l + 1)
                for n in range(6):
                    m = nc.tensor.matmul(mod_ps[:, l, n // 3, n % 3:n % 3 + 1], wmod[:, n * P:(n + 1) * P],
                                         c_silu[:, l:l + 1], start=True, stop=True)
            m.then_inc(mod_full, 1)

        @block.vector
        def _(dve):
            dve.wait_ge(mod_full, 1)
            nc.vector.tensor_copy(mod[:, :, :, 0], mod_ps[:, :, :, 0])
            nc.vector.tensor_scalar(mod[:, :, :, 1], mod_ps[:, :, :, 1], 1.0, None, ALU.add)
            nc.vector.tensor_scalar(sign[:, :, :], mod_ps[:, :, :, 2], 0.0, 2.0, ALU.is_ge, ALU.mult).then_inc(mod_step, 1)
            nc.vector.tensor_scalar(size[:, :, :], mod_ps[:, :, :, 2], -1.0, 0.25, ALU.mult, ALU.max).then_inc(mod_step, 1)
            dve.wait_ge(mod_step, 2)
            nc.vector.tensor_tensor(size[:, :, :], size[:, :, :], mod_ps[:, :, :, 2], ALU.max).then_inc(mod_step, 1)
            dve.wait_ge(mod_step, 3)
            nc.vector.scalar_tensor_tensor(mod[:, :, :, 2], sign[:, :, :], -1.0, size[:, :, :], ALU.add, ALU.mult).then_inc(mod_step, 1)
            dve.wait_ge(mod_step, 4)
            nc.vector.tensor_tensor(gated[:, 0:1], gamma, mod[:, 0, 0, 2:3], ALU.mult)
            nc.vector.tensor_tensor(gated[:, 1:2], beta, mod[:, 0, 0, 2:3], ALU.mult)


def norm(nc, psum, name, src_T, out_T, mean_of, eps, scale, shift=None, add_to=None):
    centred = shift is not None
    with ExitStack() as ctx:
        sb = lambda n: ctx.enter_context(nc.sbuf_tensor(f"{name}_{n}", [P, S], F32))
        square, std, inv = sb("square"), sb("std"), sb("inv")
        centre = sb("centre") if centred else src_T
        eps_col = ctx.enter_context(nc.sbuf_tensor(f"{name}_eps", [P, 1], F32))
        mean = [bank(psum, c) for c in range(NC)]
        var = [bank(psum, NC + c) for c in range(NC)]
        sem = lambda n: ctx.enter_context(nc.semaphore(f"{name}_{n}"))
        eps_set = sem("eps_set")
        mean_full = sem("mean_full")
        centre_done = sem("centre_done")
        square_done = sem("square_done")
        var_full = sem("var_full")
        std_done = sem("std_done")
        inv_done = sem("inv_done")
        out_step = sem("out_step")
        block = ctx.enter_context(nc.Block())

        @block.tensor
        def _(pe):
            if centred:
                for c in range(NC):
                    nc.tensor.matmul(mean[c][:, :], mean_of, src_T[:, chunk(c)], start=True, stop=True).then_inc(mean_full, 1)
            for c in range(NC):
                pe.wait_ge(square_done, c + 1)
                nc.tensor.matmul(var[c][:, :], mean_of, square[:, chunk(c)], start=True, stop=True).then_inc(var_full, 1)

        @block.scalar
        def _(act):
            for c in range(NC):
                if centred:
                    act.wait_ge(centre_done, c + 1)
                nc.scalar.activation(square[:, chunk(c)], centre[:, chunk(c)], ACT.Square).then_inc(square_done, 1)
            act.wait_ge(eps_set, 1)
            for c in range(NC):
                act.wait_ge(var_full, c + 1)
                nc.scalar.activation(std[:, chunk(c)], var[c][:, :], ACT.Sqrt, bias=eps_col[:, :]).then_inc(std_done, 1)

        @block.vector
        def _(dve):
            nc.vector.memset(eps_col[:, :], eps).then_inc(eps_set, 1)
            if centred:
                for c in range(NC):
                    dve.wait_ge(mean_full, c + 1)
                    nc.vector.tensor_tensor(centre[:, chunk(c)], src_T[:, chunk(c)], mean[c][:, :], ALU.subtract).then_inc(centre_done, 1)
                dve.wait_ge(centre_done, NC)
            for c in range(NC):
                dve.wait_ge(std_done, c + 1)
                nc.vector.reciprocal(inv[:, chunk(c)], std[:, chunk(c)]).then_inc(inv_done, 1)
                dve.wait_ge(inv_done, c + 1)
                to = out_T[:, chunk(c)] if add_to is None else inv[:, chunk(c)]
                nc.vector.scalar_tensor_tensor(to, centre[:, chunk(c)], scale, inv[:, chunk(c)], ALU.mult, ALU.mult).then_inc(out_step, 1)
                if centred:
                    dve.wait_ge(out_step, c + 1)
                    if add_to is None:
                        nc.vector.tensor_scalar(to, to, shift, None, ALU.add)
                    else:
                        nc.vector.scalar_tensor_tensor(add_to[:, chunk(c)], to, shift, add_to[:, chunk(c)], ALU.add, ALU.add)


def project(nc, psum, name, h_T, wq, wk, wv, q_dram, k_dram, v_tok, bias=None, rope=None):
    with ExitStack() as ctx:
        raw = [[bank(psum, 2 * b + n) for n in range(2)] for b in range(2)]
        v_ps = [bank(psum, 4 + b) for b in range(2)]
        full = ctx.enter_context(nc.sbuf_tensor(f"{name}_full", [P, 2, BANK], F32))
        rest = ctx.enter_context(nc.sbuf_tensor(f"{name}_rest", [P, 2, BANK], F32))
        turn = ctx.enter_context(nc.sbuf_tensor(f"{name}_turn", [P, 2, BANK], F32))
        piece = ctx.enter_context(nc.sbuf_tensor(f"{name}_piece", [P, 2, NPIECE, BANK], BF16))
        sem = lambda n: ctx.enter_context(nc.semaphore(f"{name}_{n}"))
        raw_full = sem("raw_full")
        raw_free = sem("raw_free")
        full_done = sem("full_done")
        turn_done = sem("turn_done")
        piece1 = sem("piece1")
        rest_done = sem("rest_done")
        piece2 = sem("piece2")
        piece3 = sem("piece3")
        v_full = sem("v_full")
        v_free = sem("v_free")
        stored = [sem(f"stored{b}") for b in range(2)]
        block = ctx.enter_context(nc.Block())
        work = [(c, i) for c in range(NC) for i in range(2)]

        @block.tensor
        def _(pe):
            for n, (c, i) in enumerate(work):
                if n >= 2:
                    pe.wait_ge(raw_free, n - 1)
                m = nc.tensor.matmul(raw[n % 2][0][:, :], (wq, wk)[i], h_T[:, chunk(c)], start=True, stop=True)
                if rope:
                    m = nc.tensor.matmul(raw[n % 2][1][:, :], rope[i], h_T[:, chunk(c)], start=True, stop=True)
                m.then_inc(raw_full, 1)
            for t in range(NT):
                if t % 4 == 0 and t >= 8:
                    pe.wait_ge(v_free, t // 4 - 1)
                m = nc.tensor.matmul(v_ps[t // 4 % 2][:, t % 4 * P:(t % 4 + 1) * P], h_T[:, t * P:(t + 1) * P], wv, start=True, stop=True)
                if t % 4 == 3:
                    m.then_inc(v_full, 1)

        @block.vector
        def _(dve):
            for n, (c, i) in enumerate(work):
                to, ps = full[:, n % 2, :], raw[n % 2]
                dve.wait_ge(raw_full, n + 1)
                if rope:
                    nc.vector.tensor_tensor(to, ps[0][:, :], rope[2][:, chunk(c)], ALU.mult).then_inc(turn_done, 1)
                    nc.vector.tensor_tensor(turn[:, n % 2, :], ps[1][:, :], rope[3][:, chunk(c)], ALU.mult).then_inc(raw_free, 1)
                    dve.wait_ge(turn_done, n + 1)
                    dve.wait_ge(raw_free, n + 1)
                    nc.vector.tensor_tensor(to, to, turn[:, n % 2, :], ALU.add).then_inc(full_done, 1)
                elif bias:
                    nc.vector.tensor_scalar(to, ps[0][:, :], bias[i], None, ALU.add).then_inc(raw_free, 1)
                else:
                    nc.vector.tensor_copy(to, ps[0][:, :]).then_inc(raw_free, 1)
                dve.wait_ge(full_done if rope else raw_free, n + 1)
                dve.wait_ge(piece1, n + 1)
                if n >= 2:
                    dve.wait_ge(piece3, n - 1)
                nc.vector.tensor_tensor(rest[:, n % 2, :], to, piece[:, n % 2, 0, :], ALU.subtract).then_inc(rest_done, 1)
            for c in range(NC):
                dve.wait_ge(v_full, c + 1)
                to, ps = v_tok[:, 4 * c:4 * c + 4, :], v_ps[c % 2][:, :].rearrange("p (t f) -> p t f", f=P)
                if bias:
                    nc.vector.tensor_tensor(to, ps, bias[2][:, :].unsqueeze(1).to_broadcast([P, 4, P]), ALU.add).then_inc(v_free, 1)
                else:
                    nc.vector.tensor_copy(to, ps).then_inc(v_free, 1)

        @block.scalar
        def _(act):
            for n, (c, i) in enumerate(work):
                act.wait_ge(full_done if rope else raw_free, n + 1)
                if n >= 2:
                    act.wait_ge(stored[n % 2], 16 * (n // 2))
                nc.scalar.activation(piece[:, n % 2, 0, :], full[:, n % 2, :], ACT.Copy).then_inc(piece1, 1)
                act.wait_ge(rest_done, n + 1)
                nc.scalar.activation(piece[:, n % 2, 1, :], rest[:, n % 2, :], ACT.Copy).then_inc(piece2, 1)

        @block.gpsimd
        def _(pool):
            for n, (c, i) in enumerate(work):
                pool.wait_ge(piece2, n + 1)
                nc.gpsimd.tensor_tensor(piece[:, n % 2, 2, :], rest[:, n % 2, :], piece[:, n % 2, 1, :], ALU.subtract).then_inc(piece3, 1)

        @block.sync
        def _(sp):
            for n, (c, i) in enumerate(work):
                sp.wait_ge(piece3, n + 1)
                sp.dma_start((q_dram, k_dram)[i][:, :, chunk(c)].rearrange("n p s -> p n s"),
                             piece[:, n % 2, :, :]).then_inc(stored[n % 2], 16)
            for b in range(2):
                sp.wait_ge(stored[b], 16 * NC)


def divide_by_sums(nc, psum, name, z_T, den, head_rows, x_T, wo=None, gate=None, regroup=None):
    with ExitStack() as ctx:
        den_ps = [bank(psum, c) for c in range(NC)]
        out_ps = [bank(psum, NC + c) for c in range(NC)]
        inv = ctx.enter_context(nc.sbuf_tensor(f"{name}_inv", [NH, S], F32))
        sem = lambda n: ctx.enter_context(nc.semaphore(f"{name}_{n}"))
        inv_done = sem("inv_done")
        den_full = sem("den_full")
        z_done = sem("z_done")
        out_full = sem("out_full")
        block = ctx.enter_context(nc.Block())

        @block.tensor
        def _(pe):
            for c in range(NC):
                pe.wait_ge(inv_done, c + 1)
                nc.tensor.matmul(den_ps[c][:, :], head_rows, inv[:, chunk(c)], start=True, stop=True).then_inc(den_full, 1)
            if wo is not None:
                for c in range(NC):
                    pe.wait_ge(z_done, c + 1)
                    nc.tensor.matmul(out_ps[c][:, :], wo, z_T[:, chunk(c)], start=True, stop=True).then_inc(out_full, 1)
            else:
                pe.wait_ge(z_done, NC)
                spread = z_T.rearrange("p (r g) -> p g r", g=NH)
                for h in range(NH):
                    for k in range(4):
                        for quadrant in range(4):
                            at = h * 32 + 24 - HD * k
                            m = nc.tensor.matmul(out_ps[h // 4][32 * quadrant:32 * quadrant + 32, h % 4 * P:(h % 4 + 1) * P],
                                                 regroup[:, at:at + 32], spread[:, 4 * quadrant + k, :],
                                                 start=k == 0, stop=k == 3, skip_group_check=True)
                    if h % 4 == 3:
                        m.then_inc(out_full, 1)

        @block.vector
        def _(dve):
            for c in range(NC):
                nc.vector.reciprocal(inv[:, chunk(c)], den[:, chunk(c)]).then_inc(inv_done, 1)
            for c in range(NC):
                dve.wait_ge(den_full, c + 1)
                nc.vector.tensor_tensor(z_T[:, chunk(c)], z_T[:, chunk(c)], den_ps[c][:, :], ALU.mult).then_inc(z_done, 1)
            for c in range(NC):
                dve.wait_ge(out_full, c + 1 if wo is not None else NC)
                if wo is not None:
                    nc.vector.scalar_tensor_tensor(x_T[:, chunk(c)], out_ps[c][:, :], gate, x_T[:, chunk(c)], ALU.mult, ALU.add)
                else:
                    nc.vector.tensor_tensor(z_T[:, chunk(c)], x_T[:, chunk(c)], out_ps[c][:, :], ALU.add)


def attention(nc, psum, name, causal, scale, q_dram, k_dram, v_tok, z_dram, den_dram, z_T, den, ident_bf, mask_qk, mask_kq, keep_kq=None):
    with ExitStack() as ctx:
        sb = lambda n, s, d=F32: ctx.enter_context(nc.sbuf_tensor(f"{name}_{n}", s, d))
        sem = lambda n: ctx.enter_context(nc.semaphore(f"{name}_{n}"))
        q_stack = [sb(f"q_stack{b}", [P, S], BF16) for b in range(NBUF)]
        k_stack = [sb(f"k_stack{b}", [P, S], BF16) for b in range(NBUF)]
        probs = [sb(f"probs{b}", [P, S]) for b in range(2)]
        diag = sb("diag", [P, P])
        v_one = sb("v_one", [P, NT, VW])
        v_only = sb("v_only", [P, NT, VW])
        one_only = sb("one_only", [P, VW])
        part_max = sb("part_max", [P, NT, 4])
        neg_max = sb("neg_max", [P, NT])
        rest1 = sb("rest1", [P, NT])
        rest2 = sb("rest2", [P, NT])
        max_rows = sb("max_rows", [P, NT, 32], BF16)
        zero = sb("zero", [P, 4])
        z_sb = sb("z_sb", [P, BANK])
        st = [bank(psum, 2 * b, 2) for b in range(2)]
        mx = [bank(psum, 4 + b) for b in range(3)]
        z_ps = bank(psum, 7)

        stack_in = [sem(f"stack_in{b}") for b in range(NBUF)]
        buffers_set = sem("buffers_set")
        v_in = sem("v_in")
        mx_full = sem("mx_full")
        mx_free = sem("mx_free")
        max_ready = sem("max_ready")
        max_split = sem("max_split")
        pool_step = sem("pool_step")
        st_full = sem("st_full")
        st_free = sem("st_free")
        pv_done = sem("pv_done")
        diag_done = sem("diag_done")
        z_free = sem("z_free")
        z_in = sem("z_in")
        z_out = sem("z_out")

        order = [NT - 1 - u if causal else u for u in range(NT)]
        mx_tiles = [(qt // 4 + 1) if causal else 4 for qt in order]
        mx_before = [sum(mx_tiles[:u]) for u in range(NT)]
        MX = sum(mx_tiles)
        group = [order[4 * j] // 4 for j in range(4)]
        halves = [[hf for hf in range(2) if not causal or kb * P < (hf + 1) * 1024] for kb in range(NT)]

        def ring_of(with_next):
            ring = []
            for kb in range(NT):
                ring += [("exp", kb, hf) for hf in halves[kb]]
                if with_next and (kb + AHEAD) % 4 == 0:
                    ring.append(("max", (kb + AHEAD) // 4 - 1, 0))
            return ring

        rings = {w: ring_of(w) for w in (True, False)}
        places = {w: {r: n for n, r in enumerate(rings[w])} for w in rings}
        E = len(rings[True])
        assert E % 2 == 0 and AHEAD in (1, 2, 3)
        STACK = 16 * (NPIECE * NPIECE + NPIECE)
        ZOUT = 16 * 8
        G = 4

        def width(qt, c):
            end = (qt + 1) * P if causal else S
            return min(BANK, end - c * BANK)

        block = ctx.enter_context(nc.Block())

        @block.sync
        def _(sp):
            def load(h, b):
                for stack, dram in ((q_stack[b], q_dram), (k_stack[b], k_dram)):
                    rows = dram[:, bass.ds(h * HD, HD), :]
                    if stack is q_stack[b]:
                        for i in range(NPIECE):
                            for j in range(NPIECE):
                                r = (i * NPIECE + j) * HD
                                sp.dma_start(stack[r:r + HD, :], rows[i]).then_inc(stack_in[b], 16)
                    else:
                        for i in range(NPIECE):
                            r = i * NPIECE * HD
                            sp.dma_start(stack[r:r + NPIECE * HD, :], rows).then_inc(stack_in[b], 16)

            def body(h, b, load_more):
                sp.wait_ge(pv_done, (h + 1) * NT)
                if load_more:
                    load(h + NBUF, b)
                sp.wait_ge(z_free, h + 1)
                tiles = lambda rows: rows.rearrange("r (c j i) -> r c j i", j=4, i=P)
                for j in range(4):
                    part = lambda r0, r1: z_sb[32 * j + r0:32 * j + r1, :].rearrange("r (c i) -> r c i", i=P)
                    sp.dma_start(tiles(z_dram[bass.ds(h * HD, HD), :])[:, :, j, :], part(0, HD)).then_inc(z_out, 16)
                    sp.dma_start(tiles(den_dram[bass.ds(h, 1), :])[:, :, j, :], part(HD, HD + 1)).then_inc(z_out, 16)

            sp.wait_ge(buffers_set, 2)
            for b in range(NBUF):
                load(b, b)
            with sp.Fori(0, (NH - 1) // NBUF - 1) as i:
                for r in range(NBUF):
                    body(i * NBUF + r, r, True)
            body(NH - 4, 0, True)
            for h in range(NH - 3, NH):
                body(h, h % NBUF, False)
            sp.wait_ge(z_out, ZOUT * NH)
            sp.dma_start(z_T, z_dram).then_inc(z_in, 16)
            sp.dma_start(den, den_dram).then_inc(z_in, 16)
            sp.wait_ge(z_in, 32)


        @block.gpsimd
        def _(pool):
            def values(h):
                src = v_tok[:, :, bass.ds(h * HD, HD)]
                nc.gpsimd.tensor_copy(v_one[:, :, 0:HD], src)
                nc.gpsimd.tensor_copy(v_only[:, :, 0:HD], src).then_inc(v_in, 1)

            pool.wait_ge(buffers_set, 2)

            def split(h, j):
                n = slice(4 * group[j], 4 * group[j] + 4)
                base = (h * 4 + j) * 4
                pool.wait_ge(max_ready, h * 4 + j + 1)
                nc.gpsimd.tensor_tensor(max_rows[:, n, 0], neg_max[:, n], zero[:, 0:4], ALU.add).then_inc(pool_step, 1)
                pool.wait_ge(pool_step, base + 1)
                nc.gpsimd.tensor_tensor(rest1[:, n], neg_max[:, n], max_rows[:, n, 0], ALU.subtract).then_inc(pool_step, 1)
                pool.wait_ge(pool_step, base + 2)
                nc.gpsimd.tensor_tensor(max_rows[:, n, 1], rest1[:, n], zero[:, 0:4], ALU.add).then_inc(pool_step, 1)
                pool.wait_ge(pool_step, base + 3)
                nc.gpsimd.tensor_tensor(rest2[:, n], rest1[:, n], max_rows[:, n, 1], ALU.subtract).then_inc(pool_step, 1)
                pool.wait_ge(pool_step, base + 4)
                nc.gpsimd.tensor_tensor(max_rows[:, n, 2], rest2[:, n], zero[:, 0:4], ALU.add).then_inc(max_split, 1)

            def body(h, with_next):
                for kb in range(NT):
                    if not causal:
                        pool.wait_ge(st_free, G + h * E + places[with_next][("exp", kb, kb // 8)] + 1)
                        if kb > 0:
                            pool.wait_ge(pv_done, h * NT + kb)
                        nc.gpsimd.tensor_tensor(diag[:, :], probs[kb % 2][:, kb * P:kb * P + P], keep_kq,
                                                ALU.mult).then_inc(diag_done, 1)
                    if with_next and kb + AHEAD < NT and (kb + AHEAD) % 4 == 3:
                        split(h + 1, (kb + AHEAD) // 4)
                if with_next:
                    pool.wait_ge(pv_done, h * NT + NT)
                    pool.wait_ge(buffers_set, 2)
                    values(h + 1)

            values(0)
            for j in range(4):
                split(0, j)
            with pool.Fori(0, NH - 1) as h:
                body(h, True)
            body(NH - 1, False)

        @block.vector
        def _(dve):
            for b in range(NBUF):
                nc.vector.memset(q_stack[b][64:128, :], 0.0)
                nc.vector.memset(k_stack[b][64:128, :], 0.0)
            nc.vector.memset(max_rows[:, :, :], 0.0)
            nc.vector.memset(v_one[:, :, :], 0.0)
            nc.vector.memset(v_only[:, :, :], 0.0)
            nc.vector.memset(zero[:, :], 0.0)
            nc.vector.memset(one_only[:, :], 0.0).then_inc(buffers_set, 1)
            dve.wait_ge(buffers_set, 1)
            for b in range(NBUF):
                nc.vector.memset(k_stack[b][MROW:MROW + NPIECE, :], 1.0)
            nc.vector.memset(v_one[:, :, HD:HD + 1], 1.0)
            nc.vector.memset(one_only[:, HD:HD + 1], 1.0).then_inc(buffers_set, 1)

            def maxima(h, r):
                for u, qt in enumerate(order):
                    for c in range(mx_tiles[u]):
                        n = mx_before[u] + c
                        dve.wait_ge(mx_full, h * MX + n + 1)
                        nc.vector.tensor_reduce(part_max[:, qt, c:c + 1], mx[(r * MX + n) % 3][:, 0:width(qt, c)],
                                                AX.X, ALU.max).then_inc(mx_free, 1)
                    if u % 4 == 3:
                        g = qt // 4
                        dve.wait_ge(mx_free, h * MX + n + 1)
                        nc.vector.tensor_reduce(neg_max[:, 4 * g:4 * g + 4], part_max[:, 4 * g:4 * g + 4, 0:mx_tiles[u]],
                                                AX.X, ALU.max, negate=True).then_inc(max_ready, 1)

            maxima(0, 0)
            with dve.Fori(0, (NH - 1) // NBUF) as i:
                for r in range(NBUF):
                    maxima(i * NBUF + 1 + r, 1 + r)

        @block.scalar
        def _(act):
            def body(h, b, with_next):
                for e, (kind, kb, hf) in enumerate(rings[with_next]):
                    n = G + h * E + e
                    slot = (G + e) % 2
                    if kind == "exp":
                        lo = max(kb * P, hf * 1024) if causal else hf * 1024
                        hi = (hf + 1) * 1024
                        act.wait_ge(st_full, n + 1)
                        if hf == halves[kb][0] and not (kb < 2 and isinstance(h, int) and h == 0):
                            act.wait_ge(pv_done, h * NT + kb - 1)
                        nc.scalar.activation(probs[kb % 2][:, lo:hi], st[slot][:, lo - hf * 1024:1024], ACT.Exp,
                                             scale=scale).then_inc(st_free, 1)
                    else:
                        act.wait_ge(st_full, n + 1)
                        g = group[kb]
                        nc.scalar.activation(q_stack[(b + 1) % NBUF][MROW:P, 4 * g * P:4 * (g + 1) * P],
                                             st[slot][MROW:P, 0:BANK // 2].bitcast(BF16), ACT.Copy).then_inc(st_free, 1)
                act.wait_ge(pv_done, (h + 1) * NT)
                if not (isinstance(h, int) and h == 0):
                    act.wait_ge(z_out, h * ZOUT)
                nc.scalar.activation(z_sb[:, :], z_ps[:, :], ACT.Copy).then_inc(z_free, 1)

            for j in range(4):
                g = group[j]
                act.wait_ge(st_full, j + 1)
                nc.scalar.activation(q_stack[0][MROW:P, 4 * g * P:4 * (g + 1) * P],
                                     st[j % 2][MROW:P, 0:BANK // 2].bitcast(BF16), ACT.Copy).then_inc(st_free, 1)
            body(0, 0, True)
            with act.Fori(0, NH // NBUF - 1) as i:
                for r in range(NBUF):
                    body(i * NBUF + 1 + r, (1 + r) % NBUF, True)
            for h in range(NH - 3, NH):
                body(h, h % NBUF, h < NH - 1)

        @block.tensor
        def _(pe):
            def max_tiles(h, r, u, some):
                qt, b = order[u], r % NBUF
                for c in some:
                    if c >= mx_tiles[u]:
                        continue
                    n, w = mx_before[u] + c, width(qt, c)
                    diagonal = causal and c == qt // 4
                    if not (isinstance(h, int) and h * MX + n < 3):
                        pe.wait_ge(mx_free, h * MX + n - 2)
                    tile = mx[(r * MX + n) % 3]
                    m = nc.tensor.matmul(tile[:, 0:w], q_stack[b][0:KPROD, qt * P:(qt + 1) * P],
                                         k_stack[b][0:KPROD, c * BANK:c * BANK + w], start=True, stop=not diagonal,
                                         skip_group_check=True)
                    if diagonal:
                        m = nc.tensor.matmul(tile[:, w - P:w], ident_bf, mask_qk, start=False, stop=True,
                                             skip_group_check=True)
                    m.then_inc(mx_full, 1)

            def max_transpose(h, j, n, slot):
                pe.wait_ge(max_split, h * 4 + j + 1)
                if not (isinstance(n, int) and n < 2):
                    pe.wait_ge(st_free, n - 1)
                out = st[slot][MROW:P, 0:BANK // 2].bitcast(BF16)
                for t in range(4):
                    m = nc.tensor.transpose(out[:, t * P:(t + 1) * P], max_rows[:, 4 * group[j] + t, :], ident_bf)
                m.then_inc(st_full, 1)

            def scores(h, b, kb, hf, with_next):
                e = places[with_next][("exp", kb, hf)]
                n = G + h * E + e
                slot = (G + e) % 2
                pe.wait_ge(st_free, n - 1)
                lo = max(kb * P, hf * 1024) if causal else hf * 1024
                for c in range(2):
                    a, z = max(lo, hf * 1024 + c * BANK), hf * 1024 + (c + 1) * BANK
                    if a >= z:
                        continue
                    diagonal = causal and a == kb * P
                    m = nc.tensor.matmul(st[slot][:, a - hf * 1024:z - hf * 1024], k_stack[b][:, kb * P:(kb + 1) * P],
                                         q_stack[b][:, a:z], start=True, stop=not diagonal, skip_group_check=True)
                    if diagonal:
                        m = nc.tensor.matmul(st[slot][:, a - hf * 1024:a - hf * 1024 + P], ident_bf, mask_kq,
                                             start=False, stop=True, skip_group_check=True)
                m.then_inc(st_full, 1)

            def products(h, kb, with_next):
                pe.wait_ge(st_free, G + h * E + places[with_next][("exp", kb, halves[kb][-1])] + 1)
                if kb == 0:
                    pe.wait_ge(v_in, h + 1)
                    if not (isinstance(h, int) and h == 0):
                        pe.wait_ge(z_free, h)
                pr = probs[kb % 2][:, :].rearrange("p (c j i) -> p c j i", j=4, i=P)
                done = []

                def part(j, c0, c1, weights, start):
                    if c0 < c1:
                        done.append(nc.tensor.matmul(z_ps[32 * j:32 * j + VW, c0 * P:c1 * P], weights,
                                                     pr[:, c0:c1, j, :], start=start, stop=kb == NT - 1,
                                                     skip_group_check=True))

                mid = [max(0, -(-(kb - j) // 4)) for j in range(4)]
                for j in range(4):
                    part(j, mid[j], 4, v_one[:, kb, :] if causal else one_only[:, :], kb == 0)
                if not causal:
                    for j in range(4):
                        part(j, 0, mid[j], v_one[:, kb, :], False)
                    pe.wait_ge(diag_done, h * NT + kb + 1)
                    j, c = kb % 4, kb // 4
                    done.append(nc.tensor.matmul(z_ps[32 * j:32 * j + VW, c * P:(c + 1) * P], v_only[:, kb, :],
                                                 diag[:, :], start=False, stop=kb == NT - 1, skip_group_check=True))
                done[-1].then_inc(pv_done, 1)

            def body(h, r, loads, next1=True, next2=True):
                b = r % NBUF
                for kb in range(NT):
                    ahead, u = divmod(kb + AHEAD, NT)
                    go = next2 if ahead else next1
                    if ahead and u == 0 and next2:
                        pe.wait_ge(stack_in[(r + 2) % NBUF], loads * STACK)
                    first, *second = halves[kb]
                    scores(h, b, kb, first, next1)
                    if go:
                        max_tiles(h + 1 + ahead, r + 1 + ahead, u, (0, 1))
                    if kb > 0:
                        products(h, kb - 1, next1)
                    if second:
                        scores(h, b, kb, second[0], next1)
                    if go:
                        max_tiles(h + 1 + ahead, r + 1 + ahead, u, (2, 3))
                    if next1 and (kb + AHEAD) % 4 == 0:
                        j = (kb + AHEAD) // 4 - 1
                        e = places[True][("max", j, 0)]
                        max_transpose(h + 1, j, G + h * E + e, (G + e) % 2)
                products(h, NT - 1, next1)

            pe.wait_ge(buffers_set, 2)
            pe.wait_ge(stack_in[0], STACK)
            for u in range(NT):
                max_tiles(0, 0, u, range(4))
                if u % 4 == 3:
                    max_transpose(0, u // 4, u // 4, u // 4 % 2)
            pe.wait_ge(stack_in[1], STACK)
            for u in range(AHEAD):
                max_tiles(1, 1, u, range(4))
            pe.wait_ge(st_free, G)
            body(0, 0, 1)
            with pe.Fori(0, NH // NBUF - 1) as i:
                for r in range(NBUF):
                    body(i * NBUF + 1 + r, 1 + r, i + 2)
            for h in range(NH - 3, NH):
                body(h, h % NBUF, (h + 2) // NBUF + 1, h + 1 < NH, h + 2 < NH)

def router(nc, psum, h_T, gate_w, rank, ident, w_rows):
    with ExitStack() as ctx:
        sb = lambda n, d=F32: ctx.enter_context(nc.sbuf_tensor(f"route_{n}", [P, NT, NE], d))
        logits, is_top, order, taken, left = sb("logits"), sb("is_top"), sb("order"), [sb("first"), sb("second")], sb("left")
        share = sb("share")
        col = lambda n: ctx.enter_context(nc.sbuf_tensor(f"route_{n}", [P, NT], F32))
        top, best, gap, odds, total, w1, w2 = [col("top1"), col("top2")], col("best"), col("gap"), col("odds"), col("total"), col("w1"), col("w2")
        pieces = ctx.enter_context(nc.sbuf_tensor("route_pieces", [P, NT, NPIECE, NE], BF16))
        logit_ps = bank(psum, 0)[:, 0:NT * NE].rearrange("p (t e) -> p t e", e=NE)
        row_ps = [bank(psum, 1 + b)[0:NPIECE * NE, :].bitcast(BF16) for b in range(2)]
        logits_full = ctx.enter_context(nc.semaphore("logits_full"))
        rows_clear = ctx.enter_context(nc.semaphore("rows_clear"))
        step = ctx.enter_context(nc.semaphore("route_step"))
        gap_done = ctx.enter_context(nc.semaphore("gap_done"))
        odds_done = ctx.enter_context(nc.semaphore("odds_done"))
        pieces_done = ctx.enter_context(nc.semaphore("pieces_done"))
        rows_full = ctx.enter_context(nc.semaphore("rows_full"))
        wide = lambda a: a[:, :].unsqueeze(2).to_broadcast([P, NT, NE])
        block = ctx.enter_context(nc.Block())

        @block.tensor
        def _(pe):
            for t in range(NT):
                m = nc.tensor.matmul(logit_ps[:, t, :], h_T[:, t * P:(t + 1) * P], gate_w, start=True, stop=True)
            m.then_inc(logits_full, 1)
            pe.wait_ge(pieces_done, 1)
            for t in range(NT):
                m = nc.tensor.transpose(row_ps[t // 8][:, t % 8 * P:(t % 8 + 1) * P],
                                        pieces[:, t, :, :].rearrange("p n e -> p (n e)"), ident)
                if t % 8 == 7:
                    m.then_inc(rows_full, 1)

        @block.scalar
        def _(act):
            act.wait_ge(gap_done, 1)
            nc.scalar.activation(odds[:, :], gap[:, :], ACT.Exp).then_inc(odds_done, 1)

        @block.vector
        def _(dve):
            nc.vector.memset(w_rows[:, :], 0.0).then_inc(rows_clear, 1)
            dve.wait_ge(logits_full, 1)
            nc.vector.tensor_copy(logits[:, :, :], logit_ps[:, :, :]).then_inc(step, 1)
            n = 1
            for r, source in enumerate((logits, left)):
                dve.wait_ge(step, n)
                nc.vector.tensor_reduce(top[r][:, :], source[:, :, :], AX.X, ALU.max).then_inc(step, 1)
                dve.wait_ge(step, n + 1)
                nc.vector.tensor_tensor(is_top[:, :, :], source[:, :, :], wide(top[r]), ALU.is_equal).then_inc(step, 1)
                dve.wait_ge(step, n + 2)
                nc.vector.tensor_tensor(order[:, :, :], is_top[:, :, :], rank.unsqueeze(1).to_broadcast([P, NT, NE]), ALU.mult).then_inc(step, 1)
                dve.wait_ge(step, n + 3)
                nc.vector.tensor_reduce(best[:, :], order[:, :, :], AX.X, ALU.max).then_inc(step, 1)
                dve.wait_ge(step, n + 4)
                nc.vector.tensor_tensor(taken[r][:, :, :], order[:, :, :], wide(best), ALU.is_equal).then_inc(step, 1)
                n += 5
                if r == 0:
                    dve.wait_ge(step, n)
                    nc.vector.scalar_tensor_tensor(left[:, :, :], taken[0][:, :, :], NEG, logits[:, :, :], ALU.mult, ALU.add).then_inc(step, 1)
                    n += 1
            nc.vector.tensor_tensor(gap[:, :], top[1][:, :], top[0][:, :], ALU.subtract).then_inc(gap_done, 1)
            dve.wait_ge(odds_done, 1)
            nc.vector.tensor_scalar(total[:, :], odds[:, :], 1.0, None, ALU.add).then_inc(step, 1)
            dve.wait_ge(step, n + 1)
            nc.vector.reciprocal(w1[:, :], total[:, :]).then_inc(step, 1)
            dve.wait_ge(step, n + 2)
            nc.vector.tensor_tensor(w2[:, :], odds[:, :], w1[:, :], ALU.mult).then_inc(step, 1)
            dve.wait_ge(step, n + 3)
            nc.vector.tensor_tensor(share[:, :, :], taken[0][:, :, :], wide(w1), ALU.mult)
            nc.vector.tensor_tensor(left[:, :, :], taken[1][:, :, :], wide(w2), ALU.mult).then_inc(step, 1)
            dve.wait_ge(step, n + 4)
            nc.vector.tensor_tensor(share[:, :, :], share[:, :, :], left[:, :, :], ALU.add).then_inc(step, 1)
            for i in range(NPIECE):
                dve.wait_ge(step, n + 5 + 2 * i)
                last = nc.vector.tensor_copy(pieces[:, :, i, :], share[:, :, :])
                if i < NPIECE - 1:
                    last.then_inc(step, 1)
                    dve.wait_ge(step, n + 6 + 2 * i)
                    nc.vector.tensor_tensor(share[:, :, :], share[:, :, :], pieces[:, :, i, :], ALU.subtract).then_inc(step, 1)
                else:
                    last.then_inc(pieces_done, 1)
            dve.wait_ge(rows_clear, 1)
            for b in range(2):
                dve.wait_ge(rows_full, b + 1)
                nc.vector.tensor_copy(w_rows[0:NPIECE * NE, b * 2 * BANK:(b + 1) * 2 * BANK], row_ps[b][:, :])


def experts(nc, psum, h_T, w13, w2, w_rows, pick, y_T, x_T, gate):
    with ExitStack() as ctx:
        g_ps, u_ps, w_ps = ([bank(psum, 2 * n + b) for b in range(2)] for n in range(3))
        out_ps = bank(psum, 6)
        sb = lambda n: [ctx.enter_context(nc.sbuf_tensor(f"moe_{n}{b}", [P, BANK], F32)) for b in range(2)]
        silu, up, act_w = sb("silu"), sb("up"), sb("act_w")
        total = sb("total")[0]
        sem = lambda n: ctx.enter_context(nc.semaphore(f"moe_{n}"))
        up_full = sem("up_full")
        w_full = sem("w_full")
        silu_done = sem("silu_done")
        up_done = sem("up_done")
        act_done = sem("act_done")
        down_done = sem("down_done")
        out_free = sem("out_free")
        N = 2 * NE
        block = ctx.enter_context(nc.Block())

        @block.tensor
        def _(pe):
            def down(c, n):
                pe.wait_ge(act_done, c * N + n + 1)
                nc.tensor.matmul(out_ps[:, :], w2[:, n // 2, n % 2, :], act_w[n % 2][:, :], start=n == 0,
                                 stop=n == N - 1).then_inc(down_done, 1)

            def body(c, some_before):
                at = bass.ds(c * BANK, BANK)
                for n in range(N):
                    e, f = divmod(n, 2)
                    if some_before or n >= 2:
                        pe.wait_ge(up_done, c * N + n - 1)
                    if f == 0:
                        if some_before or e >= 2:
                            pe.wait_ge(act_done, c * N + n - 2)
                        nc.tensor.matmul(w_ps[e % 2][:, :], pick[:, e, :], w_rows[:, at], start=True, stop=True).then_inc(w_full, 1)
                    nc.tensor.matmul(g_ps[n % 2][:, :], w13[:, e, f * P:(f + 1) * P], h_T[:, at], start=True, stop=True)
                    nc.tensor.matmul(u_ps[n % 2][:, :], w13[:, e, FF + f * P:FF + (f + 1) * P], h_T[:, at],
                                     start=True, stop=True).then_inc(up_full, 1)
                    if n >= 1:
                        if n == 1 and some_before:
                            pe.wait_ge(out_free, c)
                        down(c, n - 1)
                down(c, N - 1)

            body(0, False)
            with pe.Fori(1, NC) as c:
                body(c, True)

        @block.scalar
        def _(act):
            def body(c):
                for n in range(N):
                    act.wait_ge(up_full, c * N + n + 1)
                    nc.scalar.activation(silu[n % 2][:, :], g_ps[n % 2][:, :], ACT.Silu).then_inc(silu_done, 1)

            with act.Fori(0, NC) as c:
                body(c)

        @block.vector
        def _(dve):
            def body(c, some_before):
                at = bass.ds(c * BANK, BANK)
                for n in range(N):
                    dve.wait_ge(silu_done, c * N + n + 1)
                    nc.vector.tensor_tensor(up[n % 2][:, :], silu[n % 2][:, :], u_ps[n % 2][:, :], ALU.mult).then_inc(up_done, 1)
                    dve.wait_ge(up_done, c * N + n + 1)
                    dve.wait_ge(w_full, c * NE + n // 2 + 1)
                    if some_before or n >= 2:
                        dve.wait_ge(down_done, c * N + n - 1)
                    nc.vector.tensor_tensor(act_w[n % 2][:, :], up[n % 2][:, :], w_ps[n // 2 % 2][:, :], ALU.mult).then_inc(act_done, 1)
                dve.wait_ge(down_done, c * N + N)
                nc.vector.tensor_tensor(total[:, :], y_T[:, at], out_ps[:, :], ALU.add).then_inc(out_free, 1)
                dve.wait_ge(out_free, c + 1)
                nc.vector.scalar_tensor_tensor(x_T[:, at], total[:, :], gate, x_T[:, at], ALU.mult, ALU.add)

            body(0, False)
            with dve.Fori(1, NC) as c:
                body(c, True)


def shift_tokens(nc, name, src_T, out_T):
    with ExitStack() as ctx:
        block = ctx.enter_context(nc.Block())

        @block.vector
        def _(dve):
            nc.vector.tensor_copy(out_T[0:P // 2, :], src_T[0:P // 2, :])

        @block.scalar
        def _(act):
            nc.scalar.activation(out_T[P // 2:P, 1:S], src_T[P // 2:P, 0:S - 1], ACT.Copy)

        @block.gpsimd
        def _(pool):
            nc.gpsimd.memset(out_T[P // 2:P, 0:1], 0.0)


def after(engine, semaphore, count):
    if not isinstance(count, int) or count > 0:
        engine.wait_ge(semaphore, count)


def local_project(nc, psum, name, hs_T, w_in, w_v, tables, scales, pair_rows, pair_spread, q_T, k_T, v_tok, q_scale):
    with ExitStack() as ctx:
        sb = lambda n, s: ctx.enter_context(nc.sbuf_tensor(f"{name}_{n}", s, F32))
        sem = lambda n: ctx.enter_context(nc.semaphore(f"{name}_{n}"))
        table = [sb(f"table{i}", [P, 2, BANK]) for i in range(2)]
        straight = [sb(f"straight{b}", [P, BANK]) for b in range(2)]
        swapped = [sb(f"swapped{b}", [P, BANK]) for b in range(2)]
        q_square = [sb(f"q_square{b}", [P, BANK]) for b in range(2)]
        k_square = sb("k_square", [P, NPAIR, BANK])
        k_turned = sb("k_turned", [P, NPAIR, BANK])
        k_std, k_inv = sb("k_std", [P, BANK]), sb("k_inv", [P, BANK])
        q_std, q_inv = sb("q_std", [P, 4, LH]), sb("q_inv", [P, 4, LH])
        raw = [[bank(psum, 2 * b + n) for n in range(2)] for b in range(2)]
        k_sum, v_ps, spread = bank(psum, 4), bank(psum, 6), bank(psum, 7)
        q_sum = bank(psum, 5)[:, 0:4 * LH].rearrange("p (t h) -> p t h", t=4)

        table_in = [sem(f"table_in{i}") for i in range(2)]
        raw_full = sem("raw_full")
        square_done = sem("square_done")
        swapped_done = sem("swapped_done")
        straight_done = sem("straight_done")
        turned = sem("turned")
        k_sum_full = sem("k_sum_full")
        k_std_done = sem("k_std_done")
        k_clipped = sem("k_clipped")
        k_inv_done = sem("k_inv_done")
        q_sum_full = sem("q_sum_full")
        q_std_done = sem("q_std_done")
        q_step = sem("q_step")
        v_full = sem("v_full")
        v_done = sem("v_done")
        spread_full = sem("spread_full")
        k_done = sem("k_done")
        pad_set = sem("pad_set")
        N = 2 * NPAIR
        MIN_NORM = 1e-12
        SCALE = 8.0
        block = ctx.enter_context(nc.Block())

        items = [(c, n) for c in range(NC) for n in range(N)]

        @block.sync
        def _(sp):
            for c in range(NC):
                for i, w in ((0, 2), (1, 0)):
                    if c > 0:
                        sp.wait_ge(straight_done, (c - 1) * N + (i + 1) * NPAIR)
                    sp.dma_start(table[i][:, :, :], tables[:, w:w + 2, chunk(c)]).then_inc(table_in[i], 16)

        @block.tensor
        def _(pe):
            def q_sums(c, m):
                pe.wait_ge(square_done, c * N + NPAIR + m + 1)
                if m == 0 and c > 0:
                    pe.wait_ge(q_std_done, c)
                for t in range(4):
                    last = nc.tensor.matmul(q_sum[:, t, 2 * m:2 * m + 2], q_square[m % 2][:, t * P:(t + 1) * P],
                                            pair_rows[:, 15:17], start=True, stop=True)
                last.then_inc(q_sum_full, 1)

            for g, (c, n) in enumerate(items):
                first = 2 if n < NPAIR else 0
                if g >= 2:
                    pe.wait_ge(straight_done, g - 1)
                for i in range(2):
                    last = nc.tensor.matmul(raw[g % 2][i], w_in[:, first + i, n % NPAIR, :], hs_T[:, chunk(c)], start=True, stop=True)
                last.then_inc(raw_full, 1)
                if n == NPAIR:
                    pe.wait_ge(square_done, c * N + NPAIR)
                    if c > 0:
                        pe.wait_ge(k_std_done, c)
                    for m in range(NPAIR):
                        last = nc.tensor.matmul(k_sum[32 * m:32 * m + 32, :], pair_rows, k_square[:, m, :], start=True, stop=True)
                    last.then_inc(k_sum_full, 1)
                if n > NPAIR:
                    q_sums(c, n - NPAIR - 1)
                if n == N - 1:
                    for t in range(4):
                        if c + t > 0:
                            pe.wait_ge(v_done, c * 4 + t)
                        tokens = slice(c * BANK + t * P, c * BANK + (t + 1) * P)
                        nc.tensor.matmul(v_ps, hs_T[:, tokens], w_v, start=True, stop=True).then_inc(v_full, 1)
                        if t == 0:
                            q_sums(c, NPAIR - 1)
                            pe.wait_ge(k_inv_done, c + 1)
                        if c + t > 0:
                            pe.wait_ge(k_done, c * NPAIR + t)
                        nc.tensor.matmul(spread, pair_spread[32 * t:32 * t + 32, :], k_inv[32 * t:32 * t + 32, :],
                                         start=True, stop=True).then_inc(spread_full, 1)

        @block.scalar
        def _(act):
            for g, (c, n) in enumerate(items):
                m = n % NPAIR
                act.wait_ge(raw_full, g + 1)
                if n == 0 and c > 0:
                    act.wait_ge(k_sum_full, c)
                if n >= NPAIR and c * NPAIR + m >= 2:
                    act.wait_ge(q_sum_full, c * NPAIR + m - 1)
                to = k_square[:, m, :] if n < NPAIR else q_square[m % 2][:, :]
                nc.scalar.activation(to, raw[g % 2][0], ACT.Square).then_inc(square_done, 1)
                if n == NPAIR:
                    act.wait_ge(k_sum_full, c + 1)
                    if c > 0:
                        act.wait_ge(k_clipped, c)
                    nc.scalar.activation(k_std[:, :], k_sum, ACT.Sqrt).then_inc(k_std_done, 1)
                if n == N - 1:
                    for t in range(4):
                        act.wait_ge(v_full, c * 4 + t + 1)
                        nc.scalar.activation(v_tok[:, 1 + 4 * c + t, :], v_ps, ACT.Copy).then_inc(v_done, 1)
                        if t == 0:
                            act.wait_ge(q_sum_full, (c + 1) * NPAIR)
                            if c > 0:
                                act.wait_ge(q_step, c * 3)
                            nc.scalar.activation(q_std[:, :, :], q_sum, ACT.Sqrt).then_inc(q_std_done, 1)

        @block.vector
        def _(dve):
            nc.vector.memset(v_tok[:, 0, :], 0.0)
            nc.vector.memset(k_T[:, :, 0:WINDOW], 0.0).then_inc(pad_set, 1)
            for g, (c, n) in enumerate(items):
                kind = 0 if n < NPAIR else 1
                column = 2 - 2 * kind
                dve.wait_ge(raw_full, g + 1)
                if n % NPAIR == 0:
                    dve.wait_ge(table_in[kind], 16 * (c + 1))
                if g >= 2:
                    dve.wait_ge(turned, g - 1)
                nc.vector.scalar_tensor_tensor(swapped[g % 2][:, :], raw[g % 2][1], scales[column + 1], table[kind][:, 1, :],
                                               ALU.mult, ALU.mult).then_inc(swapped_done, 1)
                dve.wait_ge(square_done, g + 1)
                nc.vector.scalar_tensor_tensor(straight[g % 2][:, :], raw[g % 2][0], scales[column], table[kind][:, 0, :],
                                               ALU.mult, ALU.mult).then_inc(straight_done, 1)
                if n == NPAIR + 1:
                    dve.wait_ge(k_std_done, c + 1)
                    nc.vector.tensor_scalar(k_std[:, :], k_std[:, :], MIN_NORM, None, ALU.max).then_inc(k_clipped, 1)
                    dve.wait_ge(k_clipped, c + 1)
                    nc.vector.reciprocal(k_inv[:, :], k_std[:, :]).then_inc(k_inv_done, 1)
                if n == N - 1:
                    dve.wait_ge(turned, c * N + NPAIR)
                    for m in range(NPAIR):
                        dve.wait_ge(spread_full, c * NPAIR + m + 1)
                        nc.vector.tensor_tensor(k_T[:, m, WINDOW + c * BANK:WINDOW + (c + 1) * BANK], k_turned[:, m, :], spread,
                                                ALU.mult).then_inc(k_done, 1)
                    dve.wait_ge(q_std_done, c + 1)
                    nc.vector.tensor_scalar(q_inv[:, :, :], q_std[:, :, :], MIN_NORM, None, ALU.max).then_inc(q_step, 1)
                    dve.wait_ge(q_step, 3 * c + 1)
                    nc.vector.reciprocal(q_inv[:, :, :], q_inv[:, :, :]).then_inc(q_step, 1)
                    dve.wait_ge(q_step, 3 * c + 2)
                    nc.vector.tensor_scalar(q_scale[:, 4 * c:4 * c + 4, :], q_inv[:, :, :], SCALE, None, ALU.mult).then_inc(q_step, 1)

        @block.gpsimd
        def _(pool):
            for g, (c, n) in enumerate(items):
                m = n % NPAIR
                pool.wait_ge(swapped_done, g + 1)
                pool.wait_ge(straight_done, g + 1)
                if n < NPAIR and c > 0:
                    pool.wait_ge(k_done, (c - 1) * NPAIR + m + 1)
                to = k_turned[:, m, :] if n < NPAIR else q_T[:, 4 * c:4 * c + 4, m, :]
                tiles = lambda a: a if n < NPAIR else a.rearrange("p (t i) -> p t i", t=4)
                nc.gpsimd.tensor_tensor(to, tiles(straight[g % 2][:, :]), tiles(swapped[g % 2][:, :]), ALU.add).then_inc(turned, 1)
            pool.wait_ge(pad_set, 1)


def local_attend(nc, psum, name, q_T, k_T, v_tok, q_scale, w_out, bands, ident, ident_bf, x_T):
    with ExitStack() as ctx:
        sb = lambda n, s, d=F32: ctx.enter_context(nc.sbuf_tensor(f"{name}_{n}", s, d))
        sem = lambda n: ctx.enter_context(nc.semaphore(f"{name}_{n}"))
        q = [sb(f"q{b}", [P, NPAIR, P]) for b in range(2)]
        k = [sb(f"k{b}", [P, NPAIR, KEYS]) for b in range(2)]
        v_own = [sb(f"v_own{b}", [P, INNER]) for b in range(2)]
        v_past = [sb(f"v_past{b}", [P, NPAIR, LD]) for b in range(2)]
        scale = [sb(f"scale{b}", [P, LH]) for b in range(2)]
        neg_max = [sb(f"neg_max{b}", [P, LH]) for b in range(2)]
        bias = [sb(f"bias{b}", [P, LH]) for b in range(2)]
        den = [sb(f"den{b}", [P, LH]) for b in range(2)]
        inv = [sb(f"inv{b}", [P, LH]) for b in range(2)]
        probs = [sb(f"probs{b}", [P, LH, KEYS]) for b in range(2)]
        own_T = [sb(f"own_T{b}", [P, LH, P]) for b in range(2)]
        past_T = [sb(f"past_T{b}", [P, NPAIR, P]) for b in range(2)]
        o_T = sb("o_T", [P, NPAIR, P])
        score = [bank(psum, n) for n in range(4)]
        own_ps, past_ps, o_ps, out_ps = (bank(psum, 4 + n) for n in range(4))

        qk_in = [sem(f"qk_in{b}") for b in range(2)]
        scale_in = sem("scale_in")
        v_in = [sem(f"v_in{b}") for b in range(2)]
        score_full = sem("score_full")
        max_done = sem("max_done")
        bias_done = sem("bias_done")
        exp_done = sem("exp_done")
        inv_done = sem("inv_done")
        share_done = sem("share_done")
        own_full = sem("own_full")
        own_done = sem("own_done")
        past_full = sem("past_full")
        past_done = sem("past_done")
        o_full = sem("o_full")
        o_done = sem("o_done")
        out_full = sem("out_full")
        out_done = sem("out_done")
        heads_of = lambda u: slice(4 * u, 4 * u + 4)
        block = ctx.enter_context(nc.Block())

        def steps(engine, step):
            step(-1, 1, True, False, False)
            step(0, 0, True, True, False)
            with engine.Fori(0, NT // 2 - 1) as i:
                step(2 * i + 1, 1, True, True, True)
                step(2 * i + 2, 0, True, True, True)
            step(NT - 1, 1, False, True, True)
            step(NT, 0, False, False, True)

        @block.sync
        def _(sp):
            def queries_and_keys(t, b):
                after(sp, score_full, (t - 1) * 2)
                sp.dma_start(q[b][:, :, :], q_T[:, bass.ds(t, 1), :, :].rearrange("p t m i -> p (t m) i")).then_inc(qk_in[b], 16)
                sp.dma_start(k[b][:, :, :], k_T[:, :, bass.ds(t * P, KEYS)]).then_inc(qk_in[b], 16)

            def values(t, b):
                after(sp, o_full, t - 1)
                past = v_tok[WINDOW:P, bass.ds(t, 1), :].rearrange("p t (m two d) -> p two (t m) d", two=2, d=LD)
                for half in range(2):
                    sp.dma_start(v_past[b][half * LD:(half + 1) * LD, :, :], past[:, half]).then_inc(v_in[b], 16)
                sp.dma_start(v_own[b][:, :], v_tok[:, bass.ds(t + 1, 1), :].rearrange("p t d -> p (t d)")).then_inc(v_in[b], 16)

            for t in range(2):
                queries_and_keys(t, t)
            for t in range(2):
                values(t, t)
                queries_and_keys(t + 2, t)
            with sp.Fori(1, NT // 2 - 1) as i:
                for b in range(2):
                    values(2 * i + b, b)
                    queries_and_keys(2 * i + b + 2, b)
            for t in range(NT - 2, NT):
                values(t, t % 2)

        @block.gpsimd
        def _(pool):
            def step(i, b, now, flip, put):
                if now:
                    t = i + 1
                    for u in range(2):
                        pool.wait_ge(inv_done, t * 2 + u + 1)
                        pool.wait_ge(exp_done, t * 2 + u + 1)
                        mine = probs[1 - b][:, heads_of(u), :]
                        nc.gpsimd.tensor_tensor(mine, mine, inv[1 - b][:, heads_of(u)].unsqueeze(2).to_broadcast([P, 4, KEYS]),
                                                ALU.mult).then_inc(share_done, 1)

            steps(pool, step)

        @block.tensor
        def _(pe):
            def scores(t, b, u, first):
                if u == 0:
                    pe.wait_ge(qk_in[b], 16 * (t - b) + 32)
                after(pe, exp_done, t * 2 + u - 1)
                for m in (2 * u, 2 * u + 1):
                    even, odd = (score[2 * half + u][:, m % 2 * KEYS:(m % 2 + 1) * KEYS] for half in range(2))
                    nc.tensor.matmul(even[:, 0:P], q[b][0:LD, m, :], k[b][0:LD, m, WINDOW:KEYS],
                                     start=m % 2 == 0, stop=False, skip_group_check=True)
                    nc.tensor.matmul(odd, q[b][LD:P, m, :], k[b][LD:P, m, :],
                                     start=m % 2 == 0, stop=False, skip_group_check=True)
                    nc.tensor.matmul(even[:, P:KEYS], q[b][0:LD, m, :], k[b][0:LD, m, 0:WINDOW],
                                     start=False, stop=False, skip_group_check=True)
                for half in range(2):
                    last = nc.tensor.matmul(score[2 * half + u][:, 0:2 * KEYS], ident_bf, bands[half][0 if first else 1],
                                            start=False, stop=True, skip_group_check=True)
                last.then_inc(score_full, 1)

            def flip_own(t, b, u):
                pe.wait_ge(share_done, t * 2 + u + 1)
                after(pe, own_done, t * 2 + u)
                for n in range(4):
                    last = nc.tensor.transpose(own_ps[:, n * P:(n + 1) * P], probs[b][:, 4 * u + n, n % 2 * WINDOW:n % 2 * WINDOW + P], ident)
                last.then_inc(own_full, 1)

            def flip_past(t, b):
                after(pe, past_done, t)
                both = probs[b][:, :, :].rearrange("p h k -> p (h k)")
                for m in range(NPAIR):
                    last = nc.tensor.transpose(past_ps[:, m * P:(m + 1) * P], both[:, 2 * m * KEYS + P:2 * m * KEYS + 2 * P], ident)
                last.then_inc(past_full, 1)

            def outputs(t, b):
                pe.wait_ge(v_in[b], 24 * (t - b) + 48)
                after(pe, o_done, t)
                pe.wait_ge(past_done, t + 1)
                pe.wait_ge(own_done, t * 2 + 2)
                for m in range(NPAIR):
                    for half in range(2):
                        r = slice(half * LD, (half + 1) * LD)
                        nc.tensor.matmul(o_ps[r, m * P:(m + 1) * P], v_own[b][:, (2 * m + half) * LD:(2 * m + half + 1) * LD], own_T[b][:, 2 * m + half, :],
                                         start=True, stop=False, skip_group_check=True)
                    for half in range(2):
                        r = slice(half * LD, (half + 1) * LD)
                        last = nc.tensor.matmul(o_ps[r, m * P:(m + 1) * P], v_past[b][r, m, :], past_T[b][r, m, :],
                                                start=False, stop=True, skip_group_check=True)
                last.then_inc(o_full, 1)

            def project_out(t):
                pe.wait_ge(o_done, t + 1)
                after(pe, out_done, t)
                for m in range(NPAIR):
                    last = nc.tensor.matmul(out_ps[:, 0:P], w_out[:, m, :], o_T[:, m, :], start=m == 0, stop=m == NPAIR - 1)
                last.then_inc(out_full, 1)

            def step(i, b, now, flip, put):
                first = isinstance(i, int) and i == -1
                if now:
                    scores(i + 1, 1 - b, 0, first)
                if flip:
                    flip_own(i, b, 0)
                if put:
                    outputs(i - 1, 1 - b)
                if flip:
                    flip_own(i, b, 1)
                if now:
                    scores(i + 1, 1 - b, 1, first)
                if flip:
                    flip_past(i, b)
                if put:
                    project_out(i - 1)

            steps(pe, step)

        @block.scalar
        def _(act):
            def exponentials(t, b, u):
                act.wait_ge(bias_done, t * 2 + u + 1)
                if u == 0:
                    after(act, past_full, t - 1)
                for h in range(4 * u, 4 * u + 4):
                    m, half = divmod(h, 2)
                    last = nc.scalar.activation(probs[b][:, h, :], score[2 * half + u][:, m % 2 * KEYS:(m % 2 + 1) * KEYS], ACT.Exp,
                                                scale=scale[b][:, h:h + 1], bias=bias[b][:, h:h + 1], accum_out=den[b][:, h:h + 1])
                last.then_inc(exp_done, 1)

            def own(t, b, u):
                if u == 0:
                    after(act, o_full, t - 1)
                act.wait_ge(own_full, t * 2 + u + 1)
                nc.scalar.activation(own_T[b][:, heads_of(u), :], own_ps.rearrange("p (h i) -> p h i", h=4), ACT.Copy).then_inc(own_done, 1)

            def step(i, b, now, flip, put):
                if flip:
                    own(i, b, 0)
                if now:
                    exponentials(i + 1, 1 - b, 0)
                if put:
                    after(act, out_full, i - 1)
                    act.wait_ge(o_full, i)
                    nc.scalar.activation(o_T[:, :, :], o_ps.rearrange("p (m i) -> p m i", m=NPAIR), ACT.Copy).then_inc(o_done, 1)
                if flip:
                    own(i, b, 1)
                if now:
                    exponentials(i + 1, 1 - b, 1)

            steps(act, step)

        @block.vector
        def _(dve):
            def maxima(t, b, u):
                if u == 0:
                    after(dve, exp_done, (t - 1) * 2)
                    nc.vector.tensor_copy(scale[b][:, :].unsqueeze(1), q_scale[:, bass.ds(t, 1), :]).then_inc(scale_in, 1)
                dve.wait_ge(score_full, t * 2 + u + 1)
                for half in range(2):
                    nc.vector.tensor_reduce(neg_max[b][:, 4 * u + half:4 * u + half + 3:2],
                                            score[2 * half + u][:, 0:2 * KEYS].rearrange("p (h k) -> p h k", h=2),
                                            AX.X, ALU.max, negate=True).then_inc(max_done, 1)
                dve.wait_ge(scale_in, t + 1)
                dve.wait_ge(max_done, t * 4 + 2 * u + 2)
                nc.vector.tensor_tensor(bias[b][:, heads_of(u)], neg_max[b][:, heads_of(u)], scale[b][:, heads_of(u)], ALU.mult).then_inc(bias_done, 1)

            def inverses(t, b, u):
                dve.wait_ge(exp_done, t * 2 + u + 1)
                after(dve, share_done, (t - 2) * 2 + u + 1)
                nc.vector.reciprocal(inv[b][:, heads_of(u)], den[b][:, heads_of(u)]).then_inc(inv_done, 1)

            def step(i, b, now, flip, put):
                if now:
                    maxima(i + 1, 1 - b, 0)
                    inverses(i + 1, 1 - b, 0)
                    maxima(i + 1, 1 - b, 1)
                if flip:
                    after(dve, o_full, i - 1)
                    dve.wait_ge(past_full, i + 1)
                    nc.vector.tensor_copy(past_T[b][:, :, :], past_ps.rearrange("p (m i) -> p m i", m=NPAIR)).then_inc(past_done, 1)
                if now:
                    inverses(i + 1, 1 - b, 1)
                if put:
                    dve.wait_ge(out_full, i)
                    at = bass.ds((i - 1) * P, P)
                    nc.vector.tensor_tensor(x_T[:, at], x_T[:, at], out_ps[:, 0:P], ALU.add).then_inc(out_done, 1)

            steps(dve, step)


def feed_forward(nc, psum, name, u_T, w1, b1, w2, b2, x_T):
    parts = [min(P, HID - n * P) for n in range(-(-HID // P))]
    NP = len(parts)
    with ExitStack() as ctx:
        a_ps, g_ps, out_ps = ([bank(psum, 2 * n + b) for b in range(2)] for n in range(3))
        gelu = [ctx.enter_context(nc.sbuf_tensor(f"{name}_gelu{b}", [P, BANK], F32)) for b in range(2)]
        mixed = [ctx.enter_context(nc.sbuf_tensor(f"{name}_mixed{b}", [P, BANK], F32)) for b in range(2)]
        sem = lambda n: ctx.enter_context(nc.semaphore(f"{name}_{n}"))
        up_full = sem("up_full")
        gelu_done = sem("gelu_done")
        mixed_done = sem("mixed_done")
        down_done = sem("down_done")
        out_done = sem("out_done")
        work = [(c, n) for c in range(NC) for n in range(NP)]
        block = ctx.enter_context(nc.Block())

        @block.tensor
        def _(pe):
            def down(i):
                c, n = work[i]
                pe.wait_ge(mixed_done, i + 1)
                if n == 0 and c >= 2:
                    pe.wait_ge(out_done, c - 1)
                nc.tensor.matmul(out_ps[c % 2][:, :], w2[0:parts[n], n, :], mixed[i % 2][0:parts[n], :], start=n == 0,
                                 stop=n == NP - 1).then_inc(down_done, 1)

            for i, (c, n) in enumerate(work):
                if i >= 2:
                    pe.wait_ge(mixed_done, i - 1)
                for to, at in ((a_ps, 0), (g_ps, HID)):
                    m = nc.tensor.matmul(to[i % 2][0:parts[n], :], w1[:, at + n * P:at + n * P + parts[n]], u_T[:, chunk(c)], start=True, stop=True)
                m.then_inc(up_full, 1)
                if i >= 1:
                    down(i - 1)
            down(len(work) - 1)

        @block.scalar
        def _(act):
            for i, (c, n) in enumerate(work):
                act.wait_ge(up_full, i + 1)
                r = slice(0, parts[n])
                nc.scalar.activation(gelu[i % 2][r, :], g_ps[i % 2][r, :], ACT.Gelu, bias=b1[r, 1, n:n + 1]).then_inc(gelu_done, 1)

        @block.vector
        def _(dve):
            def add(c):
                dve.wait_ge(down_done, (c + 1) * NP)
                nc.vector.scalar_tensor_tensor(x_T[:, chunk(c)], out_ps[c % 2][:, :], b2, x_T[:, chunk(c)], ALU.add, ALU.add).then_inc(out_done, 1)

            for i, (c, n) in enumerate(work):
                dve.wait_ge(gelu_done, i + 1)
                if i >= 2:
                    dve.wait_ge(down_done, i - 1)
                r = slice(0, parts[n])
                nc.vector.scalar_tensor_tensor(mixed[i % 2][r, :], a_ps[i % 2][r, :], b1[r, 0, n:n + 1], gelu[i % 2][r, :], ALU.add, ALU.mult).then_inc(mixed_done, 1)
                if n == 0 and c >= 1:
                    add(c - 1)
            add(NC - 1)


def clear_semaphores(nc, first):
    last = max(nc.released_uncleared_semaphores)
    with nc.Block() as block:
        @block.gpsimd
        def _(pool):
            pool.sem_clear(range(first, last + 1))


def forward(nc, a, out):
    with ExitStack() as ctx:
        sb = lambda n, s, d=F32: ctx.enter_context(nc.sbuf_tensor(n, s, d))
        x_T, h_T, u_T = (sb(n, [P, S])[:, :] for n in ("x_T", "h_T", "u_T"))
        psum = ctx.enter_context(nc.psum_tensor("psum", [P, 8 * BANK], F32))
        q_dram = nc.dram_tensor("q_pieces", [NPIECE, P, S], BF16, kind="Internal").ap()
        k_dram = nc.dram_tensor("k_pieces", [NPIECE, P, S], BF16, kind="Internal").ap()
        z_dram = nc.dram_tensor("z_heads", [P, S], F32, kind="Internal").ap()
        den_dram = nc.dram_tensor("den_heads", [NH, S], F32, kind="Internal").ap()

        def held(scope, *names):
            return {n: scope.enter_context(nc.sbuf_tensor(f"{n}_sb", list(a[n].shape), a[n].dtype)) for n in names}

        full = lambda t: t[tuple(slice(None) for _ in t.shape)]
        early = held(ctx, "mean_of", "masks", "cols")
        mod = sb("mod", [P, 2, 2, 3])
        gated = sb("gated", [P, 2])
        ident = sb("ident_sb", [P, P])[:, :]
        late = held(ctx, "w_in", "w_v", "w_out", "pair_rows", "pair_spread", "bands", "w_up", "b_up", "w_down")
        attend = ctx.enter_context(ExitStack())
        z_T = attend.enter_context(nc.sbuf_tensor("z_T", [P, S], F32))[:, :]
        v_tok = attend.enter_context(nc.sbuf_tensor("v_tok", [P, NT, P], F32))
        den = attend.enter_context(nc.sbuf_tensor("den", [NH, S], F32))[:, :]
        early.update(held(attend, "head_rows", "regroup", "keep_kq", "wmods", "cs", "w_attn0", "bv0", "w_attn1", "w_attn2"))
        moe = ctx.enter_context(ExitStack())
        late.update(held(moe, "gate_w", "rank", "pick", "w13", "w2"))
        late_in = ctx.enter_context(nc.semaphore("late_in"))

        first_sem = nc.free_semaphores[0]
        load_inputs(nc, psum, a["x"], x_T, (ident, a["ident"]), [(full(b), a[n]) for n, b in early.items()])
        with nc.Block() as block:
            @block.scalar
            def _(act):
                for n, b in late.items():
                    act.dma_start(full(b), a[n]).then_inc(late_in, 16)

        w0, w1, w2 = early["w_attn0"], early["w_attn1"], early["w_attn2"]
        mean_of, head_rows = full(early["mean_of"]), full(early["head_rows"])
        cols = {n: early["cols"][:, i:i + 1] for i, n in enumerate(COLS)}
        ident_bf, mask_qk, mask_kq = (early["masks"][:, i, :] for i in range(3))
        shift_of = lambda l, i: mod[:, l, i, 0:1]
        scale_of = lambda l, i: mod[:, l, i, 1:2]
        gate_of = lambda l, i: mod[:, l, i, 2:3]
        modulation(nc, psum, [(early["cs"][:, l:l + 1], early["wmods"][:, l, :]) for l in range(2)], mod,
                   cols["gamma"], cols["beta"], gated)

        norm(nc, psum, "ln0a", x_T, h_T, mean_of, LN_EPS, scale_of(0, 0), shift_of(0, 0))
        project(nc, psum, "proj0", h_T, w0[:, 0, :], w0[:, 1, :], w0[:, 2, :], q_dram, k_dram, v_tok,
                bias=(cols["bq"], cols["bk"], early["bv0"]))
        attention(nc, psum, "att0", False, S ** -0.5, q_dram, k_dram, v_tok, z_dram, den_dram, z_T, den,
                  ident_bf, mask_qk, mask_kq, early["keep_kq"][:, :])
        divide_by_sums(nc, psum, "com0", z_T, den, head_rows, h_T, regroup=full(early["regroup"]))
        norm(nc, psum, "ln0z", z_T, None, mean_of, LN_EPS, gated[:, 0:1], gated[:, 1:2], add_to=x_T)
        norm(nc, psum, "ln0b", x_T, h_T, mean_of, LN_EPS, scale_of(0, 1), shift_of(0, 1))
        norm(nc, psum, "rms1", h_T, u_T, mean_of, 1e-5, cols["ln1"])
        with ExitStack() as rope:
            angle = rope.enter_context(nc.sbuf_tensor("rope_sb", [P, 2, S], F32))
            rope_in = rope.enter_context(nc.semaphore("rope_in"))
            with nc.Block() as block:
                @block.sync
                def _(sp):
                    sp.dma_start(angle[:, :, :], a["rope"]).then_inc(rope_in, 16)
                    sp.wait_ge(rope_in, 16)
            project(nc, psum, "proj1", u_T, w1[:, 0, :], w1[:, 1, :], w1[:, 2, :], q_dram, k_dram, v_tok,
                    rope=(w1[:, 3, :], w1[:, 4, :], angle[:, 0, :], angle[:, 1, :]))
        attention(nc, psum, "att1", True, HD ** -0.5, q_dram, k_dram, v_tok, z_dram, den_dram, z_T, den, ident_bf, mask_qk, mask_kq)
        divide_by_sums(nc, psum, "com1", z_T, den, head_rows, h_T, w1[:, 5, :], 1.0)
        norm(nc, psum, "rms2", h_T, u_T, mean_of, 1e-5, cols["ln2"])
        with nc.Block() as block:
            @block.sync
            def _(sp):
                sp.wait_ge(late_in, 16 * len(late))
        w_rows = moe.enter_context(nc.sbuf_tensor("w_rows", [P, S], BF16))[:, :]
        router(nc, psum, u_T, full(late["gate_w"]), full(late["rank"]), ident_bf, w_rows)
        experts(nc, psum, u_T, late["w13"], late["w2"], w_rows, late["pick"], h_T, x_T, gate_of(0, 1))
        moe.close()
        clear_semaphores(nc, first_sem)
        norm(nc, psum, "ln1a", x_T, h_T, mean_of, LN_EPS, scale_of(1, 0), shift_of(1, 0))
        project(nc, psum, "proj2", h_T, w2[:, 0, :], w2[:, 1, :], w2[:, 2, :], q_dram, k_dram, v_tok)
        attention(nc, psum, "att2", True, P ** -0.5, q_dram, k_dram, v_tok, z_dram, den_dram, z_T, den, ident_bf, mask_qk, mask_kq)
        divide_by_sums(nc, psum, "com2", z_T, den, head_rows, x_T, w2[:, 3, :], gate_of(1, 0))
        norm(nc, psum, "ln1b", x_T, h_T, mean_of, LN_EPS, scale_of(1, 1), shift_of(1, 1))
        attend.close()
        for l in range(2):
            shift_tokens(nc, f"shift{l}a", h_T, u_T)
            with ExitStack() as local:
                hold = lambda n, s: local.enter_context(nc.sbuf_tensor(f"local{l}_{n}", s, F32))
                q_local, k_local = hold("q_T", [P, NT, NPAIR, P]), hold("k_T", [P, NPAIR, WINDOW + S])
                v_local, q_scale = hold("v_tok", [P, 1 + NT, INNER]), hold("q_scale", [P, NT, LH])
                local_project(nc, psum, f"lproj{l}", u_T, late["w_in"][:, l], late["w_v"][:, l, :], a["tables"],
                              [cols[f"scale{l}{n}"] for n in range(4)], full(late["pair_rows"]), full(late["pair_spread"]),
                              q_local, k_local, v_local, q_scale)
                local_attend(nc, psum, f"latt{l}", q_local, k_local, v_local, q_scale, late["w_out"][:, l],
                             [[late["bands"][:, half, i] for i in range(2)] for half in range(2)], ident, ident_bf, h_T)
            shift_tokens(nc, f"shift{l}b", h_T, u_T)
            with ExitStack() as ffn:
                normed = ffn.enter_context(nc.sbuf_tensor(f"ffn{l}_T", [P, S], F32))[:, :]
                norm(nc, psum, f"lnf{l}", u_T, normed, mean_of, LN_EPS, cols[f"lg{l}"], cols[f"lb{l}"])
                feed_forward(nc, psum, f"ff{l}", normed, late["w_up"][:, l, :], late["b_up"][:, l], late["w_down"][:, l], cols[f"b2{l}"], h_T)
        with ExitStack() as last:
            with nc.Block() as block:
                @block.vector
                def _(dve):
                    nc.vector.scalar_tensor_tensor(x_T, h_T, gate_of(1, 1), x_T, ALU.mult, ALU.add)
        store_output(nc, psum, x_T, out, ident)


COLS = ["gamma", "beta", "bq", "bk", "ln1", "ln2"] + [f"scale{l}{n}" for l in range(2) for n in range(4)] \
    + [f"{n}{l}" for l in range(2) for n in ("lg", "lb", "b2")]


def constants():
    import numpy as np
    f32, bf16 = np.float32, mybir.dt.np(BF16)
    i = np.arange(P)
    c = {"ident": np.eye(P, dtype=f32), "mean_of": np.full((P, P), 1.0 / P, f32)}
    c["head_rows"] = np.repeat(np.eye(NH, dtype=f32), HD, axis=1)
    regroup = np.zeros((P, NH * 32 + 24), f32)
    for p in range(P):
        regroup[p, 24 + p // HD * 32 + p % HD] = 1
    c["regroup"] = regroup
    mask_qk = np.where(i[None, :] > i[:, None], NEG, 0.0)
    c["masks"] = np.stack([np.eye(P), mask_qk, mask_qk.T], axis=1).astype(bf16)
    c["keep_kq"] = (i[:, None] >= i[None, :]).astype(f32)
    c["rank"] = np.broadcast_to(np.arange(NE, 0, -1).astype(f32), (P, NE)).copy()
    pick = np.zeros((P, NE, P), bf16)
    for e in range(NE):
        pick[e:NPIECE * NE:NE, e, :] = 1
    c["pick"] = pick
    second = i >= LD
    c["pair_rows"] = np.where(second[:, None] == (i[None, 0:32] >= 16), 1, 0).astype(f32)
    c["pair_spread"] = ((i[:, None] % 32 == 0) & ~second[None, :] | (i[:, None] % 32 == 16) & second[None, :]).astype(f32)
    j = np.arange(KEYS)[None, :] - WINDOW
    seen = (j <= i[:, None]) & (j >= i[:, None] - WINDOW)
    bands = np.stack([np.where(seen & (j >= 0), 0.0, NEG), np.where(seen, 0.0, NEG)])
    bands = np.stack([np.roll(bands, P, axis=2), bands])
    c["bands"] = np.ascontiguousarray(np.stack([bands, bands], axis=2).transpose(3, 0, 1, 2, 4)).astype(bf16)
    t = np.arange(S, dtype=f32)

    def angles(dim):
        inv = (f32(1) / (f32(10000.0) ** (np.arange(0, dim, 2, dtype=f32) / f32(dim)).astype(f32))).astype(f32)
        freq = (t[:, None] * inv[None, :]).astype(f32).astype(np.float64)
        freq = np.concatenate([freq, freq], axis=1).T
        sign = np.where(np.arange(dim) < dim // 2, -1.0, 1.0)[:, None]
        return np.cos(freq).astype(f32), (np.sin(freq) * sign).astype(f32)

    cos, sin = angles(HD)
    c["rope"] = np.ascontiguousarray(np.tile(np.stack([cos, sin], axis=1), (NH, 1, 1)))
    cos, sin = angles(LD)
    half = np.arange(0, LD, 2, dtype=f32)
    base = ((half + f32(0.4 * LD)) / f32(1.4 * LD)).astype(f32)
    power = ((t - S // 2) / f32(WINDOW // 2)).astype(f32)
    scale = (base[None, :].astype(np.float64) ** power[:, None]).astype(f32)
    scale = np.concatenate([scale, scale], axis=1).T
    tables = np.stack([cos * scale, sin * scale, cos / scale, sin / scale], axis=1).astype(f32)
    c["tables"] = np.ascontiguousarray(np.tile(tables, (2, 1, 1)))
    return c


def layout(np, i):
    cont = np.ascontiguousarray
    swap = lambda w, dim: w.reshape(-1, 2, dim // 2, w.shape[-1])[:, ::-1].reshape(w.shape)
    a = {"x": i["L0_attn_embedded"], "cs": cont(np.concatenate([i["L0_c"], i["L1_c"]], axis=0).T)}
    a["wmods"] = cont(np.stack([i["L0_wmod"], i["L1_wmod"]], axis=1))
    a["w_attn0"] = cont(np.stack([i[f"L0_attn_W{n}"].T for n in "qkv"], axis=1))
    a["bv0"] = cont(np.broadcast_to(i["L0_attn_bv"], (P, P)))
    w = i["L0_ffn_wqkv"]
    q, kv = w[:P], w[P:]
    nkv = kv.shape[0] // HD // 2
    k, v = (np.repeat(part.reshape(nkv, HD, P), NH // nkv, axis=0).reshape(P, P) for part in (kv[:nkv * HD], kv[nkv * HD:]))
    a["w_attn1"] = cont(np.stack([q.T, k.T, v.T, swap(q, HD).T, swap(k, HD).T, i["L0_ffn_wo"].T], axis=1))
    by_head = lambda w: w.reshape(P, HD, NH).transpose(0, 2, 1).reshape(P, P)
    a["w_attn2"] = cont(np.stack([by_head(i["L1_attn_qw"]), by_head(i["L1_attn_kw"]), by_head(i["L1_attn_vw"]),
                                  by_head(i["L1_attn_ow"].T).T], axis=1))
    a["gate_w"] = cont(i["L0_ffn_gate_w"].T)
    a["w13"] = cont(i["L0_ffn_w13"].transpose(2, 0, 1))
    a["w2"] = cont(i["L0_ffn_w2"].reshape(NE, P, 2, P).transpose(3, 0, 2, 1))
    w = i["L1_ffn_wqkv"]
    cols = lambda n: w[:, :, n * INNER:(n + 1) * INNER]
    swap_cols = lambda w: w.reshape(2, P, LH, 2, LD // 2)[:, :, :, ::-1].reshape(2, P, INNER)
    four = np.stack([cols(0), swap_cols(cols(0)), cols(1), swap_cols(cols(1))], axis=2)
    a["w_in"] = cont(four.reshape(2, P, 4, NPAIR, P).transpose(1, 0, 2, 3, 4))
    a["w_v"] = cont(cols(2).transpose(1, 0, 2))
    a["w_out"] = cont(i["L1_ffn_wo"].reshape(2, NPAIR, P, P).transpose(2, 0, 1, 3))
    parts = -(-HID // P)
    a["w_up"] = cont(i["L1_ffn_w1"].transpose(1, 0, 2))
    padded = lambda x: np.concatenate([x, np.zeros((*x.shape[:-2], parts * P - HID, x.shape[-1]), x.dtype)], axis=-2)
    a["b_up"] = cont(padded(i["L1_ffn_b1"].reshape(2, 2, HID, 1)).reshape(2, 2, parts, P).transpose(3, 0, 1, 2))
    a["w_down"] = cont(padded(i["L1_ffn_w2"]).reshape(2, parts, P, P).transpose(2, 0, 1, 3))
    one = {"gamma": i["L0_attn_gamma"], "beta": i["L0_attn_beta"], "bq": i["L0_attn_bq"], "bk": i["L0_attn_bk"],
           "ln1": i["L0_ffn_ln1_w"], "ln2": i["L0_ffn_ln2_w"]}
    for l in range(2):
        for n, s in enumerate((i["L1_ffn_q_scale"][l], i["L1_ffn_k_scale"][l])):
            one[f"scale{l}{2 * n}"] = np.tile(s, 2)
            one[f"scale{l}{2 * n + 1}"] = np.tile(s.reshape(2, -1)[::-1].reshape(-1), 2)
        one[f"lg{l}"], one[f"lb{l}"], one[f"b2{l}"] = i["L1_ffn_ln_g"][l], i["L1_ffn_ln_b"][l], i["L1_ffn_b2"][l]
    a["cols"] = cont(np.stack([one[n] for n in COLS], axis=1))
    return a


def kernel(**inputs):
    import numpy as _np
    import concourse.bacc as _bacc
    from concourse import mybir as _mybir
    from concourse.bass_utils import run_bass_kernel_spmd as _run

    nc = _bacc.Bacc("TRN2", target_bir_lowering=False, num_devices=1)
    arrays = {**layout(_np, {n: _np.asarray(x) for n, x in inputs.items()}), **constants()}
    views = {n: nc.dram_tensor(f"in_{n}", x.shape, _mybir.dt.from_np(x.dtype), kind="ExternalInput").ap()
             for n, x in arrays.items()}
    out = nc.dram_tensor("out_0", (1, S, P), F32, kind="ExternalOutput").ap()
    forward(nc, views, out)
    r = _run(nc, [{f"in_{n}": x for n, x in arrays.items()}], core_ids=[0])
    return r.results[0]["out_0"]
```

```python
from contextlib import ExitStack

import concourse.bass as bass
from concourse import mybir

F32 = mybir.dt.float32
BF16 = mybir.dt.bfloat16
ACT = mybir.ActivationFunctionType
ALU = mybir.AluOpType
AX = mybir.AxisListType

P = 128
S = 2048
NT = S // P
BANK = 512
NC = S // BANK
NH = 16
HD = P // NH
NPIECE = 3
KPROD = NPIECE * NPIECE * HD
MROW = 96
NBUF = 3
LAG = 0
NPROBS = 4
VW = 32
PART = S * NH // P
NE, FF = 8, 256
LH, LD = 8, 64
INNER = LH * LD
NPAIR = LH // 2
WINDOW = 64
KEYS = P + WINDOW
HID = int(P * 4 * 2 / 3)
LN_EPS = 1e-5
NEG = -1e30


def chunk(c):
    return slice(c * BANK, (c + 1) * BANK)


def bank(psum, n, wide=1):
    return psum[:, n * BANK:(n + wide) * BANK]


def load_inputs(nc, psum, x, x_T, ident, loads):
    with ExitStack() as ctx:
        x_tok = ctx.enter_context(nc.sbuf_tensor("x_tok", [P, NT, P], F32))
        turned = [bank(psum, c) for c in range(NC)]
        x_in = ctx.enter_context(nc.semaphore("x_in"))
        loaded = ctx.enter_context(nc.semaphore("loaded"))
        turned_full = ctx.enter_context(nc.semaphore("turned_full"))
        x_done = ctx.enter_context(nc.semaphore("x_done"))
        block = ctx.enter_context(nc.Block())
        here, there = loads[0::2], loads[1::2]

        @block.sync
        def _(sp):
            sp.dma_start(x_tok[:, :, :], x[0].rearrange("(t p) f -> p t f", p=P)).then_inc(x_in, 16)
            sp.dma_start(ident[0], ident[1]).then_inc(x_in, 16)
            for to, source in here:
                sp.dma_start(to, source).then_inc(loaded, 16)
            sp.wait_ge(loaded, 16 * len(loads))

        @block.scalar
        def _(act):
            for to, source in there:
                act.dma_start(to, source).then_inc(loaded, 16)

        @block.tensor
        def _(pe):
            pe.wait_ge(x_in, 32)
            for t in range(NT):
                m = nc.tensor.transpose(turned[t // 4][:, t % 4 * P:(t % 4 + 1) * P], x_tok[:, t, :], ident[0])
                if t % 4 == 3:
                    m.then_inc(turned_full, 1)

        @block.vector
        def _(dve):
            for c in range(NC):
                dve.wait_ge(turned_full, c + 1)
                nc.vector.tensor_copy(x_T[:, chunk(c)], turned[c][:, :]).then_inc(x_done, 1)


def store_output(nc, psum, x_T, out, ident):
    with ExitStack() as ctx:
        x_tok = ctx.enter_context(nc.sbuf_tensor("out_tok", [P, NT, P], F32))
        turned = [bank(psum, c) for c in range(NC)]
        turned_full = ctx.enter_context(nc.semaphore("out_turned_full"))
        tok_done = ctx.enter_context(nc.semaphore("tok_done"))
        stored = ctx.enter_context(nc.semaphore("stored"))
        block = ctx.enter_context(nc.Block())

        @block.tensor
        def _(pe):
            for t in range(NT):
                m = nc.tensor.transpose(turned[t // 4][:, t % 4 * P:(t % 4 + 1) * P], x_T[:, t * P:(t + 1) * P], ident)
                if t % 4 == 3:
                    m.then_inc(turned_full, 1)

        @block.vector
        def _(dve):
            for c in range(NC):
                dve.wait_ge(turned_full, c + 1)
                nc.vector.tensor_copy(x_tok[:, 4 * c:4 * c + 4, :], turned[c][:, :].rearrange("p (t f) -> p t f", f=P)).then_inc(tok_done, 1)

        @block.sync
        def _(sp):
            for c in range(NC):
                sp.wait_ge(tok_done, c + 1)
                sp.dma_start(out[0, c * BANK:(c + 1) * BANK, :].rearrange("(t p) f -> p t f", p=P),
                             x_tok[:, 4 * c:4 * c + 4, :]).then_inc(stored, 16)
            sp.wait_ge(stored, 16 * NC)


def modulation(nc, psum, layers, mod, gamma, beta, gated):
    NL = len(layers)
    with ExitStack() as ctx:
        c_silu = ctx.enter_context(nc.sbuf_tensor("c_silu", [P, NL], F32))
        sign = ctx.enter_context(nc.sbuf_tensor("gate_sign", [P, NL, 2], F32))
        size = ctx.enter_context(nc.sbuf_tensor("gate_size", [P, NL, 2], F32))
        mod_ps = bank(psum, 0)[:, 0:6 * NL].rearrange("p (l i n) -> p l i n", l=NL, i=2)
        silu_done = ctx.enter_context(nc.semaphore("silu_done"))
        mod_full = ctx.enter_context(nc.semaphore("mod_full"))
        mod_step = ctx.enter_context(nc.semaphore("mod_step"))
        block = ctx.enter_context(nc.Block())

        @block.scalar
        def _(act):
            for l, (c, _) in enumerate(layers):
                nc.scalar.activation(c_silu[:, l:l + 1], c, ACT.Silu).then_inc(silu_done, 1)

        @block.tensor
        def _(pe):
            for l, (_, wmod) in enumerate(layers):
                pe.wait_ge(silu_done, l + 1)
                for n in range(6):
                    m = nc.tensor.matmul(mod_ps[:, l, n // 3, n % 3:n % 3 + 1], wmod[:, n * P:(n + 1) * P],
                                         c_silu[:, l:l + 1], start=True, stop=True)
            m.then_inc(mod_full, 1)

        @block.vector
        def _(dve):
            dve.wait_ge(mod_full, 1)
            nc.vector.tensor_copy(mod[:, :, :, 0], mod_ps[:, :, :, 0])
            nc.vector.tensor_scalar(mod[:, :, :, 1], mod_ps[:, :, :, 1], 1.0, None, ALU.add)
            nc.vector.tensor_scalar(sign[:, :, :], mod_ps[:, :, :, 2], 0.0, 2.0, ALU.is_ge, ALU.mult).then_inc(mod_step, 1)
            nc.vector.tensor_scalar(size[:, :, :], mod_ps[:, :, :, 2], -1.0, 0.25, ALU.mult, ALU.max).then_inc(mod_step, 1)
            dve.wait_ge(mod_step, 2)
            nc.vector.tensor_tensor(size[:, :, :], size[:, :, :], mod_ps[:, :, :, 2], ALU.max).then_inc(mod_step, 1)
            dve.wait_ge(mod_step, 3)
            nc.vector.scalar_tensor_tensor(mod[:, :, :, 2], sign[:, :, :], -1.0, size[:, :, :], ALU.add, ALU.mult).then_inc(mod_step, 1)
            dve.wait_ge(mod_step, 4)
            nc.vector.tensor_tensor(gated[:, 0:1], gamma, mod[:, 0, 0, 2:3], ALU.mult)
            nc.vector.tensor_tensor(gated[:, 1:2], beta, mod[:, 0, 0, 2:3], ALU.mult)


def norm(nc, psum, name, src_T, out_T, averages, eps, scale, shift=None, add_to=None):
    centred = shift is not None
    centring, mean_rows, first_rows = averages[:, 0:P], averages[:, P:P + 32], averages[:, 2 * P:3 * P]
    with ExitStack() as ctx:
        sb = lambda n, s: ctx.enter_context(nc.sbuf_tensor(f"{name}_{n}", s, F32))
        square, scaled = sb("square", [P, S]), sb("scaled", [P, S])
        centre = sb("centre", [P, S]) if centred else src_T
        std, inv, eps_col = sb("std", [P, BANK]), sb("inv", [P, BANK]), sb("eps", [P, 1])
        less_mean = [bank(psum, c) for c in range(NC)]
        var, spread = bank(psum, NC), [bank(psum, NC + c) for c in range(NC)]
        sem = lambda n: ctx.enter_context(nc.semaphore(f"{name}_{n}"))
        eps_set = sem("eps_set")
        mean_off = sem("mean_off")
        square_done = sem("square_done")
        centre_done = sem("centre_done")
        var_full = sem("var_full")
        std_done = sem("std_done")
        inv_done = sem("inv_done")
        spread_full = sem("spread_full")
        scaled_done = sem("scaled_done")
        block = ctx.enter_context(nc.Block())

        @block.tensor
        def _(pe):
            if centred:
                for c in range(NC):
                    nc.tensor.matmul(less_mean[c], centring, src_T[:, chunk(c)], start=True, stop=True).then_inc(mean_off, 1)
            pe.wait_ge(square_done, NC)
            for c in range(NC):
                last = nc.tensor.matmul(var[32 * c:32 * c + 32, :], mean_rows, square[:, chunk(c)], start=True, stop=True)
            last.then_inc(var_full, 1)
            pe.wait_ge(inv_done, 1)
            for c in range(NC):
                rows = slice(32 * c, 32 * c + 32)
                nc.tensor.matmul(spread[c], first_rows[rows, :], inv[rows, :], start=True, stop=True).then_inc(spread_full, 1)

        @block.scalar
        def _(act):
            for c in range(NC):
                if centred:
                    act.wait_ge(mean_off, c + 1)
                nc.scalar.activation(square[:, chunk(c)], less_mean[c] if centred else src_T[:, chunk(c)], ACT.Square).then_inc(square_done, 1)
            act.wait_ge(eps_set, 1)
            act.wait_ge(var_full, 1)
            nc.scalar.activation(std[:, :], var, ACT.Sqrt, bias=eps_col[:, :]).then_inc(std_done, 1)
            if centred and add_to is None:
                for c in range(NC):
                    act.wait_ge(scaled_done, c + 1)
                    nc.scalar.activation(out_T[:, chunk(c)], scaled[:, chunk(c)], ACT.Identity, bias=shift)

        @block.vector
        def _(dve):
            nc.vector.memset(eps_col[:, :], eps).then_inc(eps_set, 1)
            if centred:
                for c in range(NC):
                    dve.wait_ge(square_done, c + 1)
                    nc.vector.tensor_copy(centre[:, chunk(c)], less_mean[c]).then_inc(centre_done, 1)
            dve.wait_ge(std_done, 1)
            nc.vector.reciprocal(inv[:, :], std[:, :]).then_inc(inv_done, 1)
            if centred:
                dve.wait_ge(centre_done, NC)
            for c in range(NC):
                dve.wait_ge(spread_full, c + 1)
                to = (scaled if centred else out_T)[:, chunk(c)]
                nc.vector.scalar_tensor_tensor(to, centre[:, chunk(c)], scale, spread[c], ALU.mult, ALU.mult).then_inc(scaled_done, 1)
                if add_to is not None:
                    dve.wait_ge(scaled_done, c + 1)
                    nc.vector.scalar_tensor_tensor(add_to[:, chunk(c)], to, shift, add_to[:, chunk(c)], ALU.add, ALU.add)


def project(nc, psum, name, h_T, wq, wk, wv, q_dram, k_dram, v_tok, bias=None, rope=None):
    NB = 3
    with ExitStack() as ctx:
        raw = [[bank(psum, 2 * b + n) for n in range(2)] for b in range(2)]
        v_ps = [bank(psum, 4 + b) for b in range(2)]
        sb = lambda n: ctx.enter_context(nc.sbuf_tensor(f"{name}_{n}", [P, NB, BANK], F32))
        full, rest, turn = sb("full"), sb("rest"), sb("turn")
        piece = ctx.enter_context(nc.sbuf_tensor(f"{name}_piece", [P, NB, NPIECE, BANK], BF16))
        sem = lambda n: ctx.enter_context(nc.semaphore(f"{name}_{n}"))
        raw_full = sem("raw_full")
        raw_free = sem("raw_free")
        full_done = sem("full_done")
        turn_done = sem("turn_done")
        piece1 = sem("piece1")
        rest_done = sem("rest_done")
        piece2 = sem("piece2")
        piece3 = sem("piece3")
        v_full = sem("v_full")
        v_free = sem("v_free")
        stored = [sem(f"stored{b}") for b in range(NB)]
        block = ctx.enter_context(nc.Block())
        work = [(c, i) for c in range(NC) for i in range(2)]

        @block.tensor
        def _(pe):
            for n, (c, i) in enumerate(work):
                if n >= 2:
                    pe.wait_ge(raw_free, n - 1)
                m = nc.tensor.matmul(raw[n % 2][0][:, :], (wq, wk)[i], h_T[:, chunk(c)], start=True, stop=True)
                if rope:
                    m = nc.tensor.matmul(raw[n % 2][1][:, :], rope[i], h_T[:, chunk(c)], start=True, stop=True)
                m.then_inc(raw_full, 1)
            for t in range(NT):
                if t % 4 == 0 and t >= 8:
                    pe.wait_ge(v_free, t // 4 - 1)
                m = nc.tensor.matmul(v_ps[t // 4 % 2][:, t % 4 * P:(t % 4 + 1) * P], h_T[:, t * P:(t + 1) * P], wv, start=True, stop=True)
                if t % 4 == 3:
                    m.then_inc(v_full, 1)

        @block.vector
        def _(dve):
            def first_rest(n):
                dve.wait_ge(full_done if rope else raw_free, n + 1)
                dve.wait_ge(piece1, n + 1)
                if n >= NB:
                    dve.wait_ge(piece3, n - NB + 1)
                nc.vector.tensor_tensor(rest[:, n % NB, :], full[:, n % NB, :], piece[:, n % NB, 0, :], ALU.subtract).then_inc(rest_done, 1)

            for n, (c, i) in enumerate(work):
                to, ps = full[:, n % NB, :], raw[n % 2]
                dve.wait_ge(raw_full, n + 1)
                if n >= NB:
                    dve.wait_ge(rest_done, n - NB + 1)
                if rope:
                    nc.vector.tensor_tensor(to, ps[0][:, :], rope[2][:, chunk(c)], ALU.mult).then_inc(turn_done, 1)
                    nc.vector.tensor_tensor(turn[:, n % NB, :], ps[1][:, :], rope[3][:, chunk(c)], ALU.mult).then_inc(raw_free, 1)
                    dve.wait_ge(turn_done, n + 1)
                    dve.wait_ge(raw_free, n + 1)
                    nc.vector.tensor_tensor(to, to, turn[:, n % NB, :], ALU.add).then_inc(full_done, 1)
                elif bias:
                    nc.vector.tensor_scalar(to, ps[0][:, :], bias[i], None, ALU.add).then_inc(raw_free, 1)
                else:
                    nc.vector.tensor_copy(to, ps[0][:, :]).then_inc(raw_free, 1)
                if n >= 1:
                    first_rest(n - 1)
            first_rest(len(work) - 1)
            for c in range(NC):
                dve.wait_ge(v_full, c + 1)
                to, ps = v_tok[:, 4 * c:4 * c + 4, :], v_ps[c % 2][:, :].rearrange("p (t f) -> p t f", f=P)
                if bias:
                    nc.vector.tensor_tensor(to, ps, bias[2][:, :].unsqueeze(1).to_broadcast([P, 4, P]), ALU.add).then_inc(v_free, 1)
                else:
                    nc.vector.tensor_copy(to, ps).then_inc(v_free, 1)

        @block.scalar
        def _(act):
            def second(n):
                act.wait_ge(rest_done, n + 1)
                nc.scalar.activation(piece[:, n % NB, 1, :], rest[:, n % NB, :], ACT.Copy).then_inc(piece2, 1)

            for n in range(len(work)):
                act.wait_ge(full_done if rope else raw_free, n + 1)
                if n >= NB:
                    act.wait_ge(stored[n % NB], 16 * (n // NB))
                nc.scalar.activation(piece[:, n % NB, 0, :], full[:, n % NB, :], ACT.Copy).then_inc(piece1, 1)
                if n >= 1:
                    second(n - 1)
            second(len(work) - 1)

        @block.gpsimd
        def _(pool):
            for n in range(len(work)):
                pool.wait_ge(piece2, n + 1)
                nc.gpsimd.tensor_tensor(piece[:, n % NB, 2, :], rest[:, n % NB, :], piece[:, n % NB, 1, :], ALU.subtract).then_inc(piece3, 1)

        @block.sync
        def _(sp):
            for n, (c, i) in enumerate(work):
                sp.wait_ge(piece3, n + 1)
                sp.dma_start((q_dram, k_dram)[i][:, :, chunk(c)].rearrange("n p s -> p n s"),
                             piece[:, n % NB, :, :]).then_inc(stored[n % NB], 16)
            for b in range(NB):
                sp.wait_ge(stored[b], 16 * len(work[b::NB]))


def divide_by_sums(nc, psum, name, z_T, den, den_rows, x_T, ident, wo=None, gate=None):
    with ExitStack() as ctx:
        front = [bank(psum, c) for c in range(NC)]
        back = [bank(psum, NC + c) for c in range(NC)]
        inv = ctx.enter_context(nc.sbuf_tensor(f"{name}_inv", [P, PART], F32))
        regrouped = ctx.enter_context(nc.sbuf_tensor(f"{name}_regrouped", [P, NH, P], F32)) if wo is None else None
        sem = lambda n: ctx.enter_context(nc.semaphore(f"{name}_{n}"))
        inv_done = sem("inv_done")
        den_full = sem("den_full")
        z_done = sem("z_done")
        turned_full = sem("turned_full")
        regroup_done = sem("regroup_done")
        out_full = sem("out_full")
        block = ctx.enter_context(nc.Block())

        @block.tensor
        def _(pe):
            pe.wait_ge(inv_done, 1)
            for part in range(S // PART):
                c, at = divmod(part * PART, BANK)
                last = nc.tensor.matmul(front[c][:, at:at + PART], den_rows[:, part, :], inv[:, :], start=True, stop=True, skip_group_check=True)
                if at + PART == BANK:
                    last.then_inc(den_full, 1)
            if wo is not None:
                for c in range(NC):
                    pe.wait_ge(z_done, c + 1)
                    nc.tensor.matmul(back[c], wo, z_T[:, chunk(c)], start=True, stop=True).then_inc(out_full, 1)
            else:
                pe.wait_ge(z_done, NC)
                spread = z_T.rearrange("p (r g) -> p g r", g=NH)
                for g in range(NH):
                    last = nc.tensor.transpose(back[g // 4][:, g % 4 * P:(g % 4 + 1) * P], spread[:, g, :], ident)
                    if g % 4 == 3:
                        last.then_inc(turned_full, 1)
                pe.wait_ge(regroup_done, NC)
                for h in range(NH):
                    last = nc.tensor.transpose(front[h // 4][:, h % 4 * P:(h % 4 + 1) * P], regrouped[:, h, :], ident)
                    if h % 4 == 3:
                        last.then_inc(out_full, 1)

        @block.vector
        def _(dve):
            nc.vector.reciprocal(inv[:, :], den).then_inc(inv_done, 1)
            for c in range(NC):
                dve.wait_ge(den_full, c + 1)
                nc.vector.tensor_tensor(z_T[:, chunk(c)], z_T[:, chunk(c)], front[c], ALU.mult).then_inc(z_done, 1)
            if wo is None:
                for n in range(NC):
                    dve.wait_ge(turned_full, n + 1)
                    nc.vector.tensor_copy(regrouped[:, :, :].rearrange("r h (g d) -> r g h d", d=HD)[:, 4 * n:4 * n + 4],
                                          back[n].rearrange("r (g h d) -> r g h d", g=4, d=HD)).then_inc(regroup_done, 1)
            for c in range(NC):
                dve.wait_ge(out_full, c + 1)
                if wo is not None:
                    nc.vector.scalar_tensor_tensor(x_T[:, chunk(c)], back[c], gate, x_T[:, chunk(c)], ALU.mult, ALU.add)
                else:
                    nc.vector.tensor_tensor(z_T[:, chunk(c)], x_T[:, chunk(c)], front[c], ALU.add)


def attention(nc, psum, name, causal, scale, q_dram, k_dram, v_tok, z_dram, z_T, den, ident_bf, mask_qk, mask_kq, keep_kq=None):
    with ExitStack() as ctx:
        sb = lambda n, s, d=F32: ctx.enter_context(nc.sbuf_tensor(f"{name}_{n}", s, d))
        sem = lambda n: ctx.enter_context(nc.semaphore(f"{name}_{n}"))
        q_stack = [sb(f"q_stack{b}", [P, S], BF16) for b in range(NBUF)]
        k_stack = [sb(f"k_stack{b}", [P, S], BF16) for b in range(NBUF)]
        probs = [sb(f"probs{b}", [P, S]) for b in range(NPROBS)]
        diag = sb("diag", [P, P])
        v_one = sb("v_one", [P, NT, VW])
        v_only = sb("v_only", [P, NT, VW])
        one_only = sb("one_only", [P, VW])
        part_max = sb("part_max", [P, NT, 4])
        neg_max = sb("neg_max", [P, NT])
        rest1 = sb("rest1", [P, NT])
        rest2 = sb("rest2", [P, NT])
        max_rows = sb("max_rows", [P, NT, 32], BF16)
        zero = sb("zero", [P, 4])
        z_sb = sb("z_sb", [P, BANK])
        st = [bank(psum, 2 * b, 2) for b in range(2)]
        mx = [bank(psum, 4 + b) for b in range(3)]
        z_ps = bank(psum, 7)

        stack_in = [sem(f"stack_in{b}") for b in range(NBUF)]
        zeros_set = sem("zeros_set")
        rest_set = sem("rest_set")
        buffers_set = sem("buffers_set")
        v_in = sem("v_in")
        mx_full = sem("mx_full")
        mx_free = sem("mx_free")
        max_ready = sem("max_ready")
        max_split = sem("max_split")
        pool_step = sem("pool_step")
        st_full = sem("st_full")
        st_free = sem("st_free")
        pv_done = sem("pv_done")
        diag_done = sem("diag_done")
        z_free = sem("z_free")
        z_in = sem("z_in")
        z_out = sem("z_out")

        ahead_of_exp = 2 if causal else 1
        behind_exp = 3 if causal else 1
        order = [NT - 1 - u if causal else u for u in range(NT)]
        mx_tiles = [(qt // 4 + 1) if causal else 4 for qt in order]
        mx_before = [sum(mx_tiles[:u]) for u in range(NT)]
        MX = sum(mx_tiles)
        group = [order[4 * j] // 4 for j in range(4)]
        halves = [[hf for hf in range(2) if not causal or kb * P < (hf + 1) * 1024] for kb in range(NT)]

        def rows_at(kb):
            return kb + ahead_of_exp >= 4 and (kb + ahead_of_exp) % 4 == LAG

        def ring_of(with_next):
            ring = []
            for kb in range(NT):
                ring += [("exp", kb, hf) for hf in halves[kb]]
                if with_next and rows_at(kb):
                    ring.append(("max", (kb + ahead_of_exp) // 4 - 1, 0))
            return ring

        rings = {w: ring_of(w) for w in (True, False)}
        places = {w: {r: n for n, r in enumerate(rings[w])} for w in rings}
        E = len(rings[True])
        assert E % 2 == 0 and LAG < ahead_of_exp < 4
        STACK = 16 * 2 * NPIECE
        ZOUT = 16 * 4
        G = 4

        def width(qt, c):
            end = (qt + 1) * P if causal else S
            return min(BANK, end - c * BANK)

        block = ctx.enter_context(nc.Block())

        @block.sync
        def _(sp):
            def load(h, b):
                q_rows, k_rows = (dram[:, bass.ds(h * HD, HD), :] for dram in (q_dram, k_dram))
                for i in range(NPIECE):
                    rows = slice(i * NPIECE * HD, (i + 1) * NPIECE * HD)
                    sp.dma_start(q_stack[b][rows, :], q_rows[i].unsqueeze(0).to_broadcast([NPIECE, HD, S])).then_inc(stack_in[b], 16)
                    sp.dma_start(k_stack[b][rows, :], k_rows).then_inc(stack_in[b], 16)

            def body(h, b, load_more):
                sp.wait_ge(pv_done, (h + 1) * NT)
                if load_more:
                    load(h + NBUF, b)
                sp.wait_ge(z_free, h + 1)
                tiles = lambda rows: rows.rearrange("r (c j i) -> r c j i", j=4, i=P)
                for j in range(4):
                    sp.dma_start(tiles(z_dram[bass.ds(h * (HD + 1), HD + 1), :])[:, :, j, :],
                                 z_sb[32 * j:32 * j + HD + 1, :].rearrange("r (c i) -> r c i", i=P)).then_inc(z_out, 16)

            for b in range(NBUF):
                if b == 0:
                    sp.wait_ge(zeros_set, 2)
                else:
                    sp.wait_ge(rest_set, 3 * b - 1)
                load(b, b)
            with sp.Fori(0, (NH - 1) // NBUF - 1) as i:
                for r in range(NBUF):
                    body(i * NBUF + r, r, True)
            body(NH - 4, 0, True)
            for h in range(NH - 3, NH):
                body(h, h % NBUF, False)
            sp.wait_ge(z_out, ZOUT * NH)
            of_heads = z_dram.rearrange("(h r) s -> h r s", r=HD + 1)
            for n in range(4):
                some = slice(n * NH // 4, (n + 1) * NH // 4)
                sp.dma_start(z_T[n * P // 4:(n + 1) * P // 4, :], of_heads[some, 0:HD, :]).then_inc(z_in, 16)
            sp.dma_start(den, of_heads[:, HD, :].rearrange("h (a s) -> h a s", s=PART)).then_inc(z_in, 16)
            sp.wait_ge(z_in, 16 * 5)


        @block.gpsimd
        def _(pool):
            def values(h):
                src = v_tok[:, :, bass.ds(h * HD, HD)]
                nc.gpsimd.tensor_copy(v_one[:, :, 0:HD], src)
                nc.gpsimd.tensor_copy(v_only[:, :, 0:HD], src).then_inc(v_in, 1)

            for b in range(1, NBUF):
                nc.gpsimd.memset(q_stack[b][64:128, :], 0.0).then_inc(rest_set, 1)
                pool.wait_ge(rest_set, 3 * b - 2)
                nc.gpsimd.memset(k_stack[b][64:128, :], 0.0).then_inc(rest_set, 1)
                pool.wait_ge(rest_set, 3 * b - 1)
                nc.gpsimd.memset(k_stack[b][MROW:MROW + NPIECE, :], 1.0).then_inc(rest_set, 1)
                pool.wait_ge(rest_set, 3 * b)
            pool.wait_ge(buffers_set, 2)

            def split(h, j):
                n = slice(4 * group[j], 4 * group[j] + 4)
                base = (h * 4 + j) * 4
                pool.wait_ge(max_ready, h * 4 + j + 1)
                nc.gpsimd.tensor_tensor(max_rows[:, n, 0], neg_max[:, n], zero[:, 0:4], ALU.add).then_inc(pool_step, 1)
                pool.wait_ge(pool_step, base + 1)
                nc.gpsimd.tensor_tensor(rest1[:, n], neg_max[:, n], max_rows[:, n, 0], ALU.subtract).then_inc(pool_step, 1)
                pool.wait_ge(pool_step, base + 2)
                nc.gpsimd.tensor_tensor(max_rows[:, n, 1], rest1[:, n], zero[:, 0:4], ALU.add).then_inc(pool_step, 1)
                pool.wait_ge(pool_step, base + 3)
                nc.gpsimd.tensor_tensor(rest2[:, n], rest1[:, n], max_rows[:, n, 1], ALU.subtract).then_inc(pool_step, 1)
                pool.wait_ge(pool_step, base + 4)
                nc.gpsimd.tensor_tensor(max_rows[:, n, 2], rest2[:, n], zero[:, 0:4], ALU.add).then_inc(max_split, 1)

            def body(h, with_next):
                for kb in range(NT):
                    if not causal:
                        pool.wait_ge(st_free, G + h * E + places[with_next][("exp", kb, kb // 8)] + 1)
                        if kb > 0:
                            pool.wait_ge(pv_done, h * NT + kb)
                        nc.gpsimd.tensor_tensor(diag[:, :], probs[kb % NPROBS][:, kb * P:kb * P + P], keep_kq,
                                                ALU.mult).then_inc(diag_done, 1)
                    if with_next and kb + ahead_of_exp < NT and (kb + ahead_of_exp) % 4 == 3:
                        split(h + 1, (kb + ahead_of_exp) // 4)
                if with_next:
                    pool.wait_ge(pv_done, h * NT + NT)
                    pool.wait_ge(buffers_set, 2)
                    values(h + 1)

            values(0)
            for j in range(4):
                split(0, j)
            with pool.Fori(0, NH - 1) as h:
                body(h, True)
            body(NH - 1, False)

        @block.vector
        def _(dve):
            nc.vector.memset(q_stack[0][64:128, :], 0.0).then_inc(zeros_set, 1)
            nc.vector.memset(k_stack[0][64:128, :], 0.0).then_inc(zeros_set, 1)
            dve.wait_ge(zeros_set, 2)
            nc.vector.memset(k_stack[0][MROW:MROW + NPIECE, :], 1.0).then_inc(zeros_set, 1)
            nc.vector.memset(zero[:, :], 0.0)
            nc.vector.memset(max_rows[:, :, :], 0.0)
            nc.vector.memset(v_one[:, :, :], 0.0)
            nc.vector.memset(v_only[:, :, :], 0.0)
            nc.vector.memset(one_only[:, :], 0.0).then_inc(buffers_set, 1)
            dve.wait_ge(buffers_set, 1)
            nc.vector.memset(v_one[:, :, HD:HD + 1], 1.0)
            nc.vector.memset(one_only[:, HD:HD + 1], 1.0).then_inc(buffers_set, 1)

            def maxima(h, r):
                for u, qt in enumerate(order):
                    for c in range(mx_tiles[u]):
                        n = mx_before[u] + c
                        dve.wait_ge(mx_full, h * MX + n + 1)
                        nc.vector.tensor_reduce(part_max[:, qt, c:c + 1], mx[(r * MX + n) % 3][:, 0:width(qt, c)],
                                                AX.X, ALU.max).then_inc(mx_free, 1)
                    if u % 4 == 3:
                        g = qt // 4
                        dve.wait_ge(mx_free, h * MX + n + 1)
                        nc.vector.tensor_reduce(neg_max[:, 4 * g:4 * g + 4], part_max[:, 4 * g:4 * g + 4, 0:mx_tiles[u]],
                                                AX.X, ALU.max, negate=True).then_inc(max_ready, 1)

            maxima(0, 0)
            with dve.Fori(0, (NH - 1) // NBUF) as i:
                for r in range(NBUF):
                    maxima(i * NBUF + 1 + r, 1 + r)

        @block.scalar
        def _(act):
            def body(h, b, with_next):
                for e, (kind, kb, hf) in enumerate(rings[with_next]):
                    n = G + h * E + e
                    slot = (G + e) % 2
                    if kind == "exp":
                        lo = max(kb * P, hf * 1024) if causal else hf * 1024
                        hi = (hf + 1) * 1024
                        act.wait_ge(st_full, n + 1)
                        if hf == halves[kb][0] and not (kb < NPROBS and isinstance(h, int) and h == 0):
                            act.wait_ge(pv_done, h * NT + kb - NPROBS + 1)
                        nc.scalar.activation(probs[kb % NPROBS][:, lo:hi], st[slot][:, lo - hf * 1024:1024], ACT.Exp,
                                             scale=scale).then_inc(st_free, 1)
                    else:
                        act.wait_ge(st_full, n + 1)
                        g = group[kb]
                        nc.scalar.activation(q_stack[(b + 1) % NBUF][MROW:P, 4 * g * P:4 * (g + 1) * P],
                                             st[slot][MROW:P, 0:BANK // 2].bitcast(BF16), ACT.Copy).then_inc(st_free, 1)
                act.wait_ge(pv_done, (h + 1) * NT)
                if not (isinstance(h, int) and h == 0):
                    act.wait_ge(z_out, h * ZOUT)
                nc.scalar.activation(z_sb[:, :], z_ps[:, :], ACT.Copy).then_inc(z_free, 1)

            for j in range(4):
                g = group[j]
                act.wait_ge(st_full, j + 1)
                nc.scalar.activation(q_stack[0][MROW:P, 4 * g * P:4 * (g + 1) * P],
                                     st[j % 2][MROW:P, 0:BANK // 2].bitcast(BF16), ACT.Copy).then_inc(st_free, 1)
            body(0, 0, True)
            with act.Fori(0, NH // NBUF - 1) as i:
                for r in range(NBUF):
                    body(i * NBUF + 1 + r, (1 + r) % NBUF, True)
            for h in range(NH - 3, NH):
                body(h, h % NBUF, h < NH - 1)

        @block.tensor
        def _(pe):
            def max_tiles(h, r, u, some):
                qt, b = order[u], r % NBUF
                for c in some:
                    if c >= mx_tiles[u]:
                        continue
                    n, w = mx_before[u] + c, width(qt, c)
                    diagonal = causal and c == qt // 4
                    if not (isinstance(h, int) and h * MX + n < 3):
                        pe.wait_ge(mx_free, h * MX + n - 2)
                    tile = mx[(r * MX + n) % 3]
                    m = nc.tensor.matmul(tile[:, 0:w], q_stack[b][0:KPROD, qt * P:(qt + 1) * P],
                                         k_stack[b][0:KPROD, c * BANK:c * BANK + w], start=True, stop=not diagonal,
                                         skip_group_check=True)
                    if diagonal:
                        m = nc.tensor.matmul(tile[:, w - P:w], ident_bf, mask_qk, start=False, stop=True,
                                             skip_group_check=True)
                    m.then_inc(mx_full, 1)

            def max_transpose(h, j, n, slot):
                pe.wait_ge(max_split, h * 4 + j + 1)
                if not (isinstance(n, int) and n < 2):
                    pe.wait_ge(st_free, n - 1)
                out = st[slot][MROW:P, 0:BANK // 2].bitcast(BF16)
                for t in range(4):
                    m = nc.tensor.transpose(out[:, t * P:(t + 1) * P], max_rows[:, 4 * group[j] + t, :], ident_bf)
                m.then_inc(st_full, 1)

            def scores(h, b, kb, hf, with_next):
                e = places[with_next][("exp", kb, hf)]
                n = G + h * E + e
                slot = (G + e) % 2
                pe.wait_ge(st_free, n - 1)
                lo = max(kb * P, hf * 1024) if causal else hf * 1024
                for c in range(2):
                    a, z = max(lo, hf * 1024 + c * BANK), hf * 1024 + (c + 1) * BANK
                    if a >= z:
                        continue
                    diagonal = causal and a == kb * P
                    m = nc.tensor.matmul(st[slot][:, a - hf * 1024:z - hf * 1024], k_stack[b][:, kb * P:(kb + 1) * P],
                                         q_stack[b][:, a:z], start=True, stop=not diagonal, skip_group_check=True)
                    if diagonal:
                        m = nc.tensor.matmul(st[slot][:, a - hf * 1024:a - hf * 1024 + P], ident_bf, mask_kq,
                                             start=False, stop=True, skip_group_check=True)
                m.then_inc(st_full, 1)

            def products(h, kb, with_next):
                pe.wait_ge(st_free, G + h * E + places[with_next][("exp", kb, halves[kb][-1])] + 1)
                if kb == 0:
                    pe.wait_ge(v_in, h + 1)
                    if not (isinstance(h, int) and h == 0):
                        pe.wait_ge(z_free, h)
                pr = probs[kb % NPROBS][:, :].rearrange("p (c j i) -> p c j i", j=4, i=P)
                done = []

                def part(j, c0, c1, weights, start):
                    if c0 < c1:
                        done.append(nc.tensor.matmul(z_ps[32 * j:32 * j + VW, c0 * P:c1 * P], weights,
                                                     pr[:, c0:c1, j, :], start=start, stop=kb == NT - 1,
                                                     skip_group_check=True))

                mid = [max(0, -(-(kb - j) // 4)) for j in range(4)]
                for j in range(4):
                    part(j, mid[j], 4, v_one[:, kb, :] if causal else one_only[:, :], kb == 0)
                if not causal:
                    for j in range(4):
                        part(j, 0, mid[j], v_one[:, kb, :], False)
                    pe.wait_ge(diag_done, h * NT + kb + 1)
                    j, c = kb % 4, kb // 4
                    done.append(nc.tensor.matmul(z_ps[32 * j:32 * j + VW, c * P:(c + 1) * P], v_only[:, kb, :],
                                                 diag[:, :], start=False, stop=kb == NT - 1, skip_group_check=True))
                done[-1].then_inc(pv_done, 1)

            def body(h, r, loads, next1=True, next2=True):
                b = r % NBUF
                for kb in range(NT):
                    ahead, u = divmod(kb + ahead_of_exp, NT)
                    go = next2 if ahead else next1
                    if ahead and u == 0 and next2:
                        pe.wait_ge(stack_in[(r + 2) % NBUF], loads * STACK)
                    first, *second = halves[kb]
                    scores(h, b, kb, first, next1)
                    if go:
                        max_tiles(h + 1 + ahead, r + 1 + ahead, u, (0, 1))
                    if kb >= behind_exp:
                        products(h, kb - behind_exp, next1)
                    if second:
                        scores(h, b, kb, second[0], next1)
                    if go:
                        max_tiles(h + 1 + ahead, r + 1 + ahead, u, (2, 3))
                    if next1 and rows_at(kb):
                        j = (kb + ahead_of_exp) // 4 - 1
                        e = places[True][("max", j, 0)]
                        max_transpose(h + 1, j, G + h * E + e, (G + e) % 2)
                for kb in range(NT - behind_exp, NT):
                    products(h, kb, next1)

            pe.wait_ge(stack_in[0], STACK)
            for u in range(NT):
                max_tiles(0, 0, u, range(4))
                if u % 4 == 3:
                    max_transpose(0, u // 4, u // 4, u // 4 % 2)
            pe.wait_ge(stack_in[1], STACK)
            for u in range(ahead_of_exp):
                max_tiles(1, 1, u, range(4))
            pe.wait_ge(buffers_set, 2)
            pe.wait_ge(zeros_set, 3)
            pe.wait_ge(rest_set, 3 * (NBUF - 1))
            pe.wait_ge(st_free, G)
            body(0, 0, 1)
            with pe.Fori(0, NH // NBUF - 1) as i:
                for r in range(NBUF):
                    body(i * NBUF + 1 + r, 1 + r, i + 2)
            for h in range(NH - 3, NH):
                body(h, h % NBUF, (h + 2) // NBUF + 1, h + 1 < NH, h + 2 < NH)

def router(nc, psum, h_T, gate_w, rank, ident, w_rows):
    with ExitStack() as ctx:
        sb = lambda n, d=F32: ctx.enter_context(nc.sbuf_tensor(f"route_{n}", [P, NT, NE], d))
        logits, is_top, order, taken, left = sb("logits"), sb("is_top"), sb("order"), [sb("first"), sb("second")], sb("left")
        share = sb("share")
        col = lambda n: ctx.enter_context(nc.sbuf_tensor(f"route_{n}", [P, NT], F32))
        top, best, gap, odds, total, w1, w2 = [col("top1"), col("top2")], col("best"), col("gap"), col("odds"), col("total"), col("w1"), col("w2")
        pieces = ctx.enter_context(nc.sbuf_tensor("route_pieces", [P, NT, NPIECE, NE], BF16))
        logit_ps = bank(psum, 0)[:, 0:NT * NE].rearrange("p (t e) -> p t e", e=NE)
        row_ps = [bank(psum, 1 + b)[0:NPIECE * NE, :].bitcast(BF16) for b in range(2)]
        logits_full = ctx.enter_context(nc.semaphore("logits_full"))
        rows_clear = ctx.enter_context(nc.semaphore("rows_clear"))
        step = ctx.enter_context(nc.semaphore("route_step"))
        gap_done = ctx.enter_context(nc.semaphore("gap_done"))
        odds_done = ctx.enter_context(nc.semaphore("odds_done"))
        pieces_done = ctx.enter_context(nc.semaphore("pieces_done"))
        rows_full = ctx.enter_context(nc.semaphore("rows_full"))
        wide = lambda a: a[:, :].unsqueeze(2).to_broadcast([P, NT, NE])
        block = ctx.enter_context(nc.Block())

        @block.tensor
        def _(pe):
            for t in range(NT):
                m = nc.tensor.matmul(logit_ps[:, t, :], h_T[:, t * P:(t + 1) * P], gate_w, start=True, stop=True)
            m.then_inc(logits_full, 1)
            pe.wait_ge(pieces_done, 1)
            for t in range(NT):
                m = nc.tensor.transpose(row_ps[t // 8][:, t % 8 * P:(t % 8 + 1) * P],
                                        pieces[:, t, :, :].rearrange("p n e -> p (n e)"), ident)
                if t % 8 == 7:
                    m.then_inc(rows_full, 1)

        @block.scalar
        def _(act):
            act.wait_ge(gap_done, 1)
            nc.scalar.activation(odds[:, :], gap[:, :], ACT.Exp).then_inc(odds_done, 1)

        @block.vector
        def _(dve):
            nc.vector.memset(w_rows[:, :], 0.0).then_inc(rows_clear, 1)
            dve.wait_ge(logits_full, 1)
            nc.vector.tensor_copy(logits[:, :, :], logit_ps[:, :, :]).then_inc(step, 1)
            n = 1
            for r, source in enumerate((logits, left)):
                dve.wait_ge(step, n)
                nc.vector.tensor_reduce(top[r][:, :], source[:, :, :], AX.X, ALU.max).then_inc(step, 1)
                dve.wait_ge(step, n + 1)
                nc.vector.tensor_tensor(is_top[:, :, :], source[:, :, :], wide(top[r]), ALU.is_equal).then_inc(step, 1)
                dve.wait_ge(step, n + 2)
                nc.vector.tensor_tensor(order[:, :, :], is_top[:, :, :], rank.unsqueeze(1).to_broadcast([P, NT, NE]), ALU.mult).then_inc(step, 1)
                dve.wait_ge(step, n + 3)
                nc.vector.tensor_reduce(best[:, :], order[:, :, :], AX.X, ALU.max).then_inc(step, 1)
                dve.wait_ge(step, n + 4)
                nc.vector.tensor_tensor(taken[r][:, :, :], order[:, :, :], wide(best), ALU.is_equal).then_inc(step, 1)
                n += 5
                if r == 0:
                    dve.wait_ge(step, n)
                    nc.vector.scalar_tensor_tensor(left[:, :, :], taken[0][:, :, :], NEG, logits[:, :, :], ALU.mult, ALU.add).then_inc(step, 1)
                    n += 1
            nc.vector.tensor_tensor(gap[:, :], top[1][:, :], top[0][:, :], ALU.subtract).then_inc(gap_done, 1)
            dve.wait_ge(odds_done, 1)
            nc.vector.tensor_scalar(total[:, :], odds[:, :], 1.0, None, ALU.add).then_inc(step, 1)
            dve.wait_ge(step, n + 1)
            nc.vector.reciprocal(w1[:, :], total[:, :]).then_inc(step, 1)
            dve.wait_ge(step, n + 2)
            nc.vector.tensor_tensor(w2[:, :], odds[:, :], w1[:, :], ALU.mult).then_inc(step, 1)
            dve.wait_ge(step, n + 3)
            nc.vector.tensor_tensor(share[:, :, :], taken[0][:, :, :], wide(w1), ALU.mult)
            nc.vector.tensor_tensor(left[:, :, :], taken[1][:, :, :], wide(w2), ALU.mult).then_inc(step, 1)
            dve.wait_ge(step, n + 4)
            nc.vector.tensor_tensor(share[:, :, :], share[:, :, :], left[:, :, :], ALU.add).then_inc(step, 1)
            for i in range(NPIECE):
                dve.wait_ge(step, n + 5 + 2 * i)
                last = nc.vector.tensor_copy(pieces[:, :, i, :], share[:, :, :])
                if i < NPIECE - 1:
                    last.then_inc(step, 1)
                    dve.wait_ge(step, n + 6 + 2 * i)
                    nc.vector.tensor_tensor(share[:, :, :], share[:, :, :], pieces[:, :, i, :], ALU.subtract).then_inc(step, 1)
                else:
                    last.then_inc(pieces_done, 1)
            dve.wait_ge(rows_clear, 1)
            for b in range(2):
                dve.wait_ge(rows_full, b + 1)
                nc.vector.tensor_copy(w_rows[0:NPIECE * NE, b * 2 * BANK:(b + 1) * 2 * BANK], row_ps[b][:, :])


def experts(nc, psum, h_T, w13, w2, w_rows, pick, y_T, x_T, gate):
    with ExitStack() as ctx:
        g_ps, u_ps, w_ps = ([bank(psum, 2 * n + b) for b in range(2)] for n in range(3))
        out_ps = bank(psum, 6)
        sb = lambda n, k: [ctx.enter_context(nc.sbuf_tensor(f"moe_{n}{b}", [P, BANK], F32)) for b in range(k)]
        silu, up, act_w = sb("silu", 2), sb("up", 2), sb("act_w", 4)
        total = sb("total", 1)[0]
        sem = lambda n: ctx.enter_context(nc.semaphore(f"moe_{n}"))
        up_full = sem("up_full")
        w_full = sem("w_full")
        silu_done = sem("silu_done")
        up_done = sem("up_done")
        act_done = sem("act_done")
        down_done = sem("down_done")
        out_free = sem("out_free")
        N = 2 * NE
        block = ctx.enter_context(nc.Block())

        @block.tensor
        def _(pe):
            def down(c, n):
                pe.wait_ge(act_done, c * N + n + 1)
                nc.tensor.matmul(out_ps[:, :], w2[:, n // 2, n % 2, :], act_w[n % 4][:, :], start=n == 0,
                                 stop=n == N - 1).then_inc(down_done, 1)

            def body(c, some_before):
                at = bass.ds(c * BANK, BANK)
                for n in range(N):
                    e, f = divmod(n, 2)
                    if some_before or n >= 2:
                        pe.wait_ge(up_done, c * N + n - 1)
                    if f == 0:
                        if some_before or e >= 2:
                            pe.wait_ge(act_done, c * N + n - 2)
                        nc.tensor.matmul(w_ps[e % 2][:, :], pick[:, e, :], w_rows[:, at], start=True, stop=True).then_inc(w_full, 1)
                    nc.tensor.matmul(g_ps[n % 2][:, :], w13[:, e, f * P:(f + 1) * P], h_T[:, at], start=True, stop=True)
                    nc.tensor.matmul(u_ps[n % 2][:, :], w13[:, e, FF + f * P:FF + (f + 1) * P], h_T[:, at],
                                     start=True, stop=True).then_inc(up_full, 1)
                    if n >= 2:
                        if n == 2 and some_before:
                            pe.wait_ge(out_free, c)
                        down(c, n - 2)
                down(c, N - 2)
                down(c, N - 1)

            body(0, False)
            with pe.Fori(1, NC) as c:
                body(c, True)

        @block.scalar
        def _(act):
            def body(c):
                for n in range(N):
                    act.wait_ge(up_full, c * N + n + 1)
                    nc.scalar.activation(silu[n % 2][:, :], g_ps[n % 2][:, :], ACT.Silu).then_inc(silu_done, 1)

            with act.Fori(0, NC) as c:
                body(c)

        @block.vector
        def _(dve):
            def body(c, some_before):
                at = bass.ds(c * BANK, BANK)
                for n in range(N):
                    dve.wait_ge(silu_done, c * N + n + 1)
                    if some_before or n >= 2:
                        dve.wait_ge(act_done, c * N + n - 1)
                    nc.vector.tensor_tensor(up[n % 2][:, :], silu[n % 2][:, :], u_ps[n % 2][:, :], ALU.mult).then_inc(up_done, 1)
                    dve.wait_ge(up_done, c * N + n + 1)
                    dve.wait_ge(w_full, c * NE + n // 2 + 1)
                    if some_before or n >= 4:
                        dve.wait_ge(down_done, c * N + n - 3)
                    nc.vector.tensor_tensor(act_w[n % 4][:, :], up[n % 2][:, :], w_ps[n // 2 % 2][:, :], ALU.mult).then_inc(act_done, 1)
                dve.wait_ge(down_done, c * N + N)
                nc.vector.tensor_tensor(total[:, :], y_T[:, at], out_ps[:, :], ALU.add).then_inc(out_free, 1)
                dve.wait_ge(out_free, c + 1)
                nc.vector.scalar_tensor_tensor(x_T[:, at], total[:, :], gate, x_T[:, at], ALU.mult, ALU.add)

            body(0, False)
            with dve.Fori(1, NC) as c:
                body(c, True)


def shift_tokens(nc, name, src_T, out_T):
    with ExitStack() as ctx:
        block = ctx.enter_context(nc.Block())

        @block.vector
        def _(dve):
            nc.vector.tensor_copy(out_T[0:P // 2, :], src_T[0:P // 2, :])

        @block.scalar
        def _(act):
            nc.scalar.activation(out_T[P // 2:P, 1:S], src_T[P // 2:P, 0:S - 1], ACT.Copy)

        @block.gpsimd
        def _(pool):
            nc.gpsimd.memset(out_T[P // 2:P, 0:1], 0.0)


def after(engine, semaphore, count):
    if not isinstance(count, int) or count > 0:
        engine.wait_ge(semaphore, count)


def local_project(nc, psum, name, hs_T, w_in, w_v, tables, scales, pair_rows, pair_spread, q_T, k_T, v_tok, q_scale):
    with ExitStack() as ctx:
        sb = lambda n, s: ctx.enter_context(nc.sbuf_tensor(f"{name}_{n}", s, F32))
        sem = lambda n: ctx.enter_context(nc.semaphore(f"{name}_{n}"))
        table = [sb(f"table{i}", [P, 2, BANK]) for i in range(2)]
        straight = [sb(f"straight{b}", [P, BANK]) for b in range(2)]
        swapped = [sb(f"swapped{b}", [P, BANK]) for b in range(2)]
        q_square = [sb(f"q_square{b}", [P, BANK]) for b in range(2)]
        k_square = sb("k_square", [P, NPAIR, BANK])
        k_turned = sb("k_turned", [P, NPAIR, BANK])
        k_std, k_inv = sb("k_std", [P, BANK]), sb("k_inv", [P, BANK])
        q_std, q_inv = sb("q_std", [P, 4, LH]), sb("q_inv", [P, 4, LH])
        raw = [[bank(psum, 2 * b + n) for n in range(2)] for b in range(2)]
        k_sum, v_ps, spread = bank(psum, 4), bank(psum, 6), bank(psum, 7)
        q_sum = bank(psum, 5)[:, 0:4 * LH].rearrange("p (t h) -> p t h", t=4)

        table_in = [sem(f"table_in{i}") for i in range(2)]
        raw_full = sem("raw_full")
        square_done = sem("square_done")
        swapped_done = sem("swapped_done")
        straight_done = sem("straight_done")
        turned = sem("turned")
        k_sum_full = sem("k_sum_full")
        k_std_done = sem("k_std_done")
        k_clipped = sem("k_clipped")
        k_inv_done = sem("k_inv_done")
        q_sum_full = sem("q_sum_full")
        q_std_done = sem("q_std_done")
        q_step = sem("q_step")
        v_full = sem("v_full")
        v_done = sem("v_done")
        spread_full = sem("spread_full")
        k_done = sem("k_done")
        pad_set = sem("pad_set")
        N = 2 * NPAIR
        MIN_NORM = 1e-12
        SCALE = 8.0
        block = ctx.enter_context(nc.Block())

        items = [(c, n) for c in range(NC) for n in range(N)]

        @block.sync
        def _(sp):
            for c in range(NC):
                for i, w in ((0, 2), (1, 0)):
                    if c > 0:
                        sp.wait_ge(straight_done, (c - 1) * N + (i + 1) * NPAIR)
                    sp.dma_start(table[i][:, :, :], tables[:, w:w + 2, chunk(c)]).then_inc(table_in[i], 16)

        @block.tensor
        def _(pe):
            def q_sums(c, m):
                pe.wait_ge(square_done, c * N + NPAIR + m + 1)
                if m == 0 and c > 0:
                    pe.wait_ge(q_std_done, c)
                for t in range(4):
                    last = nc.tensor.matmul(q_sum[:, t, 2 * m:2 * m + 2], q_square[m % 2][:, t * P:(t + 1) * P],
                                            pair_rows[:, 15:17], start=True, stop=True)
                last.then_inc(q_sum_full, 1)

            for g, (c, n) in enumerate(items):
                first = 2 if n < NPAIR else 0
                if g >= 2:
                    pe.wait_ge(straight_done, g - 1)
                for i in range(2):
                    last = nc.tensor.matmul(raw[g % 2][i], w_in[:, first + i, n % NPAIR, :], hs_T[:, chunk(c)], start=True, stop=True)
                last.then_inc(raw_full, 1)
                if n == NPAIR:
                    pe.wait_ge(square_done, c * N + NPAIR)
                    if c > 0:
                        pe.wait_ge(k_std_done, c)
                    for m in range(NPAIR):
                        last = nc.tensor.matmul(k_sum[32 * m:32 * m + 32, :], pair_rows, k_square[:, m, :], start=True, stop=True)
                    last.then_inc(k_sum_full, 1)
                if n > NPAIR:
                    q_sums(c, n - NPAIR - 1)
                if n == N - 1:
                    for t in range(4):
                        if c + t > 0:
                            pe.wait_ge(v_done, c * 4 + t)
                        tokens = slice(c * BANK + t * P, c * BANK + (t + 1) * P)
                        nc.tensor.matmul(v_ps, hs_T[:, tokens], w_v, start=True, stop=True).then_inc(v_full, 1)
                        if t == 0:
                            q_sums(c, NPAIR - 1)
                            pe.wait_ge(k_inv_done, c + 1)
                        if c + t > 0:
                            pe.wait_ge(k_done, c * NPAIR + t)
                        nc.tensor.matmul(spread, pair_spread[32 * t:32 * t + 32, :], k_inv[32 * t:32 * t + 32, :],
                                         start=True, stop=True).then_inc(spread_full, 1)

        @block.scalar
        def _(act):
            for g, (c, n) in enumerate(items):
                m = n % NPAIR
                act.wait_ge(raw_full, g + 1)
                if n == 0 and c > 0:
                    act.wait_ge(k_sum_full, c)
                if n >= NPAIR and c * NPAIR + m >= 2:
                    act.wait_ge(q_sum_full, c * NPAIR + m - 1)
                to = k_square[:, m, :] if n < NPAIR else q_square[m % 2][:, :]
                nc.scalar.activation(to, raw[g % 2][0], ACT.Square).then_inc(square_done, 1)
                if n == NPAIR:
                    act.wait_ge(k_sum_full, c + 1)
                    if c > 0:
                        act.wait_ge(k_clipped, c)
                    nc.scalar.activation(k_std[:, :], k_sum, ACT.Sqrt).then_inc(k_std_done, 1)
                if n == N - 1:
                    for t in range(4):
                        act.wait_ge(v_full, c * 4 + t + 1)
                        nc.scalar.activation(v_tok[:, 1 + 4 * c + t, :], v_ps, ACT.Copy).then_inc(v_done, 1)
                        if t == 0:
                            act.wait_ge(q_sum_full, (c + 1) * NPAIR)
                            if c > 0:
                                act.wait_ge(q_step, c * 3)
                            nc.scalar.activation(q_std[:, :, :], q_sum, ACT.Sqrt).then_inc(q_std_done, 1)

        @block.vector
        def _(dve):
            nc.vector.memset(v_tok[:, 0, :], 0.0)
            nc.vector.memset(k_T[:, :, 0:WINDOW], 0.0).then_inc(pad_set, 1)
            for g, (c, n) in enumerate(items):
                kind = 0 if n < NPAIR else 1
                column = 2 - 2 * kind
                dve.wait_ge(raw_full, g + 1)
                if n % NPAIR == 0:
                    dve.wait_ge(table_in[kind], 16 * (c + 1))
                if g >= 2:
                    dve.wait_ge(turned, g - 1)
                nc.vector.scalar_tensor_tensor(swapped[g % 2][:, :], raw[g % 2][1], scales[column + 1], table[kind][:, 1, :],
                                               ALU.mult, ALU.mult).then_inc(swapped_done, 1)
                dve.wait_ge(square_done, g + 1)
                nc.vector.scalar_tensor_tensor(straight[g % 2][:, :], raw[g % 2][0], scales[column], table[kind][:, 0, :],
                                               ALU.mult, ALU.mult).then_inc(straight_done, 1)
                if n == NPAIR + 1:
                    dve.wait_ge(k_std_done, c + 1)
                    nc.vector.tensor_scalar(k_std[:, :], k_std[:, :], MIN_NORM, None, ALU.max).then_inc(k_clipped, 1)
                    dve.wait_ge(k_clipped, c + 1)
                    nc.vector.reciprocal(k_inv[:, :], k_std[:, :]).then_inc(k_inv_done, 1)
                if n == N - 1:
                    dve.wait_ge(turned, c * N + NPAIR)
                    for m in range(NPAIR):
                        dve.wait_ge(spread_full, c * NPAIR + m + 1)
                        nc.vector.tensor_tensor(k_T[:, m, WINDOW + c * BANK:WINDOW + (c + 1) * BANK], k_turned[:, m, :], spread,
                                                ALU.mult).then_inc(k_done, 1)
                    dve.wait_ge(q_std_done, c + 1)
                    nc.vector.tensor_scalar(q_inv[:, :, :], q_std[:, :, :], MIN_NORM, None, ALU.max).then_inc(q_step, 1)
                    dve.wait_ge(q_step, 3 * c + 1)
                    nc.vector.reciprocal(q_inv[:, :, :], q_inv[:, :, :]).then_inc(q_step, 1)
                    dve.wait_ge(q_step, 3 * c + 2)
                    nc.vector.tensor_scalar(q_scale[:, 4 * c:4 * c + 4, :], q_inv[:, :, :], SCALE, None, ALU.mult).then_inc(q_step, 1)

        @block.gpsimd
        def _(pool):
            for g, (c, n) in enumerate(items):
                m = n % NPAIR
                pool.wait_ge(swapped_done, g + 1)
                pool.wait_ge(straight_done, g + 1)
                if n < NPAIR and c > 0:
                    pool.wait_ge(k_done, (c - 1) * NPAIR + m + 1)
                to = k_turned[:, m, :] if n < NPAIR else q_T[:, 4 * c:4 * c + 4, m, :]
                tiles = lambda a: a if n < NPAIR else a.rearrange("p (t i) -> p t i", t=4)
                nc.gpsimd.tensor_tensor(to, tiles(straight[g % 2][:, :]), tiles(swapped[g % 2][:, :]), ALU.add).then_inc(turned, 1)
            pool.wait_ge(pad_set, 1)


def local_attend(nc, psum, name, q_T, k_T, v_tok, q_scale, w_out, bands, ident, ident_bf, x_T):
    with ExitStack() as ctx:
        sb = lambda n, s, d=F32: ctx.enter_context(nc.sbuf_tensor(f"{name}_{n}", s, d))
        sem = lambda n: ctx.enter_context(nc.semaphore(f"{name}_{n}"))
        q = [sb(f"q{b}", [P, NPAIR, P]) for b in range(2)]
        k = [sb(f"k{b}", [P, NPAIR, KEYS]) for b in range(2)]
        v_own = [sb(f"v_own{b}", [P, INNER]) for b in range(2)]
        v_past = [sb(f"v_past{b}", [P, NPAIR, LD]) for b in range(2)]
        scale = [sb(f"scale{b}", [P, LH]) for b in range(2)]
        neg_max = [sb(f"neg_max{b}", [P, LH]) for b in range(2)]
        bias = [sb(f"bias{b}", [P, LH]) for b in range(2)]
        den = [sb(f"den{b}", [P, LH]) for b in range(2)]
        inv = [sb(f"inv{b}", [P, LH]) for b in range(2)]
        probs = [sb(f"probs{b}", [P, LH, KEYS]) for b in range(2)]
        own_T = [sb(f"own_T{b}", [P, LH, P]) for b in range(2)]
        past_T = [sb(f"past_T{b}", [P, NPAIR, P]) for b in range(2)]
        o_T = sb("o_T", [P, NPAIR, P])
        score = [bank(psum, n) for n in range(4)]
        own_ps, past_ps, o_ps, out_ps = (bank(psum, 4 + n) for n in range(4))

        qk_in = [sem(f"qk_in{b}") for b in range(2)]
        scale_in = sem("scale_in")
        v_in = [sem(f"v_in{b}") for b in range(2)]
        score_full = sem("score_full")
        max_done = sem("max_done")
        bias_done = sem("bias_done")
        exp_done = sem("exp_done")
        inv_done = sem("inv_done")
        share_done = sem("share_done")
        own_full = sem("own_full")
        own_done = sem("own_done")
        past_full = sem("past_full")
        past_done = sem("past_done")
        o_full = sem("o_full")
        o_done = sem("o_done")
        out_full = sem("out_full")
        out_done = sem("out_done")
        heads_of = lambda u: slice(4 * u, 4 * u + 4)
        block = ctx.enter_context(nc.Block())

        def steps(engine, step):
            step(-1, 1, True, False, False)
            step(0, 0, True, True, False)
            with engine.Fori(0, NT // 2 - 1) as i:
                step(2 * i + 1, 1, True, True, True)
                step(2 * i + 2, 0, True, True, True)
            step(NT - 1, 1, False, True, True)
            step(NT, 0, False, False, True)

        @block.sync
        def _(sp):
            def queries_and_keys(t, b):
                after(sp, score_full, (t - 1) * 2)
                sp.dma_start(q[b][:, :, :], q_T[:, bass.ds(t, 1), :, :].rearrange("p t m i -> p (t m) i")).then_inc(qk_in[b], 16)
                sp.dma_start(k[b][:, :, :], k_T[:, :, bass.ds(t * P, KEYS)]).then_inc(qk_in[b], 16)

            def values(t, b):
                after(sp, o_full, t - 1)
                past = v_tok[WINDOW:P, bass.ds(t, 1), :].rearrange("p t (m two d) -> p two (t m) d", two=2, d=LD)
                for half in range(2):
                    sp.dma_start(v_past[b][half * LD:(half + 1) * LD, :, :], past[:, half]).then_inc(v_in[b], 16)
                sp.dma_start(v_own[b][:, :], v_tok[:, bass.ds(t + 1, 1), :].rearrange("p t d -> p (t d)")).then_inc(v_in[b], 16)

            for t in range(2):
                queries_and_keys(t, t)
            for t in range(2):
                values(t, t)
                queries_and_keys(t + 2, t)
            with sp.Fori(1, NT // 2 - 1) as i:
                for b in range(2):
                    values(2 * i + b, b)
                    queries_and_keys(2 * i + b + 2, b)
            for t in range(NT - 2, NT):
                values(t, t % 2)

        @block.gpsimd
        def _(pool):
            def step(i, b, now, flip, put):
                if now:
                    t = i + 1
                    for u in range(2):
                        pool.wait_ge(inv_done, t * 2 + u + 1)
                        pool.wait_ge(exp_done, t * 2 + u + 1)
                        mine = probs[1 - b][:, heads_of(u), :]
                        nc.gpsimd.tensor_tensor(mine, mine, inv[1 - b][:, heads_of(u)].unsqueeze(2).to_broadcast([P, 4, KEYS]),
                                                ALU.mult).then_inc(share_done, 1)

            steps(pool, step)

        @block.tensor
        def _(pe):
            def scores(t, b, u, first):
                if u == 0:
                    pe.wait_ge(qk_in[b], 16 * (t - b) + 32)
                after(pe, exp_done, t * 2 + u - 1)
                for m in (2 * u, 2 * u + 1):
                    even, odd = (score[2 * half + u][:, m % 2 * KEYS:(m % 2 + 1) * KEYS] for half in range(2))
                    nc.tensor.matmul(even[:, 0:P], q[b][0:LD, m, :], k[b][0:LD, m, WINDOW:KEYS],
                                     start=m % 2 == 0, stop=False, skip_group_check=True)
                    nc.tensor.matmul(odd, q[b][LD:P, m, :], k[b][LD:P, m, :],
                                     start=m % 2 == 0, stop=False, skip_group_check=True)
                    nc.tensor.matmul(even[:, P:KEYS], q[b][0:LD, m, :], k[b][0:LD, m, 0:WINDOW],
                                     start=False, stop=False, skip_group_check=True)
                for half in range(2):
                    last = nc.tensor.matmul(score[2 * half + u][:, 0:2 * KEYS], ident_bf, bands[half][0 if first else 1],
                                            start=False, stop=True, skip_group_check=True)
                last.then_inc(score_full, 1)

            def flip_own(t, b, u):
                pe.wait_ge(share_done, t * 2 + u + 1)
                after(pe, own_done, t * 2 + u)
                for n in range(4):
                    last = nc.tensor.transpose(own_ps[:, n * P:(n + 1) * P], probs[b][:, 4 * u + n, n % 2 * WINDOW:n % 2 * WINDOW + P], ident)
                last.then_inc(own_full, 1)

            def flip_past(t, b):
                after(pe, past_done, t)
                both = probs[b][:, :, :].rearrange("p h k -> p (h k)")
                for m in range(NPAIR):
                    last = nc.tensor.transpose(past_ps[:, m * P:(m + 1) * P], both[:, 2 * m * KEYS + P:2 * m * KEYS + 2 * P], ident)
                last.then_inc(past_full, 1)

            def outputs(t, b):
                pe.wait_ge(v_in[b], 24 * (t - b) + 48)
                after(pe, o_done, t)
                pe.wait_ge(past_done, t + 1)
                pe.wait_ge(own_done, t * 2 + 2)
                for m in range(NPAIR):
                    for half in range(2):
                        r = slice(half * LD, (half + 1) * LD)
                        nc.tensor.matmul(o_ps[r, m * P:(m + 1) * P], v_own[b][:, (2 * m + half) * LD:(2 * m + half + 1) * LD], own_T[b][:, 2 * m + half, :],
                                         start=True, stop=False, skip_group_check=True)
                    for half in range(2):
                        r = slice(half * LD, (half + 1) * LD)
                        last = nc.tensor.matmul(o_ps[r, m * P:(m + 1) * P], v_past[b][r, m, :], past_T[b][r, m, :],
                                                start=False, stop=True, skip_group_check=True)
                last.then_inc(o_full, 1)

            def project_out(t):
                pe.wait_ge(o_done, t + 1)
                after(pe, out_done, t)
                for m in range(NPAIR):
                    last = nc.tensor.matmul(out_ps[:, 0:P], w_out[:, m, :], o_T[:, m, :], start=m == 0, stop=m == NPAIR - 1)
                last.then_inc(out_full, 1)

            def step(i, b, now, flip, put):
                first = isinstance(i, int) and i == -1
                if now:
                    scores(i + 1, 1 - b, 0, first)
                if flip:
                    flip_own(i, b, 0)
                if put:
                    outputs(i - 1, 1 - b)
                if flip:
                    flip_own(i, b, 1)
                if now:
                    scores(i + 1, 1 - b, 1, first)
                if flip:
                    flip_past(i, b)
                if put:
                    project_out(i - 1)

            steps(pe, step)

        @block.scalar
        def _(act):
            def exponentials(t, b, u):
                act.wait_ge(bias_done, t * 2 + u + 1)
                if u == 0:
                    after(act, past_full, t - 1)
                for h in range(4 * u, 4 * u + 4):
                    m, half = divmod(h, 2)
                    last = nc.scalar.activation(probs[b][:, h, :], score[2 * half + u][:, m % 2 * KEYS:(m % 2 + 1) * KEYS], ACT.Exp,
                                                scale=scale[b][:, h:h + 1], bias=bias[b][:, h:h + 1], accum_out=den[b][:, h:h + 1])
                last.then_inc(exp_done, 1)

            def own(t, b, u):
                if u == 0:
                    after(act, o_full, t - 1)
                act.wait_ge(own_full, t * 2 + u + 1)
                nc.scalar.activation(own_T[b][:, heads_of(u), :], own_ps.rearrange("p (h i) -> p h i", h=4), ACT.Copy).then_inc(own_done, 1)

            def step(i, b, now, flip, put):
                if flip:
                    own(i, b, 0)
                if now:
                    exponentials(i + 1, 1 - b, 0)
                if put:
                    after(act, out_full, i - 1)
                    act.wait_ge(o_full, i)
                    nc.scalar.activation(o_T[:, :, :], o_ps.rearrange("p (m i) -> p m i", m=NPAIR), ACT.Copy).then_inc(o_done, 1)
                if flip:
                    own(i, b, 1)
                if now:
                    exponentials(i + 1, 1 - b, 1)

            steps(act, step)

        @block.vector
        def _(dve):
            def maxima(t, b, u):
                if u == 0:
                    after(dve, exp_done, (t - 1) * 2)
                    nc.vector.tensor_copy(scale[b][:, :].unsqueeze(1), q_scale[:, bass.ds(t, 1), :]).then_inc(scale_in, 1)
                dve.wait_ge(score_full, t * 2 + u + 1)
                for half in range(2):
                    nc.vector.tensor_reduce(neg_max[b][:, 4 * u + half:4 * u + half + 3:2],
                                            score[2 * half + u][:, 0:2 * KEYS].rearrange("p (h k) -> p h k", h=2),
                                            AX.X, ALU.max, negate=True).then_inc(max_done, 1)
                dve.wait_ge(scale_in, t + 1)
                dve.wait_ge(max_done, t * 4 + 2 * u + 2)
                nc.vector.tensor_tensor(bias[b][:, heads_of(u)], neg_max[b][:, heads_of(u)], scale[b][:, heads_of(u)], ALU.mult).then_inc(bias_done, 1)

            def inverses(t, b, u):
                dve.wait_ge(exp_done, t * 2 + u + 1)
                after(dve, share_done, (t - 2) * 2 + u + 1)
                nc.vector.reciprocal(inv[b][:, heads_of(u)], den[b][:, heads_of(u)]).then_inc(inv_done, 1)

            def step(i, b, now, flip, put):
                if now:
                    maxima(i + 1, 1 - b, 0)
                    inverses(i + 1, 1 - b, 0)
                    maxima(i + 1, 1 - b, 1)
                if flip:
                    after(dve, o_full, i - 1)
                    dve.wait_ge(past_full, i + 1)
                    nc.vector.tensor_copy(past_T[b][:, :, :], past_ps.rearrange("p (m i) -> p m i", m=NPAIR)).then_inc(past_done, 1)
                if now:
                    inverses(i + 1, 1 - b, 1)
                if put:
                    dve.wait_ge(out_full, i)
                    at = bass.ds((i - 1) * P, P)
                    nc.vector.tensor_tensor(x_T[:, at], x_T[:, at], out_ps[:, 0:P], ALU.add).then_inc(out_done, 1)

            steps(dve, step)


def feed_forward(nc, psum, name, u_T, w1, b1, w2, b2, x_T):
    parts = [min(P, HID - n * P) for n in range(-(-HID // P))]
    NP = len(parts)
    with ExitStack() as ctx:
        a_ps, g_ps, out_ps = ([bank(psum, 2 * n + b) for b in range(2)] for n in range(3))
        gelu = [ctx.enter_context(nc.sbuf_tensor(f"{name}_gelu{b}", [P, BANK], F32)) for b in range(2)]
        mixed = [ctx.enter_context(nc.sbuf_tensor(f"{name}_mixed{b}", [P, BANK], F32)) for b in range(3)]
        sem = lambda n: ctx.enter_context(nc.semaphore(f"{name}_{n}"))
        up_full = sem("up_full")
        gelu_done = sem("gelu_done")
        mixed_done = sem("mixed_done")
        down_done = sem("down_done")
        out_done = sem("out_done")
        work = [(c, n) for c in range(NC) for n in range(NP)]
        block = ctx.enter_context(nc.Block())

        @block.tensor
        def _(pe):
            def down(i):
                c, n = work[i]
                pe.wait_ge(mixed_done, i + 1)
                if n == 0 and c >= 2:
                    pe.wait_ge(out_done, c - 1)
                nc.tensor.matmul(out_ps[c % 2][:, :], w2[0:parts[n], n, :], mixed[i % 3][0:parts[n], :], start=n == 0,
                                 stop=n == NP - 1).then_inc(down_done, 1)

            for i, (c, n) in enumerate(work):
                if i >= 2:
                    pe.wait_ge(mixed_done, i - 1)
                for to, at in ((a_ps, 0), (g_ps, HID)):
                    m = nc.tensor.matmul(to[i % 2][0:parts[n], :], w1[:, at + n * P:at + n * P + parts[n]], u_T[:, chunk(c)], start=True, stop=True)
                m.then_inc(up_full, 1)
                if i >= 2:
                    down(i - 2)
            for i in range(len(work) - 2, len(work)):
                down(i)

        @block.scalar
        def _(act):
            for i, (c, n) in enumerate(work):
                act.wait_ge(up_full, i + 1)
                r = slice(0, parts[n])
                nc.scalar.activation(gelu[i % 2][r, :], g_ps[i % 2][r, :], ACT.Gelu, bias=b1[r, 1, n:n + 1]).then_inc(gelu_done, 1)

        @block.vector
        def _(dve):
            def add(c):
                dve.wait_ge(down_done, (c + 1) * NP)
                nc.vector.scalar_tensor_tensor(x_T[:, chunk(c)], out_ps[c % 2][:, :], b2, x_T[:, chunk(c)], ALU.add, ALU.add).then_inc(out_done, 1)

            for i, (c, n) in enumerate(work):
                dve.wait_ge(gelu_done, i + 1)
                if i >= 3:
                    dve.wait_ge(down_done, i - 2)
                r = slice(0, parts[n])
                nc.vector.scalar_tensor_tensor(mixed[i % 3][r, :], a_ps[i % 2][r, :], b1[r, 0, n:n + 1], gelu[i % 2][r, :], ALU.add, ALU.mult).then_inc(mixed_done, 1)
                if n == 0 and c >= 1:
                    add(c - 1)
            add(NC - 1)


def clear_semaphores(nc, first):
    last = max(nc.released_uncleared_semaphores)
    with nc.Block() as block:
        @block.gpsimd
        def _(pool):
            pool.sem_clear(range(first, last + 1))


def forward(nc, a, out):
    with ExitStack() as ctx:
        sb = lambda n, s, d=F32: ctx.enter_context(nc.sbuf_tensor(n, s, d))
        x_T, h_T, u_T = (sb(n, [P, S])[:, :] for n in ("x_T", "h_T", "u_T"))
        psum = ctx.enter_context(nc.psum_tensor("psum", [P, 8 * BANK], F32))
        q_dram = nc.dram_tensor("q_pieces", [NPIECE, P, S], BF16, kind="Internal").ap()
        k_dram = nc.dram_tensor("k_pieces", [NPIECE, P, S], BF16, kind="Internal").ap()
        z_dram = nc.dram_tensor("z_heads", [NH * (HD + 1), S], F32, kind="Internal").ap()

        def held(scope, *names):
            return {n: scope.enter_context(nc.sbuf_tensor(f"{n}_sb", list(a[n].shape), a[n].dtype)) for n in names}

        full = lambda t: t[tuple(slice(None) for _ in t.shape)]
        early = held(ctx, "averages", "masks", "cols")
        mod = sb("mod", [P, 2, 2, 3])
        gated = sb("gated", [P, 2])
        ident = sb("ident_sb", [P, P])[:, :]
        late = held(ctx, "w_in", "w_v", "w_out", "pair_rows", "pair_spread", "bands", "w_up", "b_up", "w_down")
        attend = ctx.enter_context(ExitStack())
        z_T = attend.enter_context(nc.sbuf_tensor("z_T", [P, S], F32))[:, :]
        v_tok = attend.enter_context(nc.sbuf_tensor("v_tok", [P, NT, P], F32))
        den = attend.enter_context(nc.sbuf_tensor("den", [P, PART], F32))[:, :]
        early.update(held(attend, "den_rows", "keep_kq", "wmods", "cs", "w_attn0", "bv0", "w_attn1", "w_attn2"))
        moe = ctx.enter_context(ExitStack())
        late.update(held(moe, "gate_w", "rank", "pick", "w13", "w2"))
        late_in = ctx.enter_context(nc.semaphore("late_in"))

        first_sem = nc.free_semaphores[0]
        load_inputs(nc, psum, a["x"], x_T, (ident, a["ident"]), [(full(b), a[n]) for n, b in early.items()])
        with nc.Block() as block:
            @block.scalar
            def _(act):
                for n, b in late.items():
                    act.dma_start(full(b), a[n]).then_inc(late_in, 16)

        w0, w1, w2 = early["w_attn0"], early["w_attn1"], early["w_attn2"]
        averages, den_rows = full(early["averages"]), full(early["den_rows"])
        cols = {n: early["cols"][:, i:i + 1] for i, n in enumerate(COLS)}
        ident_bf, mask_qk, mask_kq = (early["masks"][:, i, :] for i in range(3))
        shift_of = lambda l, i: mod[:, l, i, 0:1]
        scale_of = lambda l, i: mod[:, l, i, 1:2]
        gate_of = lambda l, i: mod[:, l, i, 2:3]
        modulation(nc, psum, [(early["cs"][:, l:l + 1], early["wmods"][:, l, :]) for l in range(2)], mod,
                   cols["gamma"], cols["beta"], gated)

        norm(nc, psum, "ln0a", x_T, h_T, averages, LN_EPS, scale_of(0, 0), shift_of(0, 0))
        project(nc, psum, "proj0", h_T, w0[:, 0, :], w0[:, 1, :], w0[:, 2, :], q_dram, k_dram, v_tok,
                bias=(cols["bq"], cols["bk"], early["bv0"]))
        attention(nc, psum, "att0", False, S ** -0.5, q_dram, k_dram, v_tok, z_dram, z_T, den,
                  ident_bf, mask_qk, mask_kq, early["keep_kq"][:, :])
        divide_by_sums(nc, psum, "com0", z_T, den, den_rows, h_T, ident)
        norm(nc, psum, "ln0z", z_T, None, averages, LN_EPS, gated[:, 0:1], gated[:, 1:2], add_to=x_T)
        norm(nc, psum, "ln0b", x_T, h_T, averages, LN_EPS, scale_of(0, 1), shift_of(0, 1))
        norm(nc, psum, "rms1", h_T, u_T, averages, 1e-5, cols["ln1"])
        with ExitStack() as rope:
            angle = rope.enter_context(nc.sbuf_tensor("rope_sb", [P, 2, S], F32))
            rope_in = rope.enter_context(nc.semaphore("rope_in"))
            with nc.Block() as block:
                @block.sync
                def _(sp):
                    sp.dma_start(angle[:, :, :], a["rope"]).then_inc(rope_in, 16)
                    sp.wait_ge(rope_in, 16)
            project(nc, psum, "proj1", u_T, w1[:, 0, :], w1[:, 1, :], w1[:, 2, :], q_dram, k_dram, v_tok,
                    rope=(w1[:, 3, :], w1[:, 4, :], angle[:, 0, :], angle[:, 1, :]))
        attention(nc, psum, "att1", True, HD ** -0.5, q_dram, k_dram, v_tok, z_dram, z_T, den, ident_bf, mask_qk, mask_kq)
        divide_by_sums(nc, psum, "com1", z_T, den, den_rows, h_T, ident, w1[:, 5, :], 1.0)
        norm(nc, psum, "rms2", h_T, u_T, averages, 1e-5, cols["ln2"])
        with nc.Block() as block:
            @block.sync
            def _(sp):
                sp.wait_ge(late_in, 16 * len(late))
        w_rows = moe.enter_context(nc.sbuf_tensor("w_rows", [P, S], BF16))[:, :]
        router(nc, psum, u_T, full(late["gate_w"]), full(late["rank"]), ident_bf, w_rows)
        experts(nc, psum, u_T, late["w13"], late["w2"], w_rows, late["pick"], h_T, x_T, gate_of(0, 1))
        moe.close()
        clear_semaphores(nc, first_sem)
        norm(nc, psum, "ln1a", x_T, h_T, averages, LN_EPS, scale_of(1, 0), shift_of(1, 0))
        project(nc, psum, "proj2", h_T, w2[:, 0, :], w2[:, 1, :], w2[:, 2, :], q_dram, k_dram, v_tok)
        attention(nc, psum, "att2", True, P ** -0.5, q_dram, k_dram, v_tok, z_dram, z_T, den, ident_bf, mask_qk, mask_kq)
        divide_by_sums(nc, psum, "com2", z_T, den, den_rows, x_T, ident, w2[:, 3, :], gate_of(1, 0))
        norm(nc, psum, "ln1b", x_T, h_T, averages, LN_EPS, scale_of(1, 1), shift_of(1, 1))
        attend.close()
        clear_semaphores(nc, first_sem)
        for l in range(2):
            shift_tokens(nc, f"shift{l}a", h_T, u_T)
            with ExitStack() as local:
                hold = lambda n, s: local.enter_context(nc.sbuf_tensor(f"local{l}_{n}", s, F32))
                q_local, k_local = hold("q_T", [P, NT, NPAIR, P]), hold("k_T", [P, NPAIR, WINDOW + S])
                v_local, q_scale = hold("v_tok", [P, 1 + NT, INNER]), hold("q_scale", [P, NT, LH])
                local_project(nc, psum, f"lproj{l}", u_T, late["w_in"][:, l], late["w_v"][:, l, :], a["tables"],
                              [cols[f"scale{l}{n}"] for n in range(4)], full(late["pair_rows"]), full(late["pair_spread"]),
                              q_local, k_local, v_local, q_scale)
                local_attend(nc, psum, f"latt{l}", q_local, k_local, v_local, q_scale, late["w_out"][:, l],
                             [[late["bands"][:, half, i] for i in range(2)] for half in range(2)], ident, ident_bf, h_T)
            shift_tokens(nc, f"shift{l}b", h_T, u_T)
            with ExitStack() as ffn:
                normed = ffn.enter_context(nc.sbuf_tensor(f"ffn{l}_T", [P, S], F32))[:, :]
                norm(nc, psum, f"lnf{l}", u_T, normed, averages, LN_EPS, cols[f"lg{l}"], cols[f"lb{l}"])
                feed_forward(nc, psum, f"ff{l}", normed, late["w_up"][:, l, :], late["b_up"][:, l], late["w_down"][:, l], cols[f"b2{l}"], h_T)
        with ExitStack() as last:
            with nc.Block() as block:
                @block.vector
                def _(dve):
                    nc.vector.scalar_tensor_tensor(x_T, h_T, gate_of(1, 1), x_T, ALU.mult, ALU.add)
        store_output(nc, psum, x_T, out, ident)


COLS = ["gamma", "beta", "bq", "bk", "ln1", "ln2"] + [f"scale{l}{n}" for l in range(2) for n in range(4)] \
    + [f"{n}{l}" for l in range(2) for n in ("lg", "lb", "b2")]


def constants():
    import numpy as np
    f32, bf16 = np.float32, mybir.dt.np(BF16)
    i = np.arange(P)
    c = {"ident": np.eye(P, dtype=f32), "averages": np.zeros((P, 3 * P), f32)}
    c["averages"][:, 0:P] = np.eye(P) - 1.0 / P
    c["averages"][:, P:P + 32] = 1.0 / P
    c["averages"][0::32, 2 * P:] = 1
    row_head, row_part = np.divmod(i, P // NH)
    parts = np.arange(S // PART)
    c["den_rows"] = ((row_head[:, None, None] == i[None, None, :] // HD) & (row_part[:, None, None] == parts[None, :, None])).astype(f32)
    mask_qk = np.where(i[None, :] > i[:, None], NEG, 0.0)
    c["masks"] = np.stack([np.eye(P), mask_qk, mask_qk.T], axis=1).astype(bf16)
    c["keep_kq"] = (i[:, None] >= i[None, :]).astype(f32)
    c["rank"] = np.broadcast_to(np.arange(NE, 0, -1).astype(f32), (P, NE)).copy()
    pick = np.zeros((P, NE, P), bf16)
    for e in range(NE):
        pick[e:NPIECE * NE:NE, e, :] = 1
    c["pick"] = pick
    second = i >= LD
    c["pair_rows"] = np.where(second[:, None] == (i[None, 0:32] >= 16), 1, 0).astype(f32)
    c["pair_spread"] = ((i[:, None] % 32 == 0) & ~second[None, :] | (i[:, None] % 32 == 16) & second[None, :]).astype(f32)
    j = np.arange(KEYS)[None, :] - WINDOW
    seen = (j <= i[:, None]) & (j >= i[:, None] - WINDOW)
    bands = np.stack([np.where(seen & (j >= 0), 0.0, NEG), np.where(seen, 0.0, NEG)])
    bands = np.stack([np.roll(bands, P, axis=2), bands])
    c["bands"] = np.ascontiguousarray(np.stack([bands, bands], axis=2).transpose(3, 0, 1, 2, 4)).astype(bf16)
    t = np.arange(S, dtype=f32)

    def angles(dim):
        inv = (f32(1) / (f32(10000.0) ** (np.arange(0, dim, 2, dtype=f32) / f32(dim)).astype(f32))).astype(f32)
        freq = (t[:, None] * inv[None, :]).astype(f32).astype(np.float64)
        freq = np.concatenate([freq, freq], axis=1).T
        sign = np.where(np.arange(dim) < dim // 2, -1.0, 1.0)[:, None]
        return np.cos(freq).astype(f32), (np.sin(freq) * sign).astype(f32)

    cos, sin = angles(HD)
    c["rope"] = np.ascontiguousarray(np.tile(np.stack([cos, sin], axis=1), (NH, 1, 1)))
    cos, sin = angles(LD)
    half = np.arange(0, LD, 2, dtype=f32)
    base = ((half + f32(0.4 * LD)) / f32(1.4 * LD)).astype(f32)
    power = ((t - S // 2) / f32(WINDOW // 2)).astype(f32)
    scale = (base[None, :].astype(np.float64) ** power[:, None]).astype(f32)
    scale = np.concatenate([scale, scale], axis=1).T
    tables = np.stack([cos * scale, sin * scale, cos / scale, sin / scale], axis=1).astype(f32)
    c["tables"] = np.ascontiguousarray(np.tile(tables, (2, 1, 1)))
    return c


def layout(np, i):
    cont = np.ascontiguousarray
    swap = lambda w, dim: w.reshape(-1, 2, dim // 2, w.shape[-1])[:, ::-1].reshape(w.shape)
    a = {"x": i["L0_attn_embedded"], "cs": cont(np.concatenate([i["L0_c"], i["L1_c"]], axis=0).T)}
    a["wmods"] = cont(np.stack([i["L0_wmod"], i["L1_wmod"]], axis=1))
    a["w_attn0"] = cont(np.stack([i[f"L0_attn_W{n}"].T for n in "qkv"], axis=1))
    a["bv0"] = cont(np.broadcast_to(i["L0_attn_bv"], (P, P)))
    w = i["L0_ffn_wqkv"]
    q, kv = w[:P], w[P:]
    nkv = kv.shape[0] // HD // 2
    k, v = (np.repeat(part.reshape(nkv, HD, P), NH // nkv, axis=0).reshape(P, P) for part in (kv[:nkv * HD], kv[nkv * HD:]))
    a["w_attn1"] = cont(np.stack([q.T, k.T, v.T, swap(q, HD).T, swap(k, HD).T, i["L0_ffn_wo"].T], axis=1))
    by_head = lambda w: w.reshape(P, HD, NH).transpose(0, 2, 1).reshape(P, P)
    a["w_attn2"] = cont(np.stack([by_head(i["L1_attn_qw"]), by_head(i["L1_attn_kw"]), by_head(i["L1_attn_vw"]),
                                  by_head(i["L1_attn_ow"].T).T], axis=1))
    a["gate_w"] = cont(i["L0_ffn_gate_w"].T)
    a["w13"] = cont(i["L0_ffn_w13"].transpose(2, 0, 1))
    a["w2"] = cont(i["L0_ffn_w2"].reshape(NE, P, 2, P).transpose(3, 0, 2, 1))
    w = i["L1_ffn_wqkv"]
    cols = lambda n: w[:, :, n * INNER:(n + 1) * INNER]
    swap_cols = lambda w: w.reshape(2, P, LH, 2, LD // 2)[:, :, :, ::-1].reshape(2, P, INNER)
    four = np.stack([cols(0), swap_cols(cols(0)), cols(1), swap_cols(cols(1))], axis=2)
    a["w_in"] = cont(four.reshape(2, P, 4, NPAIR, P).transpose(1, 0, 2, 3, 4))
    a["w_v"] = cont(cols(2).transpose(1, 0, 2))
    a["w_out"] = cont(i["L1_ffn_wo"].reshape(2, NPAIR, P, P).transpose(2, 0, 1, 3))
    parts = -(-HID // P)
    a["w_up"] = cont(i["L1_ffn_w1"].transpose(1, 0, 2))
    padded = lambda x: np.concatenate([x, np.zeros((*x.shape[:-2], parts * P - HID, x.shape[-1]), x.dtype)], axis=-2)
    a["b_up"] = cont(padded(i["L1_ffn_b1"].reshape(2, 2, HID, 1)).reshape(2, 2, parts, P).transpose(3, 0, 1, 2))
    a["w_down"] = cont(padded(i["L1_ffn_w2"]).reshape(2, parts, P, P).transpose(2, 0, 1, 3))
    one = {"gamma": i["L0_attn_gamma"], "beta": i["L0_attn_beta"], "bq": i["L0_attn_bq"], "bk": i["L0_attn_bk"],
           "ln1": i["L0_ffn_ln1_w"], "ln2": i["L0_ffn_ln2_w"]}
    for l in range(2):
        for n, s in enumerate((i["L1_ffn_q_scale"][l], i["L1_ffn_k_scale"][l])):
            one[f"scale{l}{2 * n}"] = np.tile(s, 2)
            one[f"scale{l}{2 * n + 1}"] = np.tile(s.reshape(2, -1)[::-1].reshape(-1), 2)
        one[f"lg{l}"], one[f"lb{l}"], one[f"b2{l}"] = i["L1_ffn_ln_g"][l], i["L1_ffn_ln_b"][l], i["L1_ffn_b2"][l]
    a["cols"] = cont(np.stack([one[n] for n in COLS], axis=1))
    return a


def kernel(**inputs):
    import numpy as _np
    import concourse.bacc as _bacc
    from concourse import mybir as _mybir
    from concourse.bass_utils import run_bass_kernel_spmd as _run

    nc = _bacc.Bacc("TRN2", target_bir_lowering=False, num_devices=1)
    arrays = {**layout(_np, {n: _np.asarray(x) for n, x in inputs.items()}), **constants()}
    views = {n: nc.dram_tensor(f"in_{n}", x.shape, _mybir.dt.from_np(x.dtype), kind="ExternalInput").ap()
             for n, x in arrays.items()}
    out = nc.dram_tensor("out_0", (1, S, P), F32, kind="ExternalOutput").ap()
    forward(nc, views, out)
    r = _run(nc, [{f"in_{n}": x for n, x in arrays.items()}], core_ids=[0])
    return r.results[0]["out_0"]
```
